# Optimizing a Trainium2 kernel written in Bass

```python
import numpy as np
import jax
import jax.numpy as jnp

def _softmax(x, axis=-1):
    return jax.nn.softmax(x, axis=axis)

def _gelu(x):
    return jax.nn.gelu(x, approximate=True)

def _silu(x):
    return jax.nn.silu(x)

def _sigmoid(x):
    return jax.nn.sigmoid(x)

def _layernorm(x, axis=-1, eps=1e-05):
    m = jnp.mean(x, axis=axis, keepdims=True)
    v = jnp.var(x, axis=axis, keepdims=True)
    return (x - m) / jnp.sqrt(v + eps)

def _scatter_add(tgt, idx, src, axis=0):
    return tgt.at[idx].add(src)

def _segment_sum(src, seg, n):
    return jax.ops.segment_sum(src, seg, n)
kernel_name = 'mk_vit_tower_cls_d4_tok_img768_r4_22caa5'

def setup_inputs(seed: int=0):
    np.random.seed(seed)
    _w = jnp.asarray

    def _rec_inputs():
        import jax
        import jax.numpy as jnp
        _rk = jax.random.key(seed)
        x = -0.000222058 + 0.999998 * jax.random.normal(jax.random.fold_in(_rk, 1), (64, 3, 84, 84), jnp.float32)
        cls_tok = 0.02 * jax.random.normal(jax.random.fold_in(_rk, 5), (1, 1, 192), jnp.float32)
        return (x, cls_tok)
    x, cls_tok = _rec_inputs()

    def _L0_tok_setup():
        import jax, jax.numpy as jnp
        import numpy as np
        from jax import lax
        HIDDEN = 192
        C_IN = 3
        PATCH = 16
        SIDE = 32
        NUM_PATCHES = SIDE * SIDE

        def _position_ids(nb_h, nb_w):
            boundaries = np.arange(1.0 / SIDE, 1.0, 1.0 / SIDE, dtype=np.float32)
            frac_h = np.arange(0.0, 1.0 - 1e-06, 1.0 / nb_h, dtype=np.float32)
            frac_w = np.arange(0.0, 1.0 - 1e-06, 1.0 / nb_w, dtype=np.float32)
            bh = np.searchsorted(boundaries, frac_h, side='right')
            bw = np.searchsorted(boundaries, frac_w, side='right')
            return jnp.asarray((bh[:, None] * SIDE + bw).reshape(-1), dtype=jnp.int32)
        key = jax.random.key(seed)
        k1, k2, k3 = jax.random.split(key, 3)
        pixel_values = jax.random.normal(k1, (32, C_IN, 128, 128), dtype=jnp.float32)
        conv_w = jax.random.normal(k2, (HIDDEN, C_IN, PATCH, PATCH), dtype=jnp.float32) * 0.02
        conv_b = jnp.zeros((HIDDEN,), dtype=jnp.float32)
        pos_table = jax.random.normal(k3, (NUM_PATCHES, HIDDEN), dtype=jnp.float32) * 0.02
        return {'pixel_values': pixel_values, 'conv_w': conv_w, 'conv_b': conv_b, 'pos_table': pos_table}
    _L0_tok_all = _L0_tok_setup()
    _L0_tok_in = {k: v for k, v in _L0_tok_all.items() if k in ('conv_w', 'conv_b', 'pos_table')}
    del _L0_tok_all

    def _L0_attn_setup():
        import jax, jax.numpy as jnp
        import numpy as np
        import math
        D_MODEL = 192
        N_HEADS = 6
        HD = D_MODEL // N_HEADS
        RANK = D_MODEL // 4
        B, T = (128, 64)

        def _rope_tables(T, dim):
            inv = 1.0 / 10000.0 ** (jnp.arange(0, dim, 2, dtype=jnp.float32) / dim)
            t = jnp.arange(T, dtype=jnp.float32)
            freqs = jnp.outer(t, inv)
            emb = jnp.concatenate([freqs, freqs], axis=-1)
            return (jnp.cos(emb), jnp.sin(emb))

        def _rot(x):
            h = x.shape[-1] // 2
            return jnp.concatenate([-x[..., h:], x[..., :h]], axis=-1)
        key = jax.random.key(seed)
        ks = jax.random.split(key, 8)
        s_in = 1.0 / math.sqrt(D_MODEL)
        s_r = 1.0 / math.sqrt(RANK)
        inp = {'x': jax.random.normal(ks[0], (B, T, D_MODEL), dtype=jnp.float32), 'qA': jax.random.normal(ks[1], (D_MODEL, RANK), dtype=jnp.float32) * s_in, 'qB': jax.random.normal(ks[2], (RANK, D_MODEL), dtype=jnp.float32) * s_r, 'kA': jax.random.normal(ks[3], (D_MODEL, RANK), dtype=jnp.float32) * s_in, 'kB': jax.random.normal(ks[4], (RANK, D_MODEL), dtype=jnp.float32) * s_r, 'vA': jax.random.normal(ks[5], (D_MODEL, RANK), dtype=jnp.float32) * s_in, 'vB': jax.random.normal(ks[6], (RANK, D_MODEL), dtype=jnp.float32) * s_r, 'o_w': jax.random.normal(ks[7], (D_MODEL, D_MODEL), dtype=jnp.float32) * s_in}
        return inp
    _L0_attn_all = _L0_attn_setup()
    _L0_attn_in = {k: v for k, v in _L0_attn_all.items() if k in ('qA', 'qB', 'kA', 'kB', 'vA', 'vB', 'o_w')}
    del _L0_attn_all

    def _L0_ffn_setup():
        import jax, jax.numpy as jnp
        import numpy as np
        C = 192
        E = 32
        H = 4 * C
        key = jax.random.key(seed)
        ks = jax.random.split(key, 5)
        B, T = (2, 256)
        scale_in = 1.0 / np.sqrt(C)
        scale_hid = 1.0 / np.sqrt(H)
        return {'x': jax.random.normal(ks[0], (B, T, C), jnp.float32), 'gate_w': jax.random.normal(ks[1], (C, E), jnp.float32) * scale_in, 'gate_b': jnp.zeros((E,), jnp.float32), 'w1': jax.random.normal(ks[2], (E, C, H), jnp.float32) * scale_in, 'b1': jnp.zeros((E, H), jnp.float32), 'w2': jax.random.normal(ks[3], (E, H, C), jnp.float32) * scale_hid, 'b2': jnp.zeros((E, C), jnp.float32)}
    _L0_ffn_all = _L0_ffn_setup()
    _L0_ffn_in = {k: v for k, v in _L0_ffn_all.items() if k in ('gate_w', 'gate_b', 'w1', 'b1', 'w2', 'b2')}
    del _L0_ffn_all

    def _L1_attn_setup():
        import jax, jax.numpy as jnp
        import numpy as np
        B, N, DIM = (16, 577, 192)
        HEADS, HEAD_DIM = (12, 64)
        QKV_DIM = HEADS * HEAD_DIM
        MAX_REL = 14
        TABLE_ROWS = 2 * MAX_REL + 2

        def _rel_indices(n, max_rel):
            m = n - 1
            side = int(m ** 0.5)
            r = np.arange(m)
            dv = r[None, :] // side - r[:, None] // side
            dh = r[None, :] % side - r[:, None] % side
            iv = np.clip(dv, -max_rel, max_rel) + max_rel + 1
            ih = np.clip(dh, -max_rel, max_rel) + max_rel + 1
            iv = np.pad(iv, ((1, 0), (1, 0)))
            ih = np.pad(ih, ((1, 0), (1, 0)))
            return (jnp.asarray(iv), jnp.asarray(ih))
        key = jax.random.key(seed)
        ks = jax.random.split(key, 8)
        return {'x': jax.random.normal(ks[0], (B, N, DIM), jnp.float32), 'qkv_w': jax.random.normal(ks[1], (3 * QKV_DIM, DIM), jnp.float32) * 0.02, 'proj_w': jax.random.normal(ks[2], (DIM, QKV_DIM), jnp.float32) * 0.02, 'proj_b': jnp.zeros((DIM,), jnp.float32), 'tab_kv': jax.random.normal(ks[3], (TABLE_ROWS, HEAD_DIM), jnp.float32) * 0.02, 'tab_kh': jax.random.normal(ks[4], (TABLE_ROWS, HEAD_DIM), jnp.float32) * 0.02, 'tab_vv': jax.random.normal(ks[5], (TABLE_ROWS, HEAD_DIM), jnp.float32) * 0.02, 'tab_vh': jax.random.normal(ks[6], (TABLE_ROWS, HEAD_DIM), jnp.float32) * 0.02}
    _L1_attn_all = _L1_attn_setup()
    _L1_attn_in = {k: v for k, v in _L1_attn_all.items() if k in ('qkv_w', 'proj_w', 'proj_b', 'tab_kv', 'tab_kh', 'tab_vv', 'tab_vh')}
    del _L1_attn_all

    def _L1_ffn_setup():
        import jax, jax.numpy as jnp
        import numpy as np
        B, S, D, F, E = (2, 256, 192, 768, 8)
        key = jax.random.key(seed)
        k0, k1, k2, k3, k4, k5 = jax.random.split(key, 6)
        scale = 0.02
        return {'hidden_states': jax.random.normal(k0, (B, S, D), dtype=jnp.float32), 'Wg': jax.random.normal(k1, (D, E), dtype=jnp.float32) * scale, 'W1': jax.random.normal(k2, (E, D, F), dtype=jnp.float32) * scale, 'b1': jnp.zeros((E, F), dtype=jnp.float32), 'W2': jax.random.normal(k3, (E, F, D), dtype=jnp.float32) * scale, 'b2': jnp.zeros((E, D), dtype=jnp.float32)}
    _L1_ffn_all = _L1_ffn_setup()
    _L1_ffn_in = {k: v for k, v in _L1_ffn_all.items() if k in ('Wg', 'W1', 'b1', 'W2', 'b2')}
    del _L1_ffn_all

    def _L2_attn_setup():
        import jax, jax.numpy as jnp
        import numpy as np
        B, N, C, H = (8, 256, 192, 12)
        D = C // H
        M = 2 * D
        SCALE = D ** (-0.5)
        EPS = 1e-12

        def _feature_map(z, rand_matrix):
            logits = jnp.einsum('bhnd,hdm->bhnm', z, rand_matrix)
            sqnorm = 0.5 * jnp.sum(z * z, axis=-1, keepdims=True)
            return jnp.exp(logits - sqnorm) * M ** (-0.5)
        key = jax.random.key(seed)
        k1, k2, k3, k4, k5 = jax.random.split(key, 5)
        x = jax.random.normal(k1, (B, N, C), dtype=jnp.float32)
        qkv_w = jax.random.normal(k2, (3 * C, C), dtype=jnp.float32) * 0.02
        proj_w = jax.random.normal(k3, (C, C), dtype=jnp.float32) * 0.02
        proj_b = jax.random.normal(k4, (C,), dtype=jnp.float32) * 0.02
        rand_matrix = jax.random.normal(k5, (H, D, M), dtype=jnp.float32)
        return {'x': x, 'qkv_w': qkv_w, 'proj_w': proj_w, 'proj_b': proj_b, 'rand_matrix': rand_matrix}
    _L2_attn_all = _L2_attn_setup()
    _L2_attn_in = {k: v for k, v in _L2_attn_all.items() if k in ('qkv_w', 'proj_w', 'proj_b', 'rand_matrix')}
    del _L2_attn_all

    def _L2_ffn_setup():
        import jax, jax.numpy as jnp
        import numpy as np
        E = 192
        H = 12
        D = E // H
        HID = 768
        NEXP = 4
        TOPK = 2
        EPS = 1e-05

        def _ln(x, g, b):
            m = jnp.mean(x, axis=-1, keepdims=True)
            v = jnp.mean(jnp.square(x - m), axis=-1, keepdims=True)
            return (x - m) * jax.lax.rsqrt(v + EPS) * g + b
        key = jax.random.key(seed)
        ks = jax.random.split(key, 10)
        s = 0.02
        return {'x': jax.random.normal(ks[0], (8, 256, E), jnp.float32), 'ln1_g': jnp.ones((E,), jnp.float32), 'ln1_b': jnp.zeros((E,), jnp.float32), 'in_w': jax.random.normal(ks[1], (3 * E, E), jnp.float32) * s, 'in_b': jnp.zeros((3 * E,), jnp.float32), 'out_w': jax.random.normal(ks[2], (E, E), jnp.float32) * s, 'out_b': jnp.zeros((E,), jnp.float32), 'mlp_w1': jax.random.normal(ks[3], (E, HID), jnp.float32) * s, 'mlp_b1': jnp.zeros((HID,), jnp.float32), 'mlp_w2': jax.random.normal(ks[4], (HID, E), jnp.float32) * s, 'mlp_b2': jnp.zeros((E,), jnp.float32), 'ln2_g': jnp.ones((E,), jnp.float32), 'ln2_b': jnp.zeros((E,), jnp.float32), 'gate_w': jax.random.normal(ks[5], (NEXP, E), jnp.float32) * s, 'gate_b': jnp.zeros((NEXP,), jnp.float32), 'exp_w1': jax.random.normal(ks[6], (NEXP, E, HID), jnp.float32) * s, 'exp_b1': jnp.zeros((NEXP, HID), jnp.float32), 'exp_w2': jax.random.normal(ks[7], (NEXP, HID, E), jnp.float32) * s, 'exp_b2': jnp.zeros((NEXP, E), jnp.float32)}
    _L2_ffn_all = _L2_ffn_setup()
    _L2_ffn_in = {k: v for k, v in _L2_ffn_all.items() if k in ('ln1_g', 'ln1_b', 'in_w', 'in_b', 'out_w', 'out_b', 'mlp_w1', 'mlp_b1', 'mlp_w2', 'mlp_b2', 'ln2_g', 'ln2_b', 'gate_w', 'gate_b', 'exp_w1', 'exp_b1', 'exp_w2', 'exp_b2')}
    del _L2_ffn_all

    def _L3_attn_setup():
        import jax, jax.numpy as jnp
        import numpy as np
        LOG2E = 1.4426950408889634
        NUM_HEADS = 12

        def fake_quant_sym8(x):
            scale = jnp.maximum(jnp.max(jnp.abs(x)) / 127.0, 1e-08)
            q = jnp.clip(jnp.round(x / scale), -128.0, 127.0) * scale
            return x + jax.lax.stop_gradient(q - x)

        def integer_approx_softmax(x):
            z = x * LOG2E
            z = z - jnp.max(z, axis=-1, keepdims=True)
            zi = jnp.floor(z)
            zf = z - zi
            p = jnp.exp2(zi) * (1.0 + zf)
            return p / jnp.sum(p, axis=-1, keepdims=True)
        key = jax.random.key(seed)
        ks = jax.random.split(key, 5)
        B, N, E, P = (8, 256, 192, 192)
        s = 0.02
        return {'x': jax.random.normal(ks[0], (B, N, E), jnp.float32), 'Wq': jax.random.normal(ks[1], (E, P), jnp.float32) * s, 'bq': jnp.zeros((P,), jnp.float32), 'Wk': jax.random.normal(ks[2], (E, P), jnp.float32) * s, 'bk': jnp.zeros((P,), jnp.float32), 'Wv': jax.random.normal(ks[3], (E, P), jnp.float32) * s, 'bv': jnp.zeros((P,), jnp.float32), 'Wo': jax.random.normal(ks[4], (P, E), jnp.float32) * s, 'bo': jnp.zeros((E,), jnp.float32)}
    _L3_attn_all = _L3_attn_setup()
    _L3_attn_in = {k: v for k, v in _L3_attn_all.items() if k in ('Wq', 'bq', 'Wk', 'bk', 'Wv', 'bv', 'Wo', 'bo')}
    del _L3_attn_all

    def _L3_ffn_setup():
        import jax, jax.numpy as jnp
        import numpy as np
        B, L, D, H, F = (4, 512, 192, 12, 768)
        ROUTE_FRAC = 0.15
        LN_EPS = 1e-05

        def _ln(x, g, b):
            m = jnp.mean(x, axis=-1, keepdims=True)
            v = jnp.mean((x - m) ** 2, axis=-1, keepdims=True)
            return (x - m) * jax.lax.rsqrt(v + LN_EPS) * g + b
        key = jax.random.key(seed)
        ks = jax.random.split(key, 20)
        s = 0.02
        return {'hidden_states': jax.random.normal(ks[0], (B, L, D), dtype=jnp.float32), 'g1': jnp.ones((D,), jnp.float32), 'b1': jnp.zeros((D,), jnp.float32), 'g2': jnp.ones((D,), jnp.float32), 'b2': jnp.zeros((D,), jnp.float32), 'Wr': jax.random.normal(ks[1], (D,), jnp.float32) * s, 'br': jnp.zeros((), jnp.float32), 'Wq': jax.random.normal(ks[2], (D, D), jnp.float32) * s, 'bq': jnp.zeros((D,), jnp.float32), 'Wk': jax.random.normal(ks[3], (D, D), jnp.float32) * s, 'bk': jnp.zeros((D,), jnp.float32), 'Wv': jax.random.normal(ks[4], (D, D), jnp.float32) * s, 'bv': jnp.zeros((D,), jnp.float32), 'Wo': jax.random.normal(ks[5], (D, D), jnp.float32) * s, 'bo': jnp.zeros((D,), jnp.float32), 'Wm': jax.random.normal(ks[6], (D, D), jnp.float32) * s, 'bm': jnp.zeros((D,), jnp.float32), 'W1': jax.random.normal(ks[7], (D, F), jnp.float32) * s, 'bf1': jnp.zeros((F,), jnp.float32), 'W2': jax.random.normal(ks[8], (F, D), jnp.float32) * s, 'bf2': jnp.zeros((D,), jnp.float32)}
    _L3_ffn_all = _L3_ffn_setup()
    _L3_ffn_in = {k: v for k, v in _L3_ffn_all.items() if k in ('g1', 'b1', 'g2', 'b2', 'Wr', 'br', 'Wq', 'bq', 'Wk', 'bk', 'Wv', 'bv', 'Wo', 'bo', 'Wm', 'bm', 'W1', 'bf1', 'W2', 'bf2')}
    del _L3_ffn_all
    return {'x': x, 'cls_tok': cls_tok, 'L0_tok_conv_w': _L0_tok_in['conv_w'], 'L0_tok_conv_b': _L0_tok_in['conv_b'], 'L0_tok_pos_table': _L0_tok_in['pos_table'], 'L0_attn_qA': _L0_attn_in['qA'], 'L0_attn_qB': _L0_attn_in['qB'], 'L0_attn_kA': _L0_attn_in['kA'], 'L0_attn_kB': _L0_attn_in['kB'], 'L0_attn_vA': _L0_attn_in['vA'], 'L0_attn_vB': _L0_attn_in['vB'], 'L0_attn_o_w': _L0_attn_in['o_w'], 'L0_ffn_gate_w': _L0_ffn_in['gate_w'], 'L0_ffn_gate_b': _L0_ffn_in['gate_b'], 'L0_ffn_w1': _L0_ffn_in['w1'], 'L0_ffn_b1': _L0_ffn_in['b1'], 'L0_ffn_w2': _L0_ffn_in['w2'], 'L0_ffn_b2': _L0_ffn_in['b2'], 'L1_attn_qkv_w': _L1_attn_in['qkv_w'], 'L1_attn_proj_w': _L1_attn_in['proj_w'], 'L1_attn_proj_b': _L1_attn_in['proj_b'], 'L1_attn_tab_kv': _L1_attn_in['tab_kv'], 'L1_attn_tab_kh': _L1_attn_in['tab_kh'], 'L1_attn_tab_vv': _L1_attn_in['tab_vv'], 'L1_attn_tab_vh': _L1_attn_in['tab_vh'], 'L1_ffn_Wg': _L1_ffn_in['Wg'], 'L1_ffn_W1': _L1_ffn_in['W1'], 'L1_ffn_b1': _L1_ffn_in['b1'], 'L1_ffn_W2': _L1_ffn_in['W2'], 'L1_ffn_b2': _L1_ffn_in['b2'], 'L2_attn_qkv_w': _L2_attn_in['qkv_w'], 'L2_attn_proj_w': _L2_attn_in['proj_w'], 'L2_attn_proj_b': _L2_attn_in['proj_b'], 'L2_attn_rand_matrix': _L2_attn_in['rand_matrix'], 'L2_ffn_ln1_g': _L2_ffn_in['ln1_g'], 'L2_ffn_ln1_b': _L2_ffn_in['ln1_b'], 'L2_ffn_in_w': _L2_ffn_in['in_w'], 'L2_ffn_in_b': _L2_ffn_in['in_b'], 'L2_ffn_out_w': _L2_ffn_in['out_w'], 'L2_ffn_out_b': _L2_ffn_in['out_b'], 'L2_ffn_mlp_w1': _L2_ffn_in['mlp_w1'], 'L2_ffn_mlp_b1': _L2_ffn_in['mlp_b1'], 'L2_ffn_mlp_w2': _L2_ffn_in['mlp_w2'], 'L2_ffn_mlp_b2': _L2_ffn_in['mlp_b2'], 'L2_ffn_ln2_g': _L2_ffn_in['ln2_g'], 'L2_ffn_ln2_b': _L2_ffn_in['ln2_b'], 'L2_ffn_gate_w': _L2_ffn_in['gate_w'], 'L2_ffn_gate_b': _L2_ffn_in['gate_b'], 'L2_ffn_exp_w1': _L2_ffn_in['exp_w1'], 'L2_ffn_exp_b1': _L2_ffn_in['exp_b1'], 'L2_ffn_exp_w2': _L2_ffn_in['exp_w2'], 'L2_ffn_exp_b2': _L2_ffn_in['exp_b2'], 'L3_attn_Wq': _L3_attn_in['Wq'], 'L3_attn_bq': _L3_attn_in['bq'], 'L3_attn_Wk': _L3_attn_in['Wk'], 'L3_attn_bk': _L3_attn_in['bk'], 'L3_attn_Wv': _L3_attn_in['Wv'], 'L3_attn_bv': _L3_attn_in['bv'], 'L3_attn_Wo': _L3_attn_in['Wo'], 'L3_attn_bo': _L3_attn_in['bo'], 'L3_ffn_g1': _L3_ffn_in['g1'], 'L3_ffn_b1': _L3_ffn_in['b1'], 'L3_ffn_g2': _L3_ffn_in['g2'], 'L3_ffn_b2': _L3_ffn_in['b2'], 'L3_ffn_Wr': _L3_ffn_in['Wr'], 'L3_ffn_br': _L3_ffn_in['br'], 'L3_ffn_Wq': _L3_ffn_in['Wq'], 'L3_ffn_bq': _L3_ffn_in['bq'], 'L3_ffn_Wk': _L3_ffn_in['Wk'], 'L3_ffn_bk': _L3_ffn_in['bk'], 'L3_ffn_Wv': _L3_ffn_in['Wv'], 'L3_ffn_bv': _L3_ffn_in['bv'], 'L3_ffn_Wo': _L3_ffn_in['Wo'], 'L3_ffn_bo': _L3_ffn_in['bo'], 'L3_ffn_Wm': _L3_ffn_in['Wm'], 'L3_ffn_bm': _L3_ffn_in['bm'], 'L3_ffn_W1': _L3_ffn_in['W1'], 'L3_ffn_bf1': _L3_ffn_in['bf1'], 'L3_ffn_W2': _L3_ffn_in['W2'], 'L3_ffn_bf2': _L3_ffn_in['bf2']}

def reference(x, cls_tok, L0_tok_conv_w, L0_tok_conv_b, L0_tok_pos_table, L0_attn_qA, L0_attn_qB, L0_attn_kA, L0_attn_kB, L0_attn_vA, L0_attn_vB, L0_attn_o_w, L0_ffn_gate_w, L0_ffn_gate_b, L0_ffn_w1, L0_ffn_b1, L0_ffn_w2, L0_ffn_b2, L1_attn_qkv_w, L1_attn_proj_w, L1_attn_proj_b, L1_attn_tab_kv, L1_attn_tab_kh, L1_attn_tab_vv, L1_attn_tab_vh, L1_ffn_Wg, L1_ffn_W1, L1_ffn_b1, L1_ffn_W2, L1_ffn_b2, L2_attn_qkv_w, L2_attn_proj_w, L2_attn_proj_b, L2_attn_rand_matrix, L2_ffn_ln1_g, L2_ffn_ln1_b, L2_ffn_in_w, L2_ffn_in_b, L2_ffn_out_w, L2_ffn_out_b, L2_ffn_mlp_w1, L2_ffn_mlp_b1, L2_ffn_mlp_w2, L2_ffn_mlp_b2, L2_ffn_ln2_g, L2_ffn_ln2_b, L2_ffn_gate_w, L2_ffn_gate_b, L2_ffn_exp_w1, L2_ffn_exp_b1, L2_ffn_exp_w2, L2_ffn_exp_b2, L3_attn_Wq, L3_attn_bq, L3_attn_Wk, L3_attn_bk, L3_attn_Wv, L3_attn_bv, L3_attn_Wo, L3_attn_bo, L3_ffn_g1, L3_ffn_b1, L3_ffn_g2, L3_ffn_b2, L3_ffn_Wr, L3_ffn_br, L3_ffn_Wq, L3_ffn_bq, L3_ffn_Wk, L3_ffn_bk, L3_ffn_Wv, L3_ffn_bv, L3_ffn_Wo, L3_ffn_bo, L3_ffn_Wm, L3_ffn_bm, L3_ffn_W1, L3_ffn_bf1, L3_ffn_W2, L3_ffn_bf2):
    import jax
    import jax.numpy as jnp

    def _L0_tok_ref(pixel_values, conv_w, conv_b, pos_table):
        import jax, jax.numpy as jnp
        import numpy as np
        from jax import lax
        HIDDEN = 192
        C_IN = 3
        PATCH = 16
        SIDE = 32
        NUM_PATCHES = SIDE * SIDE

        def _position_ids(nb_h, nb_w):
            boundaries = np.arange(1.0 / SIDE, 1.0, 1.0 / SIDE, dtype=np.float32)
            frac_h = np.arange(0.0, 1.0 - 1e-06, 1.0 / nb_h, dtype=np.float32)
            frac_w = np.arange(0.0, 1.0 - 1e-06, 1.0 / nb_w, dtype=np.float32)
            bh = np.searchsorted(boundaries, frac_h, side='right')
            bw = np.searchsorted(boundaries, frac_w, side='right')
            return jnp.asarray((bh[:, None] * SIDE + bw).reshape(-1), dtype=jnp.int32)
        B, _, H, W = pixel_values.shape
        nb_h, nb_w = (H // PATCH, W // PATCH)
        patches = lax.conv_general_dilated(pixel_values, conv_w, window_strides=(PATCH, PATCH), padding='VALID', dimension_numbers=('NCHW', 'OIHW', 'NCHW'))
        patches = patches + conv_b[None, :, None, None]
        embeddings = patches.reshape(B, HIDDEN, nb_h * nb_w).transpose(0, 2, 1)
        pos_ids = _position_ids(nb_h, nb_w)
        pos_emb = pos_table[pos_ids]
        return embeddings + pos_emb[None, :, :]

    def _L0_attn_ref(x, qA, qB, kA, kB, vA, vB, o_w):
        import jax, jax.numpy as jnp
        import numpy as np
        import math
        D_MODEL = 192
        N_HEADS = 6
        HD = D_MODEL // N_HEADS
        RANK = D_MODEL // 4
        B, T = (128, 64)

        def _rope_tables(T, dim):
            inv = 1.0 / 10000.0 ** (jnp.arange(0, dim, 2, dtype=jnp.float32) / dim)
            t = jnp.arange(T, dtype=jnp.float32)
            freqs = jnp.outer(t, inv)
            emb = jnp.concatenate([freqs, freqs], axis=-1)
            return (jnp.cos(emb), jnp.sin(emb))

        def _rot(x):
            h = x.shape[-1] // 2
            return jnp.concatenate([-x[..., h:], x[..., :h]], axis=-1)
        Bb, Tt, _ = x.shape

        def proj(A, W):
            h = x @ A @ W
            return h.reshape(Bb, Tt, N_HEADS, HD).transpose(0, 2, 1, 3)
        q = proj(qA, qB)
        k = proj(kA, kB)
        v = proj(vA, vB)
        cos, sin = _rope_tables(Tt, HD)
        q = q * cos + _rot(q) * sin
        k = k * cos + _rot(k) * sin
        att = jnp.einsum('bhqd,bhkd->bhqk', q, k) / math.sqrt(HD)
        causal = jnp.tril(jnp.ones((Tt, Tt), dtype=bool))
        att = jnp.where(causal, att, -jnp.inf)
        att = jax.nn.softmax(att, axis=-1)
        out = jnp.einsum('bhqk,bhkd->bhqd', att, v)
        out = out.transpose(0, 2, 1, 3).reshape(Bb, Tt, D_MODEL)
        return out @ o_w

    def _L0_ffn_ref(x, gate_w, gate_b, w1, b1, w2, b2):
        import jax, jax.numpy as jnp
        import numpy as np
        C = 192
        E = 32
        H = 4 * C
        gates = jax.nn.softmax(x @ gate_w + gate_b, axis=-1)
        h = jax.nn.gelu(jnp.einsum('btc,ech->bteh', x, w1) + b1, approximate=False)
        y = jnp.einsum('bteh,ehc->btec', h, w2) + b2
        out = jnp.einsum('bte,btec->btc', gates, y)
        return out

    def _L1_attn_ref(x, qkv_w, proj_w, proj_b, tab_kv, tab_kh, tab_vv, tab_vh):
        import jax, jax.numpy as jnp
        import numpy as np
        B, N, DIM = (16, 577, 192)
        HEADS, HEAD_DIM = (12, 64)
        QKV_DIM = HEADS * HEAD_DIM
        MAX_REL = 14
        TABLE_ROWS = 2 * MAX_REL + 2

        def _rel_indices(n, max_rel):
            m = n - 1
            side = int(m ** 0.5)
            r = np.arange(m)
            dv = r[None, :] // side - r[:, None] // side
            dh = r[None, :] % side - r[:, None] % side
            iv = np.clip(dv, -max_rel, max_rel) + max_rel + 1
            ih = np.clip(dh, -max_rel, max_rel) + max_rel + 1
            iv = np.pad(iv, ((1, 0), (1, 0)))
            ih = np.pad(ih, ((1, 0), (1, 0)))
            return (jnp.asarray(iv), jnp.asarray(ih))
        b, n, _ = x.shape
        scale = HEAD_DIM ** (-0.5)
        qkv = (x @ qkv_w.T).reshape(b, n, 3, HEADS, HEAD_DIM).transpose(2, 0, 3, 1, 4)
        q, k, v = (qkv[0], qkv[1], qkv[2])
        attn = jnp.einsum('bhqd,bhkd->bhqk', q, k) * scale
        iv, ih = _rel_indices(n, MAX_REL)
        r_p_k = tab_kv[iv] + tab_kh[ih]
        attn = attn + jnp.einsum('bhqd,qkd->bhqk', q, r_p_k) * scale
        attn = jax.nn.softmax(attn, axis=-1)
        out = jnp.einsum('bhqk,bhkd->bhqd', attn, v)
        r_p_v = tab_vv[iv] + tab_vh[ih]
        out = out + jnp.einsum('bhqk,qkd->bhqd', attn, r_p_v)
        out = out.transpose(0, 2, 1, 3).reshape(b, n, QKV_DIM)
        return out @ proj_w.T + proj_b

    def _L1_ffn_ref(hidden_states, Wg, W1, b1, W2, b2):
        import jax, jax.numpy as jnp
        import numpy as np
        B, S, D, F, E = (2, 256, 192, 768, 8)
        b, s, d = hidden_states.shape
        e = W1.shape[0]
        x = hidden_states.reshape(-1, d)
        logits = x @ Wg
        probs = jax.nn.softmax(logits, axis=-1)
        gate = jnp.max(probs, axis=-1)
        expert_idx = jnp.argmax(probs, axis=-1)
        h = jax.nn.silu(jnp.einsum('td,edf->etf', x, W1) + b1[:, None, :])
        y = jnp.einsum('etf,efd->etd', h, W2) + b2[:, None, :]
        combine = jax.nn.one_hot(expert_idx, e, dtype=x.dtype) * gate[:, None]
        out = jnp.einsum('te,etd->td', combine, y)
        return out.reshape(b, s, d)

    def _L2_attn_ref(x, qkv_w, proj_w, proj_b, rand_matrix):
        import jax, jax.numpy as jnp
        import numpy as np
        B, N, C, H = (8, 256, 192, 12)
        D = C // H
        M = 2 * D
        SCALE = D ** (-0.5)
        EPS = 1e-12

        def _feature_map(z, rand_matrix):
            logits = jnp.einsum('bhnd,hdm->bhnm', z, rand_matrix)
            sqnorm = 0.5 * jnp.sum(z * z, axis=-1, keepdims=True)
            return jnp.exp(logits - sqnorm) * M ** (-0.5)
        b, n, c = x.shape
        qkv = (x @ qkv_w.T).reshape(b, n, 3, H, D).transpose(2, 0, 3, 1, 4)
        q, k, v = (qkv[0], qkv[1], qkv[2])
        sq = SCALE ** 0.5
        qf = _feature_map(q * sq, rand_matrix)
        kf = _feature_map(k * sq, rand_matrix)
        attn = jnp.einsum('bhnm,bhkm->bhnk', qf, kf)
        denom = jnp.maximum(jnp.sum(jnp.abs(attn), axis=-1, keepdims=True), EPS)
        attn = attn / denom
        out = jnp.einsum('bhnk,bhkd->bhnd', attn, v)
        out = out.transpose(0, 2, 1, 3).reshape(b, n, c)
        return out @ proj_w.T + proj_b

    def _L2_ffn_ref(x, ln1_g, ln1_b, in_w, in_b, out_w, out_b, mlp_w1, mlp_b1, mlp_w2, mlp_b2, ln2_g, ln2_b, gate_w, gate_b, exp_w1, exp_b1, exp_w2, exp_b2):
        import jax, jax.numpy as jnp
        import numpy as np
        E = 192
        H = 12
        D = E // H
        HID = 768
        NEXP = 4
        TOPK = 2
        EPS = 1e-05

        def _ln(x, g, b):
            m = jnp.mean(x, axis=-1, keepdims=True)
            v = jnp.mean(jnp.square(x - m), axis=-1, keepdims=True)
            return (x - m) * jax.lax.rsqrt(v + EPS) * g + b
        B, N, _ = x.shape
        h = _ln(x, ln1_g, ln1_b)
        qkv = h @ in_w.T + in_b
        q, k, v = jnp.split(qkv, 3, axis=-1)
        q = q.reshape(B, N, H, D)
        k = k.reshape(B, N, H, D)
        v = v.reshape(B, N, H, D)
        scores = jnp.einsum('bqhd,bkhd->bhqk', q, k) / jnp.sqrt(jnp.float32(D))
        attn = jax.nn.softmax(scores, axis=-1)
        ctx = jnp.einsum('bhqk,bkhd->bqhd', attn, v).reshape(B, N, E)
        x = x + ctx @ out_w.T + out_b
        x = x + jax.nn.gelu(x @ mlp_w1 + mlp_b1, approximate=False) @ mlp_w2 + mlp_b2
        xm = _ln(x, ln2_g, ln2_b)
        logits = xm @ gate_w.T + gate_b
        topv, topi = jax.lax.top_k(logits, TOPK)
        gates = jax.nn.softmax(topv, axis=-1)
        onehot = jax.nn.one_hot(topi, NEXP, dtype=x.dtype)
        comb = jnp.einsum('bnk,bnke->bne', gates, onehot)
        moe_out = jnp.zeros_like(x)
        for e in range(NEXP):
            he = jax.nn.gelu(xm @ exp_w1[e] + exp_b1[e], approximate=False)
            oe = he @ exp_w2[e] + exp_b2[e]
            moe_out = moe_out + comb[..., e:e + 1] * oe
        return x + moe_out

    def _L3_attn_ref(x, Wq, bq, Wk, bk, Wv, bv, Wo, bo):
        import jax, jax.numpy as jnp
        import numpy as np
        LOG2E = 1.4426950408889634
        NUM_HEADS = 12

        def fake_quant_sym8(x):
            scale = jnp.maximum(jnp.max(jnp.abs(x)) / 127.0, 1e-08)
            q = jnp.clip(jnp.round(x / scale), -128.0, 127.0) * scale
            return x + jax.lax.stop_gradient(q - x)

        def integer_approx_softmax(x):
            z = x * LOG2E
            z = z - jnp.max(z, axis=-1, keepdims=True)
            zi = jnp.floor(z)
            zf = z - zi
            p = jnp.exp2(zi) * (1.0 + zf)
            return p / jnp.sum(p, axis=-1, keepdims=True)
        B, N, E = x.shape
        H = NUM_HEADS
        D = Wq.shape[1] // H
        xq = fake_quant_sym8(x)
        Q = (xq @ Wq + bq).reshape(B, N, H, D).transpose(0, 2, 1, 3)
        K = (xq @ Wk + bk).reshape(B, N, H, D).transpose(0, 2, 1, 3)
        V = (xq @ Wv + bv).reshape(B, N, H, D).transpose(0, 2, 1, 3)
        logits = jnp.einsum('bhnd,bhmd->bhnm', Q, K)
        attn = integer_approx_softmax(logits)
        ctx = jnp.einsum('bhnm,bhmd->bhnd', attn, V)
        ctx = ctx.transpose(0, 2, 1, 3).reshape(B, N, H * D)
        return ctx @ Wo + bo

    def _L3_ffn_ref(hidden_states, g1, b1, g2, b2, Wr, br, Wq, bq, Wk, bk, Wv, bv, Wo, bo, Wm, bm, W1, bf1, W2, bf2):
        import jax, jax.numpy as jnp
        import numpy as np
        B, L, D, H, F = (4, 512, 192, 12, 768)
        ROUTE_FRAC = 0.15
        LN_EPS = 1e-05

        def _ln(x, g, b):
            m = jnp.mean(x, axis=-1, keepdims=True)
            v = jnp.mean((x - m) ** 2, axis=-1, keepdims=True)
            return (x - m) * jax.lax.rsqrt(v + LN_EPS) * g + b
        b, l, d = hidden_states.shape
        dh = d // H
        normed = _ln(hidden_states, g1, b1)
        scores = jax.nn.sigmoid(jnp.einsum('bld,d->bl', normed, Wr) + br)
        k = max(1, int(round(ROUTE_FRAC * l)))
        _, idx = jax.lax.top_k(-scores, k)
        attn_mask = jnp.zeros((b, l), bool).at[jnp.arange(b)[:, None], idx].set(True)
        q = (normed @ Wq + bq).reshape(b, l, H, dh)
        kk = (normed @ Wk + bk).reshape(b, l, H, dh)
        v = (normed @ Wv + bv).reshape(b, l, H, dh)
        logits = jnp.einsum('blhd,bmhd->bhlm', q, kk) / jnp.sqrt(jnp.float32(dh))
        probs = jax.nn.softmax(logits, axis=-1)
        ctx = jnp.einsum('bhlm,bmhd->blhd', probs, v).reshape(b, l, d)
        attn_out = ctx @ Wo + bo
        w = scores / (jnp.sum(scores, axis=1, keepdims=True) + 1e-06)
        pooled = jnp.einsum('bl,bld->bd', w, normed)
        mix_out = (normed + scores[..., None] * pooled[:, None, :]) @ Wm + bm
        merged = jnp.where(attn_mask[..., None], attn_out, mix_out)
        h = hidden_states + merged
        n2 = _ln(h, g2, b2)
        ffn = jax.nn.gelu(n2 @ W1 + bf1, approximate=False) @ W2 + bf2
        return h + ffn
    h = _L0_tok_ref(x, L0_tok_conv_w, L0_tok_conv_b, L0_tok_pos_table)
    h = jnp.concatenate([jnp.broadcast_to(cls_tok, (h.shape[0], 1, h.shape[2])), h], axis=1)
    h = h + _L0_attn_ref(_layernorm(h, axis=-1), L0_attn_qA, L0_attn_qB, L0_attn_kA, L0_attn_kB, L0_attn_vA, L0_attn_vB, L0_attn_o_w)
    h = h + _L0_ffn_ref(_layernorm(h, axis=-1), L0_ffn_gate_w, L0_ffn_gate_b, L0_ffn_w1, L0_ffn_b1, L0_ffn_w2, L0_ffn_b2)
    h = h + _L1_attn_ref(_layernorm(h, axis=-1), L1_attn_qkv_w, L1_attn_proj_w, L1_attn_proj_b, L1_attn_tab_kv, L1_attn_tab_kh, L1_attn_tab_vv, L1_attn_tab_vh)
    h = h + _L1_ffn_ref(_layernorm(h, axis=-1), L1_ffn_Wg, L1_ffn_W1, L1_ffn_b1, L1_ffn_W2, L1_ffn_b2)
    h = h + _L2_attn_ref(_layernorm(h, axis=-1), L2_attn_qkv_w, L2_attn_proj_w, L2_attn_proj_b, L2_attn_rand_matrix)
    h = h + _L2_ffn_ref(_layernorm(h, axis=-1), L2_ffn_ln1_g, L2_ffn_ln1_b, L2_ffn_in_w, L2_ffn_in_b, L2_ffn_out_w, L2_ffn_out_b, L2_ffn_mlp_w1, L2_ffn_mlp_b1, L2_ffn_mlp_w2, L2_ffn_mlp_b2, L2_ffn_ln2_g, L2_ffn_ln2_b, L2_ffn_gate_w, L2_ffn_gate_b, L2_ffn_exp_w1, L2_ffn_exp_b1, L2_ffn_exp_w2, L2_ffn_exp_b2)
    h = h + _L3_attn_ref(_layernorm(h, axis=-1), L3_attn_Wq, L3_attn_bq, L3_attn_Wk, L3_attn_bk, L3_attn_Wv, L3_attn_bv, L3_attn_Wo, L3_attn_bo)
    h = h + _L3_ffn_ref(_layernorm(h, axis=-1), L3_ffn_g1, L3_ffn_b1, L3_ffn_g2, L3_ffn_b2, L3_ffn_Wr, L3_ffn_br, L3_ffn_Wq, L3_ffn_bq, L3_ffn_Wk, L3_ffn_bk, L3_ffn_Wv, L3_ffn_bv, L3_ffn_Wo, L3_ffn_bo, L3_ffn_Wm, L3_ffn_bm, L3_ffn_W1, L3_ffn_bf1, L3_ffn_W2, L3_ffn_bf2)
    return h

_drawn_inputs = setup_inputs


def setup_inputs(seed=0):
    import zlib

    import numpy as np

    out = dict(_drawn_inputs(seed))
    spreads = {'L0_tok_conv_b': (0.0, 0.1),
     'L0_ffn_gate_b': (0.0, 0.322),
     'L0_ffn_b1': (0.0, 0.273),
     'L0_ffn_b2': (0.0, 0.1),
     'L1_attn_proj_b': (0.0, 0.1),
     'L1_ffn_b1': (0.0, 0.712),
     'L1_ffn_b2': (0.0, 0.279),
     'L2_ffn_ln1_g': (1.0, 0.6),
     'L2_ffn_ln1_b': (0.0, 0.8),
     'L2_ffn_in_b': (0.0, 0.451),
     'L2_ffn_out_b': (0.0, 0.1),
     'L2_ffn_mlp_b1': (0.0, 0.432),
     'L2_ffn_mlp_b2': (0.0, 0.1),
     'L2_ffn_ln2_g': (1.0, 0.6),
     'L2_ffn_ln2_b': (0.0, 0.433),
     'L2_ffn_gate_b': (0.0, 0.284),
     'L2_ffn_exp_b1': (0.0, 0.529),
     'L2_ffn_exp_b2': (0.0, 0.1),
     'L3_attn_bq': (0.0, 0.8),
     'L3_attn_bk': (0.0, 2.0),
     'L3_attn_bv': (0.0, 0.506),
     'L3_attn_bo': (0.0, 0.1),
     'L3_ffn_g1': (1.0, 0.2),
     'L3_ffn_b1': (0.0, 0.631),
     'L3_ffn_g2': (1.0, 0.6),
     'L3_ffn_b2': (0.0, 2.0),
     'L3_ffn_bq': (0.0, 0.8),
     'L3_ffn_bk': (0.0, 2.0),
     'L3_ffn_bv': (0.0, 0.8),
     'L3_ffn_bo': (0.0, 0.526),
     'L3_ffn_bm': (0.0, 0.332),
     'L3_ffn_bf1': (0.0, 0.725),
     'L3_ffn_bf2': (0.0, 0.274)}
    factors = {'L1_attn_tab_kv': 8.0,
     'L1_attn_tab_kh': 64.0,
     'L1_attn_tab_vv': 5.798,
     'L1_attn_tab_vh': 7.016,
     'L2_attn_rand_matrix': 8.0,
     'L3_attn_Wq': 8.0,
     'L3_attn_Wk': 8.0,
     'L3_ffn_Wq': 8.0,
     'L3_ffn_Wk': 8.0,
     'L3_ffn_Wv': 8.0,
     'L3_ffn_Wo': 8.0}
    for name, (base, spread) in spreads.items():
        noise = np.random.default_rng([zlib.crc32(name.encode()), seed]).standard_normal(out[name].shape)
        drawn = base * np.exp(spread * noise) if base else spread * noise
        out[name] = jnp.asarray(drawn.astype(out[name].dtype))
    for name, factor in factors.items():
        out[name] = (out[name] * factor).astype(out[name].dtype)
    return out
```

```python
import numpy as np
import concourse.bass as bass
from concourse import mybir
from contextlib import ExitStack

F32 = mybir.dt.float32
F32R = mybir.dt.float32r
I32 = mybir.dt.int32
ALU = mybir.AluOpType
ACT = mybir.ActivationFunctionType
AX = mybir.AxisListType

D = 192
DA = 128
DB = D - DA
IMG, SLOT = 64, 26
SIDE = 5
TOK = IMG * SLOT
TILES = TOK // 128
HID = 768
HC = HID // 128
PIX = 768
BLOCKS = [(0, 3), (3, 3), (6, 3), (9, 4)]
RAW = 2 * HID + HC * D
START = 64
LN_EPS = 1e-5
LOG2E = 1.4426950408889634
BIG = 1.0e30


class Signal:

    def __init__(self, sem, at):
        self.sem, self.at = sem, at


class Attention:

    def __init__(self, dram, kind, H, d, G, qk, qcol, vcol, C, dve_steps, scale=1.0, bias=None, vb=None, ob=None,
                 no=2, R=96, NC=2, low_rank=False, mix=False):
        self.dram, self.kind, self.H, self.d, self.G = dram, kind, H, d, G
        self.qk, self.qcol, self.vcol, self.C, self.dve_steps = qk, qcol, vcol, C, dve_steps
        self.scale, self.bias, self.vb, self.ob, self.no = scale, bias, vb, ob, no
        self.R, self.NC, self.HCH, self.low_rank, self.mix = R, NC, H // NC, low_rank, mix




class Columns:

    def __init__(self, spec):
        self.at, self.n = {}, 0
        for name, width in spec:
            self.at[name] = (self.n, width)
            self.n += width

    def __getitem__(self, name):
        a, w = self.at[name]
        return slice(a, a + w)

    def lo(self, name):
        return self.at[name][0]


SHAPE_COLS = Columns([("ident", 128), ("head16", 6), ("head32", 3), ("head64", 2), ("cos", SLOT), ("sin", SLOT),
                      ("causal", SLOT), ("halfnorm", D), ("relv", 50), ("relh", 50), ("order8", 8)])
DATA_COLS = Columns([("L0_b1", 32 * HC), ("L1_b1", 8 * HC), ("L2m_b1", HC), ("L2e_b1", 4 * HC), ("L3_b1", HC),
                     ("L2f_qb", 2), ("L2f_kb", 2), ("L3a_qb", 2), ("L3a_kb", 2), ("L3f_qb", 2), ("L3f_kb", 2),
                     ("L1_ob", 2), ("L2a_ob", 2), ("L2f_ob", 2), ("L3a_ob", 2), ("L3f_ob", 2),
                     ("ln_L2f1", 4), ("ln_L2f2", 4), ("ln_L3f1", 4), ("ln_L3f2", 4),
                     ("L0_g", 64), ("L1_g", 16), ("L2_g", 8), ("L3_r", 4),
                     ("L0_b2", D), ("L1_b2", D), ("L2e_b2", D),
                     ("rand", 2 * D), ("tabk", 40), ("tabv", 64)])
ROW_COLS = Columns([("ones", 128), ("L0_gb", 32), ("L1_gb", 8), ("L2_gb", 4),
                    ("L3_br", 2), ("L2f_vb", D), ("L3a_vb", D), ("L3f_vb", D), ("L2m_b2", D), ("L3_b2", D),
                    ("L3_bo", D), ("L3_bm", D)])


def vit_tower(nc, a, out, stop=99):
    ctx = ExitStack()

    def sb(name, shape, dt=F32, scope=None):
        return (scope or ctx).enter_context(nc.sbuf_tensor(name, shape, dt))

    def pb(name):
        return ctx.enter_context(nc.psum_tensor(name, [128, 512], F32))

    signals = {}

    def signal(name, start=START):
        signals[name] = Signal(ctx.enter_context(nc.semaphore(name)), start)
        return signals[name]

    with ctx:
        h_tok = sb("h_tok", [128, TILES, D])
        y_tok = sb("y_tok", [128, TILES, D])
        n_tok = sb("n_tok", [128, TILES, D])
        feat = sb("feat", [128, 2, TOK])
        XP = TOK + 8
        xa_hi = sb("xa_hi", [128, XP], F32R)
        xa_lo = sb("xa_lo", [128, XP], F32R)
        xb = sb("xb", [128, XP], F32R)
        shp = sb("shp", [128, SHAPE_COLS.n])
        dat = sb("dat", [128, DATA_COLS.n])
        row = sb("row", [1, ROW_COLS.n])
        gate = sb("gate", [128, TILES, 32])
        gate_t = feat[0:32, 1, :]
        gsc = feat[:, 0, :].rearrange("p (k n) -> p k n", k=4)
        stats = sb("stats", [128, TILES, 6])
        mv = sb("mv", [128, TILES, 2])
        rstd = sb("rstd", [128, 4, TILES])
        sml = sb("sml", [128, 160])
        gw_hi = sb("gw_hi", [128, 2, 32], F32R)
        gw_lo = sb("gw_lo", [128, 2, 32], F32R)

        ex = ExitStack()
        raw = [sb(f"raw{j}", [128, RAW], scope=ex) for j in range(2)]
        w1_hi = [sb(f"w1_hi{j}", [128, 2, HID], F32R, ex) for j in range(2)]
        w1_lo = [sb(f"w1_lo{j}", [128, 2, HID], F32R, ex) for j in range(2)]
        w2 = [sb(f"w2_{j}", [128, HC, 2 * D], F32R, ex) for j in range(2)]
        hid = [sb(f"hid{j}", [128, 512], scope=ex) for j in range(3)]
        hid_hi = [sb(f"hid_hi{j}", [128, HC, 512], F32R, ex) for j in range(2)]
        hid_lo = [sb(f"hid_lo{j}", [128, HC, 512], F32R, ex) for j in range(2)]
        ex.close()

        cv = ExitStack()
        pix = sb("pix", [128, PIX // 128, TOK], scope=cv)
        conv_w = sb("conv_w", [128, PIX // 128, D], scope=cv)
        tok0 = sb("tok0", [128, TILES, D], scope=cv)
        conv_row = sb("conv_row", [1, TOK + D], scope=cv)
        cv.close()

        AW = 5760
        at = ExitStack()
        wp_hi = sb("wp_hi", [128, AW], F32R, at)
        wp_lo = sb("wp_lo", [128, AW], F32R, at)
        xs = sb("xs", [128, 3, 512], F32R, at)
        o_hi = sb("o_hi", [128, 6 * 208], F32R, at)
        o_lo = sb("o_lo", [128, 6 * 208], F32R, at)
        rw = ExitStack()
        wp_raw = sb("wp_raw", [128, AW], scope=rw)
        low = sb("low", [48, 3 * 256 + 5 * D], scope=rw)
        rw.close()
        q_t = sb("q_t", [128, 4 * 424], scope=at)
        k_t = sb("k_t", [128, 4, 416], scope=at)
        k_x = sb("k_x", [128, 12 * 416], scope=at)
        v_t = sb("v_t", [128, 4 * 384], scope=at)
        z_t = [sb(f"z_t{j}", [128, 12, SLOT], scope=at) for j in range(2)]
        p_t = [sb(f"p_t{j}", [128, 12, 32], scope=at) for j in range(2)]
        p_x = [sb(f"p_x{j}", [128, 12, 32], scope=at) for j in range(2)]
        o_t = [sb(f"o_t{j}", [128, HID], scope=at) for j in range(2)]
        o_f = sb("o_f", [128, 6 * 208], scope=at)
        m12 = sb("m12", [128, 4, 12], scope=at)
        rel = [sb(f"rel{j}", [128, 12, 20], scope=at) for j in range(2)]
        rel_p = sb("rel_p", [128, 12, 5, 10], scope=at)
        rel_u = sb("rel_u", [128, 2, 12, 5], scope=at)
        rel_a = sb("rel_a", [128, 12, 32], scope=at)
        rel_x = sb("rel_x", [128, 12, 32], scope=at)
        at.close()

        bank = [pb(f"bank{j}") for j in range(8)]

        names = ["consts_in", "phase_done", "dve_step", "act_step", "pool_step",
                 "w_in0", "w_in1", "w_split", "h_full", "h_act", "h_split", "y_full", "y_used", "att_in",
                 "job_full", "job_used", "staged", "qk_ready", "s_full", "s_used", "z_full", "p_full",
                 "px_full", "av_full", "av_used", "t_full", "t_used", "out_done", "bridge", "k_done",
                 "o_split", "it_dve", "holds"]
        s = {n: signal(n) for n in names}
        s["consts_in"].at = s["w_in0"].at = s["w_in1"].at = s["att_in"].at = s["out_done"].at = s["bridge"].at = 0
        s["phase_done"].at = 0

        phases = []

        def base(**adds):
            b = {k: signals[k].at for k in adds}
            for k, v in adds.items():
                signals[k].at += v
            return b

        def hold(eng):
            eng.sem_inc(s["holds"].sem, 1)

        def chain(eng, sig, n):
            def link(ins):
                ins.then_inc(sig.sem, 1)
                n[0] += 1
                eng.wait_ge(sig.sem, n[0])
            return link

        def bc(ap, shape):
            return ap.to_broadcast(shape)

        def conv_phase():
            b = base(job_full=TILES, job_used=TILES)

            def tensor(pe):
                pe.wait_ge(s["consts_in"].sem, 16 * CONSTS)
                for t in range(TILES):
                    o = bank[t % 8][:, 0:D]
                    if t >= 8:
                        pe.wait_ge(s["job_used"].sem, b["job_used"] + t - 7)
                    for c in range(PIX // 128):
                        nc.tensor.matmul(o, pix[:, c, 128 * t:128 * t + 128], conv_w[:, c, :],
                                         start=c == 0, stop=False)
                    nc.tensor.matmul(o, conv_row[0:1, 128 * t:128 * t + 128], conv_row[0:1, TOK:TOK + D],
                                     start=False, stop=True).then_inc(s["job_full"].sem, 1)

            def vector(dve):
                dve.wait_ge(s["consts_in"].sem, 16 * CONSTS)
                for t in range(TILES):
                    dve.wait_ge(s["job_full"].sem, b["job_full"] + t + 1)
                    nc.vector.tensor_tensor(h_tok[:, t, :], bank[t % 8][:, 0:D], tok0[:, t, :],
                                            ALU.add).then_inc(s["job_used"].sem, 1)
            phases.append(dict(tensor=tensor, vector=vector))

        def norm_phase(src, dst):
            b = base(dve_step=2 * TILES + 2, act_step=1)

            def vector(dve):
                for t in range(TILES):
                    nc.vector.bn_stats(stats[:, t, :], src[:, t, :]).then_inc(s["dve_step"].sem, 1)
                for t in range(TILES):
                    dve.wait_ge(s["dve_step"].sem, b["dve_step"] + t + 1)
                    nc.vector.bn_aggr(mv[:, t, :], stats[:, t, :]).then_inc(s["dve_step"].sem, 1)
                dve.wait_ge(s["dve_step"].sem, b["dve_step"] + 2 * TILES)
                nc.vector.tensor_scalar(rstd[:, 0, :], mv[:, :, 1], LN_EPS, None,
                                        ALU.add).then_inc(s["dve_step"].sem, 1)
                dve.wait_ge(s["act_step"].sem, b["act_step"] + 1)
                nc.vector.reciprocal(rstd[:, 2, :], rstd[:, 1, :]).then_inc(s["dve_step"].sem, 1)
                dve.wait_ge(s["dve_step"].sem, b["dve_step"] + 2 * TILES + 2)
                for t in range(TILES):
                    nc.vector.tensor_scalar(dst[:, t, :], src[:, t, :], mv[:, t, 0:1], rstd[:, 2, t:t + 1],
                                            ALU.subtract, ALU.mult)

            def scalar(act):
                act.wait_ge(s["dve_step"].sem, b["dve_step"] + 2 * TILES + 1)
                nc.scalar.activation(rstd[:, 1, :], rstd[:, 0, :], ACT.Sqrt).then_inc(s["act_step"].sem, 1)
            phases.append(dict(vector=vector, scalar=scalar))

        def transpose_b(o, x):
            ident = shp[:, SHAPE_COLS["ident"]]
            nc.tensor.transpose(o, x[:, DB:D], ident)
            return nc.tensor.transpose(o[0:DB, :], x[:, DA:D], ident)

        TBLK = [(0, 4), (4, 4), (8, 4), (12, 1)]

        def features_phase(src, ln=None):
            b = base(t_full=4, t_used=4, dve_step=8)
            ident = shp[:, SHAPE_COLS["ident"]]

            def tensor(pe):
                for i, (t0, n) in enumerate(TBLK):
                    pa, pbk = bank[2 * (i % 2)], bank[2 * (i % 2) + 1]
                    if i >= 2:
                        pe.wait_ge(s["t_used"].sem, b["t_used"] + i - 1)
                    for j in range(n):
                        x = src[:, t0 + j, :]
                        nc.tensor.transpose(pa[:, 128 * j:128 * j + 128], x[:, 0:DA], ident)
                        ins = transpose_b(pbk[:, 128 * j:128 * j + 128], x)
                    ins.then_inc(s["t_full"].sem, 1)

            def scalar(act):
                for i, (t0, n) in enumerate(TBLK):
                    act.wait_ge(s["t_full"].sem, b["t_full"] + i + 1)
                    for part in range(2):
                        p = bank[2 * (i % 2) + part][:, 0:128 * n]
                        o = feat[:, part, 128 * t0:128 * (t0 + n)]
                        if ln is None:
                            ins = nc.scalar.activation(o, p, ACT.Identity)
                        else:
                            g = DATA_COLS.lo(ln) + part
                            ins = nc.scalar.activation(o, p, ACT.Identity, bias=dat[:, g + 2:g + 3],
                                                       scale=dat[:, g:g + 1])
                    ins.then_inc(s["t_used"].sem, 1)

            def vector(dve):
                n_step = b["dve_step"]
                for i, (t0, n) in enumerate(TBLK):
                    dve.wait_ge(s["t_used"].sem, b["t_used"] + i + 1)
                    c = slice(128 * t0, 128 * (t0 + n))
                    nc.vector.tensor_copy(xa_hi[:, c], feat[:, 0, c])
                    nc.vector.tensor_copy(xb[:, c], feat[:, 1, c]).then_inc(s["dve_step"].sem, 1)
                    n_step += 1
                    dve.wait_ge(s["dve_step"].sem, n_step)
                    nc.vector.tensor_tensor(xa_lo[:, c], feat[:, 0, c], xa_hi[:, c].bitcast(F32), ALU.subtract)
                    nc.vector.tensor_tensor(xb[64:128, c], feat[64:128, 1, c], xb[64:128, c].bitcast(F32),
                                            ALU.subtract).then_inc(s["dve_step"].sem, 1)
                    n_step += 1
            phases.append(dict(tensor=tensor, scalar=scalar, vector=vector))

        def five(o, wh, wl, xh, xl, xbt, w_first, start=True, stop=True):
            parts = [(wh[0], xh), (wh[0], xl), (wl[0], xh), (wh[1], xbt), (wl[1], xbt)]
            for n, (w, x) in enumerate(parts):
                l, r = (w, x) if w_first else (x, w)
                ins = nc.tensor.matmul(o, l, r, start=start and n == 0, stop=stop and n == 4)
            return ins

        def gates_phase(E, g_col, gb_col, kind):
            steps = {"softmax": 8, "top1": 12, "top2": 24}[kind]
            b = base(dve_step=steps, job_full=2, t_full=TILES, t_used=TILES, act_step=1)
            n3 = [128, TILES, E]

            def v3(k):
                return gsc[:, k, 0:TILES * E].rearrange("p (t e) -> p t e", e=E)
            G = gate[:, :, 0:E]

            def tensor(pe):
                pe.wait_ge(s["dve_step"].sem, b["dve_step"] + 2)
                for t in range(TILES):
                    c = slice(128 * t, 128 * t + 128)
                    o = bank[0][:, E * t:E * t + E]
                    ins = five(o, [gw_hi[:, 0, 0:E], gw_hi[:, 1, 0:E]], [gw_lo[:, 0, 0:E], gw_lo[:, 1, 0:E]],
                               xa_hi[:, c], xa_lo[:, c], xb[:, c], False, stop=not gb_col)
                    if gb_col:
                        ins = nc.tensor.matmul(o, row[0:1, ROW_COLS["ones"]], row[0:1, ROW_COLS[gb_col]],
                                               start=False, stop=True)
                ins.then_inc(s["job_full"].sem, 1)
                pe.wait_ge(s["job_full"].sem, b["job_full"] + 2)
                for t in range(TILES):
                    if t >= 4:
                        pe.wait_ge(s["t_used"].sem, b["t_used"] + t - 3)
                    nc.tensor.transpose(bank[1 + t % 4][0:E, 0:128], gate[:, t, 0:E],
                                        shp[:, SHAPE_COLS["ident"]]).then_inc(s["t_full"].sem, 1)

            def scalar(act):
                act.wait_ge(s["dve_step"].sem, b["dve_step"] + (5 if kind != "top2" else 14))
                nc.scalar.activation(v3(1) if kind != "top2" else gsc[:, 1, 0:TILES],
                                     v3(0) if kind != "top2" else gsc[:, 0, 0:TILES], ACT.Exp)\
                    .then_inc(s["act_step"].sem, 1)
                for t in range(TILES):
                    act.wait_ge(s["t_full"].sem, b["t_full"] + t + 1)
                    nc.scalar.activation(gate_t[0:E, 128 * t:128 * t + 128], bank[1 + t % 4][0:E, 0:128],
                                         ACT.Identity).then_inc(s["t_used"].sem, 1)

            def vector(dve):
                n = [b["dve_step"]]
                link = chain(dve, s["dve_step"], n)
                w = dat[:, DATA_COLS[g_col]].rearrange("p (k e) -> p k e", k=2)
                link(nc.vector.tensor_copy(gw_hi[:, :, 0:E], w))
                link(nc.vector.tensor_tensor(gw_lo[:, :, 0:E], w, gw_hi[:, :, 0:E].bitcast(F32), ALU.subtract))
                dve.wait_ge(s["job_full"].sem, b["job_full"] + 1)
                lg = bank[0][:, 0:TILES * E].rearrange("p (t e) -> p t e", e=E)
                link(nc.vector.tensor_copy(v3(3), lg))
                mx = sml[:, 0:TILES]

                def first_of(eq_src, target, dst):
                    order = shp[:, SHAPE_COLS["order8"]][:, 0:E].unsqueeze(1).to_broadcast(n3)
                    link(nc.vector.tensor_tensor(dst, eq_src, bc(target.unsqueeze(2), n3), ALU.is_equal))
                    link(nc.vector.tensor_tensor(dst, dst, order, ALU.mult))
                    link(nc.vector.tensor_reduce(sml[:, 48:48 + TILES], dst, AX.X, ALU.max))
                    link(nc.vector.tensor_tensor(dst, dst, bc(sml[:, 48:48 + TILES].unsqueeze(2), n3),
                                                 ALU.is_equal))
                link(nc.vector.tensor_reduce(mx, v3(3), AX.X, ALU.max))
                if kind != "top2":
                    link(nc.vector.tensor_tensor(v3(0), v3(3), bc(mx.unsqueeze(2), n3), ALU.subtract))
                    dve.wait_ge(s["act_step"].sem, b["act_step"] + 1)
                    link(nc.vector.tensor_reduce(sml[:, 16:16 + TILES], v3(1), AX.X, ALU.add))
                    link(nc.vector.reciprocal(sml[:, 32:32 + TILES], sml[:, 16:16 + TILES]))
                    inv = bc(sml[:, 32:32 + TILES].unsqueeze(2), n3)
                    if kind == "softmax":
                        link(nc.vector.tensor_tensor(G, v3(1), inv, ALU.mult))
                    else:
                        first_of(v3(3), mx, v3(2))
                        link(nc.vector.tensor_tensor(G, v3(2), inv, ALU.mult))
                else:
                    m2 = sml[:, 64:64 + TILES]
                    first_of(v3(3), mx, v3(2))
                    link(nc.vector.tensor_scalar(v3(1), v3(2), -BIG, None, ALU.mult))
                    link(nc.vector.tensor_tensor(v3(1), v3(1), v3(3), ALU.add))
                    link(nc.vector.tensor_reduce(m2, v3(1), AX.X, ALU.max))
                    link(nc.vector.tensor_copy(v3(3), v3(1)))
                    first = gsc[:, 0, 256:256 + TILES * E].rearrange("p (t e) -> p t e", e=E)
                    link(nc.vector.tensor_copy(first, v3(2)))
                    link(nc.vector.tensor_tensor(gsc[:, 0, 0:TILES], m2, mx, ALU.subtract))
                    dve.wait_ge(s["act_step"].sem, b["act_step"] + 1)
                    e2 = gsc[:, 1, 0:TILES]
                    link(nc.vector.tensor_scalar(sml[:, 16:16 + TILES], e2, 1.0, None, ALU.add))
                    link(nc.vector.reciprocal(sml[:, 32:32 + TILES], sml[:, 16:16 + TILES]))
                    link(nc.vector.tensor_tensor(sml[:, 80:80 + TILES], e2, sml[:, 32:32 + TILES], ALU.mult))
                    first_of(v3(3), m2, v3(2))
                    link(nc.vector.tensor_tensor(v3(2), v3(2), bc(sml[:, 80:80 + TILES].unsqueeze(2), n3),
                                                 ALU.mult))
                    link(nc.vector.tensor_tensor(first, first, bc(sml[:, 32:32 + TILES].unsqueeze(2), n3),
                                                 ALU.mult))
                    link(nc.vector.tensor_tensor(G, first, v3(2), ALU.add))
                assert n[0] == b["dve_step"] + steps
                dve.sem_inc(s["job_full"].sem, 1)
            phases.append(dict(tensor=tensor, scalar=scalar, vector=vector))

        def experts_phase(E, dram, b1_col, b2_col, res, func):
            b = base(w_split=4 * E, h_full=24 * E, h_act=24 * E, h_split=24 * E, y_full=TILES * (E + 1),
                     y_used=TILES * (E + 1), dve_step=(24 + TILES) * E,
                     w_in0=16 * ((E + 1) // 2), w_in1=16 * (E // 2))
            w_in = [s["w_in0"], s["w_in1"]]
            w_in_at = [b["w_in0"], b["w_in1"]]
            STEPS = 24 + TILES
            barrier = len(phases)

            def over_experts(eng, body, first=0):
                if E == 1:
                    body(0, 0, 0)
                else:
                    with eng.Fori(0, E // 2) as i:
                        body(2 * i, 0, i)
                        body(2 * i + 1, 1, i)

            def sync(sp):
                sp.wait_ge(s["phase_done"].sem, 4 * barrier)
                for e in range(min(E, 2)):
                    sp.dma_start(raw[e][:, :], dram[e]).then_inc(w_in[e].sem, 16)
                if E > 2:
                    with sp.Fori(0, E // 2 - 1) as i:
                        for j in range(2):
                            sp.wait_ge(s["w_split"].sem, b["w_split"] + 4 * (2 * i + j + 1))
                            sp.dma_start(raw[j][:, :], dram[bass.ds(2 * i + j + 2, 1)]
                                         .rearrange("o p n -> p (o n)")).then_inc(w_in[j].sem, 16)

            def gpsimd(pool):
                def body(e, j, i):
                    pool.wait_ge(w_in[j].sem, w_in_at[j] + 16 * (i + 1))
                    pool.wait_ge(s["y_full"].sem, b["y_full"] + TILES + TILES * (e - 1))
                    hold(pool)
                    r1 = raw[j][:, 0:2 * HID].rearrange("p (k n) -> p k n", k=2)
                    r2 = raw[j][:, 2 * HID:RAW].rearrange("p (c n) -> p c n", c=HC)
                    nc.gpsimd.tensor_copy(w1_hi[j][:, :, :], r1).then_inc(s["w_split"].sem, 1)
                    nc.gpsimd.tensor_copy(w2[j][:, :, 0:D], r2).then_inc(s["w_split"].sem, 1)
                    pool.wait_ge(s["w_split"].sem, b["w_split"] + 4 * e + 1)
                    nc.gpsimd.tensor_tensor(w1_lo[j][:, :, :], r1, w1_hi[j][:, :, :].bitcast(F32),
                                            ALU.subtract).then_inc(s["w_split"].sem, 1)
                    pool.wait_ge(s["w_split"].sem, b["w_split"] + 4 * e + 2)
                    nc.gpsimd.tensor_tensor(w2[j][:, :, D:2 * D], r2, w2[j][:, :, 0:D].bitcast(F32),
                                            ALU.subtract).then_inc(s["w_split"].sem, 1)
                over_experts(pool, body)

            def tensor(pe):
                for t in range(TILES):
                    if t >= 4:
                        pe.wait_ge(s["y_used"].sem, b["y_used"] + t - 3)
                    if E == 1:
                        l, r = row[0:1, ROW_COLS["ones"]], row[0:1, ROW_COLS[b2_col]]
                    else:
                        l, r = gate_t[0:E, 128 * t:128 * t + 128], dat[0:E, DATA_COLS[b2_col]]
                    nc.tensor.matmul(bank[t % 4][:, 0:D], l, r, start=True, stop=True)\
                        .then_inc(s["y_full"].sem, 1)

                def up(e, j, k):
                    t0, nt = BLOCKS[k]
                    c = slice(128 * t0, 128 * (t0 + nt))
                    for m in range(HC):
                        n = 24 * e + 6 * k + m
                        pe.wait_ge(s["h_act"].sem, b["h_act"] + n - 3)
                        o = bank[4 + (6 * k + m) % 4][:, 0:128 * nt]
                        mc = slice(128 * m, 128 * m + 128)
                        five(o, [w1_hi[j][:, 0, mc], w1_hi[j][:, 1, mc]],
                             [w1_lo[j][:, 0, mc], w1_lo[j][:, 1, mc]],
                             xa_hi[:, c], xa_lo[:, c], xb[:, c], True).then_inc(s["h_full"].sem, 1)

                def down(e, j, k):
                    t0, nt = BLOCKS[k]
                    for t in range(nt):
                        n = TILES * (e + 1) + t0 + t
                        if t == 0:
                            pe.wait_ge(s["h_split"].sem, b["h_split"] + 24 * e + 6 * k + 6)
                        pe.wait_ge(s["y_used"].sem, b["y_used"] + n - (3 if t0 + t else 0))
                        o = bank[(t0 + t) % 4]
                        c = slice(128 * t, 128 * t + 128)
                        for m in range(HC):
                            nc.tensor.matmul(o[:, 0:2 * D], hid_hi[k % 2][:, m, c], w2[j][:, m, :],
                                             start=m == 0, stop=False)
                            ins = nc.tensor.matmul(o[:, 0:D], hid_lo[k % 2][:, m, c], w2[j][:, m, 0:D],
                                                   start=False, stop=m == HC - 1)
                        ins.then_inc(s["y_full"].sem, 1)

                def body(e, j, i):
                    pe.wait_ge(s["w_split"].sem, b["w_split"] + 4 * (e + 1))
                    up(e, j, 0)
                    for k in range(1, 4):
                        up(e, j, k)
                        down(e, j, k - 1)
                    down(e, j, 3)
                over_experts(pe, body)

            def scalar(act):
                def body(e, j, i):
                    for k, (t0, nt) in enumerate(BLOCKS):
                        for m in range(HC):
                            n = 24 * e + 6 * k + m
                            act.wait_ge(s["h_full"].sem, b["h_full"] + n + 1)
                            act.wait_ge(s["h_split"].sem, b["h_split"] + n - 2)
                            col = DATA_COLS.lo(b1_col) + m
                            hold(act)
                            bias = dat[:, col:col + 1] if E == 1 else dat[:, bass.ds(HC * e + col, 1)]
                            nc.scalar.activation(hid[(6 * k + m) % 3][:, 0:128 * nt],
                                                 bank[4 + (6 * k + m) % 4][:, 0:128 * nt], func,
                                                 bias=bias).then_inc(s["h_act"].sem, 1)
                over_experts(act, body)

            def vector(dve):
                for t in range(TILES):
                    dve.wait_ge(s["y_full"].sem, b["y_full"] + t + 1)
                    nc.vector.tensor_tensor(res[:, t, :], bank[t % 4][:, 0:D], res[:, t, :],
                                            ALU.add).then_inc(s["y_used"].sem, 1)

                def split(e, j, k):
                    t0, nt = BLOCKS[k]
                    w = 128 * nt
                    prev = [TILES * e + BLOCKS[3][0], TILES * (e + 1), TILES * (e + 1) + BLOCKS[1][0],
                            TILES * (e + 1) + BLOCKS[2][0]][k]
                    dve.wait_ge(s["y_full"].sem, b["y_full"] + prev)
                    for m in range(HC):
                        n = 24 * e + 6 * k + m
                        dve.wait_ge(s["h_act"].sem, b["h_act"] + n + 1)
                        h = hid[(6 * k + m) % 3][:, 0:w]
                        nc.vector.tensor_copy(hid_hi[k % 2][:, m, 0:w], h).then_inc(s["dve_step"].sem, 1)
                        dve.wait_ge(s["dve_step"].sem, b["dve_step"] + STEPS * e + 6 * k + m + 1
                                    + (BLOCKS[k - 1][0] if k > 1 else 0))
                        nc.vector.tensor_tensor(hid_lo[k % 2][:, m, 0:w], h,
                                                hid_hi[k % 2][:, m, 0:w].bitcast(F32),
                                                ALU.subtract).then_inc(s["h_split"].sem, 1)

                def gather(e, j, k):
                    t0, nt = BLOCKS[k]
                    for t in range(t0, t0 + nt):
                        n = TILES * (e + 1) + t
                        dve.wait_ge(s["y_full"].sem, b["y_full"] + n + 1)
                        o = bank[t % 4]
                        g = 1.0 if E == 1 else gate[:, t, bass.ds(e, 1)]
                        nc.vector.scalar_tensor_tensor(res[:, t, :], o[:, 0:D], g, res[:, t, :], ALU.mult,
                                                       ALU.add).then_inc(s["dve_step"].sem, 1)
                        done_splits = 6 * min(k + 2, 4)
                        dve.wait_ge(s["dve_step"].sem, b["dve_step"] + STEPS * e + done_splits + t + 1)
                        nc.vector.scalar_tensor_tensor(res[:, t, :], o[:, D:2 * D], g, res[:, t, :], ALU.mult,
                                                       ALU.add).then_inc(s["y_used"].sem, 1)

                def body(e, j, i):
                    split(e, j, 0)
                    for k in range(1, 4):
                        split(e, j, k)
                        gather(e, j, k - 1)
                    gather(e, j, 3)
                over_experts(dve, body)
            phases.append(dict(tensor=tensor, scalar=scalar, vector=vector, gpsimd=gpsimd, sync=sync))

        def add_back_phase(res):
            b = base(t_full=TILES, t_used=TILES)
            ident = shp[:, SHAPE_COLS["ident"]]

            def tensor(pe):
                for t in range(TILES):
                    if t >= 8:
                        pe.wait_ge(s["t_used"].sem, b["t_used"] + t - 7)
                    c = slice(128 * t, 128 * t + 128)
                    nc.tensor.transpose(bank[t % 8][:, 0:128], feat[:, 0, c], ident)
                    nc.tensor.transpose(bank[t % 8][:, 64:192], feat[:, 1, c], ident)\
                        .then_inc(s["t_full"].sem, 1)

            def vector(dve):
                for t in range(TILES):
                    dve.wait_ge(s["t_full"].sem, b["t_full"] + t + 1)
                    nc.vector.tensor_tensor(res[:, t, :], bank[t % 8][:, 0:D], res[:, t, :],
                                            ALU.add).then_inc(s["t_used"].sem, 1)
            phases.append(dict(tensor=tensor, vector=vector))

        def quantise_phase(x):
            b = base(dve_step=10, t_full=1, job_full=1)
            v = x[:, :, :].rearrange("p t d -> p (t d)")
            q = y_tok[:, :, :].rearrange("p t d -> p (t d)")
            top, one, sc, inv = (sml[:, 150 + j:151 + j] for j in range(4))

            def tensor(pe):
                pe.wait_ge(s["dve_step"].sem, b["dve_step"] + 1)
                nc.tensor.transpose(bank[0][0:1, 0:128], top, shp[:, SHAPE_COLS["ident"]])\
                    .then_inc(s["t_full"].sem, 1)
                pe.wait_ge(s["dve_step"].sem, b["dve_step"] + 4)
                nc.tensor.matmul(bank[1][:, 0:1], row[0:1, ROW_COLS["ones"]], one[0:1, :], start=True, stop=True)\
                    .then_inc(s["job_full"].sem, 1)

            def vector(dve):
                link = chain(dve, s["dve_step"], [b["dve_step"]])
                link(nc.vector.tensor_reduce(top, v, AX.X, ALU.max, apply_absolute_value=True))
                dve.wait_ge(s["t_full"].sem, b["t_full"] + 1)
                link(nc.vector.tensor_reduce(one[0:1, :], bank[0][0:1, 0:128], AX.X, ALU.max))
                link(nc.vector.tensor_scalar(one[0:1, :], one[0:1, :], 1.0 / 127.0, None, ALU.mult))
                link(nc.vector.tensor_scalar(one[0:1, :], one[0:1, :], 1e-8, None, ALU.max))
                dve.wait_ge(s["job_full"].sem, b["job_full"] + 1)
                link(nc.vector.tensor_copy(sc, bank[1][:, 0:1]))
                link(nc.vector.reciprocal(inv, sc))
                magic = 1.5 * 2.0 ** 23
                link(nc.vector.tensor_scalar(q, v, inv, magic, ALU.mult, ALU.add))
                link(nc.vector.tensor_scalar(q, q, magic, 127.0, ALU.subtract, ALU.min))
                link(nc.vector.tensor_scalar(q, q, -128.0, sc, ALU.max, ALU.mult))
                link(nc.vector.tensor_tensor(q, q, v, ALU.subtract))
                nc.vector.tensor_tensor(v, v, q, ALU.add)
            phases.append(dict(tensor=tensor, vector=vector))

        def route_phase():
            KEEP = max(1, int(round(0.15 * SLOT)))
            b = base(dve_step=9 + 4 * 2 + 4 * 4, job_full=4 + 12, job_used=4 + 12, bridge=112)
            turn_d = nc.dram_tensor("turn", (3, TOK), F32).ap()

            def by_image(k):
                return turn_d[k, :].rearrange("(m t) -> m t", t=SLOT)
            NJ = TOK // 4
            s_row, w_row, m_row = k_x[0:1, 0:TOK], k_t[0:1, :, :].rearrange("p c n -> p (c n)"), q_t[0:1, 0:TOK]
            s26, w26, m26 = (k_x[0:IMG, c:c + SLOT] for c in (1664, 1704, 1744))
            early, less, same = (k_x[0:IMG, c:c + SLOT * SLOT].rearrange("p (t u) -> p t u", u=SLOT)
                                 for c in (1800, 2500, 3200))
            total = k_x[0:IMG, 4000:4001]
            pool = sml[:, 0:2 * IMG].rearrange("p (c m) -> p c m", c=2)

            def sync(sp):
                sp.wait_ge(s["phase_done"].sem, 4 * ROUTE[0])
                sp.dma_start(k_x[0:IMG, 1800:1800 + SLOT * SLOT], a["earlier"]).then_inc(s["bridge"].sem, 16)
                sp.wait_ge(s["job_used"].sem, b["job_used"] + 4)
                sp.dma_start(turn_d[0:1, :], s_row).then_inc(s["bridge"].sem, 16)
                sp.wait_ge(s["bridge"].sem, b["bridge"] + 32)
                sp.dma_start(s26, by_image(0)).then_inc(s["bridge"].sem, 16)
                sp.wait_ge(s["dve_step"].sem, b["dve_step"] + 9)
                sp.dma_start(by_image(1), w26).then_inc(s["bridge"].sem, 16)
                sp.dma_start(by_image(2), m26).then_inc(s["bridge"].sem, 16)
                sp.wait_ge(s["bridge"].sem, b["bridge"] + 80)
                sp.dma_start(w_row, turn_d[1:2, :]).then_inc(s["bridge"].sem, 16)
                sp.dma_start(m_row, turn_d[2:3, :]).then_inc(s["bridge"].sem, 16)

            def tensor(pe):
                pe.wait_ge(s["dve_step"].sem, b["dve_step"] + 2)
                for j in range(4):
                    c = slice(NJ * j, NJ * (j + 1))
                    five(bank[j][0:2, 0:NJ], [gw_hi[:, 0, 0:2], gw_hi[:, 1, 0:2]],
                         [gw_lo[:, 0, 0:2], gw_lo[:, 1, 0:2]], xa_hi[:, c], xa_lo[:, c], xb[:, c], True)\
                        .then_inc(s["job_full"].sem, 1)
                pe.wait_ge(s["bridge"].sem, b["bridge"] + 112)
                for x in range(12):
                    r, j = BROADCAST[x]
                    pe.wait_ge(s["job_used"].sem, b["job_used"] + (4 if x < 4 else x + 1))
                    src = (w_row, s_row, m_row)[r]
                    nc.tensor.matmul(bank[4 + x % 4][:, 0:NJ], row[0:1, ROW_COLS["ones"]],
                                     src[:, NJ * j:NJ * (j + 1)], start=True, stop=True).then_inc(s["job_full"].sem, 1)

            def scalar(act):
                for j in range(4):
                    act.wait_ge(s["job_full"].sem, b["job_full"] + j + 1)
                    nc.scalar.activation(s_row[:, NJ * j:NJ * (j + 1)], bank[j][0:1, 0:NJ], ACT.Sigmoid,
                                         bias=row[0:1, ROW_COLS.lo("L3_br"):ROW_COLS.lo("L3_br") + 1])\
                        .then_inc(s["job_used"].sem, 1)

            def vector(dve):
                link = chain(dve, s["dve_step"], [b["dve_step"]])
                w = dat[:, DATA_COLS["L3_r"]].rearrange("p (k e) -> p k e", k=2)
                link(nc.vector.tensor_copy(gw_hi[:, :, 0:2], w))
                link(nc.vector.tensor_tensor(gw_lo[:, :, 0:2], w, gw_hi[:, :, 0:2].bitcast(F32), ALU.subtract))
                dve.wait_ge(s["bridge"].sem, b["bridge"] + 48)
                n3 = [IMG, SLOT, SLOT]
                su, st = s26.unsqueeze(1).to_broadcast(n3), s26.unsqueeze(2).to_broadcast(n3)
                nc.vector.tensor_tensor(less, su, st, ALU.is_lt)
                nc.vector.tensor_reduce(total, s26, AX.X, ALU.add)
                link(nc.vector.tensor_tensor(same, su, st, ALU.is_equal))
                nc.vector.tensor_scalar(row[0:1, ROW_COLS["L3_bm"]], row[0:1, ROW_COLS["L3_bm"]], -1.0, None,
                                        ALU.mult)
                link(nc.vector.tensor_tensor(same, same, early, ALU.mult))
                nc.vector.tensor_scalar(total, total, 1e-6, None, ALU.add)
                link(nc.vector.tensor_tensor(less, less, same, ALU.add))
                nc.vector.reciprocal(total, total)
                link(nc.vector.tensor_reduce(m26, less, AX.X, ALU.add))
                link(nc.vector.tensor_scalar(m26, m26, KEEP - 0.5, None, ALU.is_lt))
                link(nc.vector.tensor_scalar(w26, s26, total, None, ALU.mult))
                link(nc.vector.memset(sml[:, 140:141], 0.0))
                g3 = [128, NJ // SLOT, SLOT]
                for x in range(12):
                    r, j = BROADCAST[x]
                    dve.wait_ge(s["job_full"].sem, b["job_full"] + 4 + x + 1)
                    p = bank[4 + x % 4][:, 0:NJ]
                    c = slice(NJ * j, NJ * (j + 1))
                    mc = slice(NJ // SLOT * j, NJ // SLOT * (j + 1))
                    if r == 0:
                        nc.vector.tensor_tensor(o_f[:, 0:NJ], feat[:, 0, c], p, ALU.mult)
                        link(nc.vector.tensor_tensor(o_f[:, NJ:2 * NJ], feat[:, 1, c], p, ALU.mult))
                        nc.vector.tensor_reduce(pool[:, :, mc], o_f[:, 0:2 * NJ].rearrange(
                            "p (c m t) -> p c m t", c=2, t=SLOT), AX.X, ALU.add).then_inc(s["job_used"].sem, 1)
                        dve.wait_ge(s["job_used"].sem, b["job_used"] + 4 + x + 1)
                        link(nc.vector.memset(sml[:, 140:141], 0.0))
                    elif r == 1:
                        for k in range(2):
                            t = nc.vector.tensor_tensor(
                                o_f[:, NJ * k:NJ * (k + 1)].rearrange("p (m t) -> p m t", t=SLOT),
                                p.rearrange("p (m t) -> p m t", t=SLOT),
                                pool[:, k, mc].unsqueeze(2).to_broadcast(g3), ALU.mult)
                        t.then_inc(s["job_used"].sem, 1)
                        dve.wait_ge(s["job_used"].sem, b["job_used"] + 4 + x + 1)
                        link(nc.vector.tensor_tensor(feat[:, :, c], feat[:, :, c], o_f[:, 0:2 * NJ].rearrange(
                            "p (c n) -> p c n", c=2), ALU.add))
                    else:
                        nc.vector.tensor_copy(mask_b[:, c], p)
                        nc.vector.tensor_scalar(o_f[:, 0:NJ], p, -1.0, 1.0, ALU.mult, ALU.add)\
                            .then_inc(s["job_used"].sem, 1)
                        dve.wait_ge(s["job_used"].sem, b["job_used"] + 4 + x + 1)
                        link(nc.vector.tensor_tensor(feat[:, :, c], feat[:, :, c],
                                                     o_f[:, 0:NJ].unsqueeze(1).to_broadcast([128, 2, NJ]),
                                                     ALU.mult))
                for _ in range(8):
                    dve.sem_inc(s["dve_step"].sem, 1)
            BROADCAST = [(0, j) for j in range(4)] + [(r, j) for j in range(4) for r in (1, 2)]
            phases.append(dict(tensor=tensor, scalar=scalar, vector=vector, sync=sync))

        mask_b = n_tok[:, :, :].rearrange("p t d -> p (t d)")[:, 0:TOK]
        ROUTE = [0]

        def add_phase(dst, src):
            def vector(dve):
                nc.vector.tensor_tensor(dst[:, :, :], dst[:, :, :], src[:, :, :], ALU.add)
            phases.append(dict(vector=vector))

        def attention_weights_phase(cfg, after):
            cols = 2 * cfg.C + (cfg.no + (2 if cfg.mix else 0)) * D
            low_rank = cfg.low_rank
            b = base(att_in=32 if low_rank else 16, dve_step=1, job_full=10 if low_rank else 0,
                     job_used=10 if low_rank else 0)
            memsets = [xs[:, :, :], q_t[:, :]] + [p[:, :, :] for p in p_t] + [rel_a[:, :, :]]

            def sync(sp):
                sp.wait_ge(s["phase_done"].sem, 4 * after)
                if low_rank:
                    sp.dma_start(low[:, :], a[cfg.dram + "_low"]).then_inc(s["att_in"].sem, 16)
                    sp.dma_start(wp_raw[:, 2 * cfg.C:cols], a[cfg.dram]).then_inc(s["att_in"].sem, 16)
                else:
                    sp.dma_start(wp_raw[:, 0:cols], a[cfg.dram]).then_inc(s["att_in"].sem, 16)

            def tensor(pe):
                if not low_rank:
                    return
                pe.wait_ge(s["att_in"].sem, b["att_in"] + 32)
                for m in range(5):
                    f = (0, 0, 1, 1, 2)[m]
                    for k in range(2):
                        n = 2 * m + k
                        if n >= 4:
                            pe.wait_ge(s["job_used"].sem, b["job_used"] + n - 3)
                        nc.tensor.matmul(bank[n % 4][:, 0:D], low[:, 256 * f + 128 * k:256 * f + 128 * k + 128],
                                         low[:, 768 + D * m:768 + D * m + D], start=True, stop=True)\
                            .then_inc(s["job_full"].sem, 1)

            def scalar(act):
                if not low_rank:
                    return
                for m in range(5):
                    for k in range(2):
                        n = 2 * m + k
                        act.wait_ge(s["job_full"].sem, b["job_full"] + n + 1)
                        c = k * cfg.C + D * m
                        nc.scalar.activation(wp_raw[:, c:c + D], bank[n % 4][:, 0:D], ACT.Identity)\
                            .then_inc(s["job_used"].sem, 1)

            def vector(dve):
                dve.wait_ge(s["att_in"].sem, b["att_in"] + (32 if low_rank else 16))
                if low_rank:
                    dve.wait_ge(s["job_used"].sem, b["job_used"] + 10)
                nc.vector.tensor_copy(wp_hi[:, 0:cols], wp_raw[:, 0:cols]).then_inc(s["dve_step"].sem, 1)
                dve.wait_ge(s["dve_step"].sem, b["dve_step"] + 1)
                nc.vector.tensor_tensor(wp_lo[:, 0:cols], wp_raw[:, 0:cols], wp_hi[:, 0:cols].bitcast(F32),
                                        ALU.subtract)
            phases.append(dict(sync=sync, tensor=tensor, scalar=scalar, vector=vector))

            def clear(dve):
                for m in memsets:
                    nc.vector.memset(m.bitcast(F32) if m.dtype == F32R else m, 0.0)
            phases.append(dict(vector=clear))

        def attention_phase(cfg):
            G, R, NC, HCH, H, d, no = cfg.G, cfg.R, cfg.NC, cfg.HCH, cfg.H, cfg.d, cfg.no
            NI, n = IMG // (4 * G), 4 * G * SLOT
            QW = n + 8
            W = H * d
            halves = 2 if W > 512 else 1
            HH, WH = H // halves, W // halves
            qk = cfg.qk
            jobs = [("qk", x) for x in range(len(qk))]
            if cfg.kind == "performer":
                jobs += [("fq", c) for c in range(4)] + [("fk", c) for c in range(4)]
            JQ = len(jobs)
            jobs += [("v", (g, v)) for g in range(G) for v in range(halves)]
            JV = len(jobs)
            for step in range(G + 2):
                if step < G and cfg.kind == "rel":
                    jobs.append(("rel", step))
                if step >= 2:
                    jobs += [("t", (step - 2, v)) for v in range(halves)]
            JT = len(jobs)
            jobs += [("out", 0), ("out", 1)]
            J = len(jobs)
            at_job = {job: x for x, job in enumerate(jobs)}
            C = cfg.dve_steps
            b = base(job_full=J * NI, job_used=J * NI, staged=3 * NI, k_done=NI, s_full=16, s_used=16, z_full=16,
                     p_full=16, px_full=16, av_full=16 * halves, av_used=16 * halves, o_split=NI, it_dve=C * NI,
                     qk_ready=2 * NI, act_step=4 * NI)
            s_free, s_free_at = (s["z_full"], b["z_full"]) if cfg.kind == "softmax" else (s["s_used"], b["s_used"])
            heads = shp[0:R, SHAPE_COLS[{16: "head16", 32: "head32", 64: "head64"}[cfg.R // HCH]]]

            def w_part(w, k, c0, m):
                return w[:, k * cfg.C + c0:k * cfg.C + c0 + m]

            def w_pair(w, c0, m):
                return [w_part(w, 0, c0, m), w_part(w, 1, c0, m)]

            def qcols(c):
                return slice(c * QW, c * QW + n)

            def wo(w, k, c0):
                return w[:, 2 * cfg.C + k * D + c0:2 * cfg.C + k * D + c0 + 128]

            def bank_of(x):
                return bank[6 + x % 2]

            def gpsimd(pool):
                with pool.Fori(0, NI) as i:
                    pool.wait_ge(s["job_full"].sem, b["job_full"] + J * (i - 1) + (J if cfg.mix else JV))
                    hold(pool)
                    for p, x in enumerate((xa_hi, xa_lo, xb)):
                        o = xs_v(p, G)[:, :, 0:SLOT]
                        nc.gpsimd.tensor_copy(o, x[:, bass.ds(n * i, n)].rearrange("p (m s) -> p m s", s=SLOT))\
                            .then_inc(s["staged"].sem, 1)

            def xs_v(p, G):
                return xs[:, p, 0:128 * G].rearrange("p (m s) -> p m s", s=32)

            def tensor(pe):
                def job(i, name):
                    x = at_job[name]
                    pe.wait_ge(s["job_used"].sem, b["job_used"] + J * i + (x - 1 if x >= 2 else 0))
                    return bank_of(x)

                def xm(p):
                    return xs_v(p, G)[:, :, 0:SLOT]

                def scores(i, g):
                    t = G * i + g
                    pe.wait_ge(s_free.sem, s_free_at + t - 1)
                    if g == 0:
                        pe.wait_ge(s["k_done"].sem, b["k_done"] + i + 1)
                        pe.wait_ge(s["job_used"].sem, b["job_used"] + J * i + JQ)
                    o = bank[4 + g % 2]
                    for im in range(4):
                        m = SLOT * (4 * g + im)
                        for c in range(NC):
                            kx = k_x[0:R, c * HCH * n:(c + 1) * HCH * n].rearrange("p (h n) -> p h n", n=n)
                            w = HCH * SLOT
                            ins = nc.tensor.matmul(o[32 * im:32 * im + 32, c * w:(c + 1) * w],
                                                   q_t[0:R, c * QW + m:c * QW + m + 32], kx[:, :, m:m + SLOT],
                                                   start=True, stop=True)
                    ins.then_inc(s["s_full"].sem, 1)

                def rel_scores(i, g):
                    o = job(i, ("rel", g))
                    for im in range(4):
                        m = SLOT * (4 * g + im)
                        for c in range(NC):
                            ins = nc.tensor.matmul(o[32 * im:32 * im + 32, 40 * c:40 * c + 40],
                                                   q_t[0:R, c * QW + m:c * QW + m + 32],
                                                   dat[0:R, DATA_COLS["tabk"]], start=True, stop=True)
                    ins.then_inc(s["job_full"].sem, 1)

                def values(i, g):
                    t = G * i + g
                    pe.wait_ge(s["px_full"].sem, b["px_full"] + t + 1)
                    if g == 0:
                        pe.wait_ge(s["job_used"].sem, b["job_used"] + J * i + JV)
                    hold(pe)
                    for v in range(halves):
                        pe.wait_ge(s["av_used"].sem, b["av_used"] + halves * t + v)
                        hold(pe)
                        for im in range(4):
                            p0 = 32 * im
                            for h in range(v * HH, v * HH + HH):
                                o = bank[im][p0:p0 + 32, (h - v * HH) * d:(h - v * HH) * d + d]
                                ins = nc.tensor.matmul(o, p_x[g % 2][p0:p0 + SLOT, h, :],
                                                       v_t[p0:p0 + SLOT, g * W + h * d:g * W + h * d + d],
                                                       start=True, stop=cfg.kind != "rel")
                                if cfg.kind == "rel":
                                    ins = nc.tensor.matmul(o, rel_x[p0:p0 + 20, h, :],
                                                           dat[p0:p0 + 20, DATA_COLS["tabv"]],
                                                           start=False, stop=True)
                        ins.then_inc(s["av_full"].sem, 1)

                def turn(i, g):
                    t = G * i + g
                    pe.wait_ge(s["av_used"].sem, b["av_used"] + halves * (t + 1))
                    x = o_t[g % 2]
                    if no == 2:
                        o = job(i, ("t", (g, 0)))
                        nc.tensor.transpose(o[:, 0:128], x[:, 0:128], shp[:, SHAPE_COLS["ident"]])
                        transpose_b(o[:, 128:256], x[:, 0:D]).then_inc(s["job_full"].sem, 1)
                    else:
                        for v in range(2):
                            o = job(i, ("t", (g, v)))
                            for k in range(3):
                                ins = nc.tensor.transpose(o[:, 128 * k:128 * k + 128],
                                                          x[:, 128 * (3 * v + k):128 * (3 * v + k) + 128],
                                                          shp[:, SHAPE_COLS["ident"]])
                            ins.then_inc(s["job_full"].sem, 1)

                with pe.Fori(0, NI) as i:
                    pe.wait_ge(s["staged"].sem, b["staged"] + 3 * (i + 1))
                    for x in range(len(qk)):
                        o = job(i, ("qk", x))
                        c0 = cfg.qcol(x)
                        five(o[0:R, 0:n], w_pair(wp_hi, c0, R), w_pair(wp_lo, c0, R), xm(0), xm(1), xm(2),
                             True).then_inc(s["job_full"].sem, 1)
                    if cfg.kind == "performer":
                        for f, first in (("fq", 0), ("fk", 2)):
                            pe.wait_ge(s["qk_ready"].sem, b["qk_ready"] + 2 * i + (1 if f == "fq" else 2))
                            for c in range(4):
                                o = job(i, (f, c))[0:96, 0:n]
                                r0 = DATA_COLS.lo("rand") + D * (c // 2) + 96 * (c % 2)
                                h0 = SHAPE_COLS.lo("halfnorm") + 96 * (c % 2)
                                nc.tensor.matmul(o, dat[0:96, r0:r0 + 96], k_t[0:96, first + c // 2, 0:n],
                                                 start=True, stop=False)
                                nc.tensor.matmul(o, shp[0:96, h0:h0 + 96],
                                                 o_f[0:96, n * (c // 2):n * (c // 2) + n],
                                                 start=False, stop=True).then_inc(s["job_full"].sem, 1)
                    for g in range(G):
                        for v in range(halves):
                            o = job(i, ("v", (g, v)))[:, 0:WH]
                            c0 = cfg.vcol + WH * v
                            gc = slice(128 * g, 128 * g + 128)
                            ins = five(o, w_pair(wp_hi, c0, WH), w_pair(wp_lo, c0, WH), xs[:, 0, gc],
                                       xs[:, 1, gc], xs[:, 2, gc], False, stop=not cfg.vb)
                            if cfg.vb:
                                ins = nc.tensor.matmul(o, row[0:1, ROW_COLS["ones"]], row[0:1, ROW_COLS[cfg.vb]],
                                                       start=False, stop=True)
                            ins.then_inc(s["job_full"].sem, 1)
                    for step in range(G + 2):
                        if step < G:
                            scores(i, step)
                            if cfg.kind == "rel":
                                rel_scores(i, step)
                        if 1 <= step <= G:
                            values(i, step - 1)
                        if step >= 2:
                            turn(i, step - 2)
                    pe.wait_ge(s["o_split"].sem, b["o_split"] + i + 1)
                    for k in range(2):
                        o = job(i, ("out", k))[:, 0:n]
                        c0 = 64 * k
                        if no == 2:
                            ins = five(o, [wo(wp_hi, 0, c0), wo(wp_hi, 1, c0)], [wo(wp_lo, 0, c0), wo(wp_lo, 1, c0)],
                                       o_hi[:, 0:n], o_lo[:, 0:n], o_hi[:, n:2 * n], True, stop=not cfg.mix)
                            if cfg.mix:
                                five(o, [wo(wp_hi, 2, c0), wo(wp_hi, 3, c0)], [wo(wp_lo, 2, c0), wo(wp_lo, 3, c0)],
                                     xs[:, 0, 0:n], xs[:, 1, 0:n], xs[:, 2, 0:n], True, start=False, stop=False)
                                for y, name in enumerate(("L3_bo", "L3_bm")):
                                    r0 = ROW_COLS.lo(name) + c0
                                    ins = nc.tensor.matmul(o, row[0:1, r0:r0 + 128], mask_b[0:1, bass.ds(n * i, n)],
                                                           start=False, stop=y == 1)
                        else:
                            for f in range(no):
                                fc = slice(n * f, n * f + n)
                                nc.tensor.matmul(o, wo(wp_hi, f, c0), o_hi[:, fc], start=f == 0, stop=False)
                                nc.tensor.matmul(o, wo(wp_hi, f, c0), o_lo[:, fc], start=False, stop=False)
                                ins = nc.tensor.matmul(o, wo(wp_lo, f, c0), o_hi[:, fc], start=False,
                                                       stop=f == no - 1)
                        ins.then_inc(s["job_full"].sem, 1)

            def scalar(act):
                def job(i, name):
                    x = at_job[name]
                    act.wait_ge(s["job_full"].sem, b["job_full"] + J * i + x + 1)
                    return bank_of(x)

                with act.Fori(0, NI) as i:
                    act.wait_ge(s["k_done"].sem, b["k_done"] + i)
                    act.wait_ge(s["o_split"].sem, b["o_split"] + i)
                    for x, (kind, c) in enumerate(qk):
                        p = job(i, ("qk", x))[0:R, 0:n]
                        dst = {"q": q_t[0:R, qcols(c)], "k": k_t[0:R, c % 4, 0:n],
                               "qr": o_f[0:R, n * (c % 2):n * (c % 2) + n], "kr": k_t[0:R, (2 + c) % 4, 0:n]}[kind]
                        if cfg.kind == "performer":
                            dst = k_t[0:R, x, 0:n]
                            ins = nc.scalar.activation(dst, p, ACT.Identity, scale=float(cfg.d) ** -0.25)
                        elif cfg.bias:
                            col = DATA_COLS.lo(cfg.bias + {"q": "_qb", "k": "_kb"}[kind]) + c
                            ins = nc.scalar.activation(dst, p, ACT.Identity, bias=dat[0:R, col:col + 1])
                        else:
                            if cfg.kind == "rel" and kind == "k" and c >= 4:
                                act.wait_ge(s["act_step"].sem, b["act_step"] + 4 * i + c - 3)
                            ins = nc.scalar.activation(dst, p, ACT.Identity)
                        ins.then_inc(s["job_used"].sem, 1)
                    if cfg.kind == "performer":
                        for f, first in (("fq", 0), ("fk", 2)):
                            act.wait_ge(s["job_used"].sem, b["job_used"] + J * i + (4 if f == "fq" else 8))
                            for c in range(2):
                                ins = nc.scalar.activation(o_f[0:96, n * c:n * c + n], k_t[0:96, first + c, 0:n],
                                                           ACT.Square)
                            ins.then_inc(s["qk_ready"].sem, 1)
                            for c in range(4):
                                dst = q_t[0:96, qcols(c)] if f == "fq" else k_t[0:96, c, 0:n]
                                nc.scalar.activation(dst, job(i, (f, c))[0:96, 0:n], ACT.Exp)\
                                    .then_inc(s["job_used"].sem, 1)
                    for g in range(G):
                        for v in range(halves):
                            nc.scalar.activation(v_t[:, g * W + WH * v:g * W + WH * v + WH],
                                                 job(i, ("v", (g, v)))[:, 0:WH], ACT.Identity)\
                                .then_inc(s["job_used"].sem, 1)
                    for step in range(G + 2):
                        if step < G:
                            t = G * i + step
                            if cfg.kind == "rel":
                                o = job(i, ("rel", step))
                                nc.scalar.activation(rel[step % 2][:, :, :].rearrange("p h r -> p (h r)"),
                                                     o[:, 0:240], ACT.Identity).then_inc(s["job_used"].sem, 1)
                            if cfg.kind in ("softmax", "rel", "causal"):
                                act.wait_ge(s["z_full"].sem, b["z_full"] + t + 1)
                                act.wait_ge(s["px_full"].sem, b["px_full"] + t - 1)
                                nc.scalar.activation(p_t[step % 2][:, 0:H, 0:SLOT], z_t[step % 2][:, 0:H, :],
                                                     ACT.Exp, scale=cfg.scale).then_inc(s["p_full"].sem, 1)
                        if 1 <= step <= G:
                            t = G * i + step - 1
                            for v in range(halves):
                                act.wait_ge(s["av_full"].sem, b["av_full"] + halves * t + v + 1)
                                for im in range(4):
                                    ins = nc.scalar.activation(
                                        o_t[(step - 1) % 2][32 * im:32 * im + 32, v * WH:v * WH + WH],
                                        bank[im][32 * im:32 * im + 32, 0:WH], ACT.Identity)
                                ins.then_inc(s["av_used"].sem, 1)
                        if step >= 2:
                            g = step - 2
                            for v in range(halves):
                                o = job(i, ("t", (g, v)))
                                m = no // halves
                                src = o[:, 0:128 * m].rearrange("p (c b s) -> p c b s", c=m, b=4)[:, :, :, 0:SLOT]
                                dst = o_f[:, 0:no * n].rearrange("p (c g b s) -> p c g b s", c=no, g=G, b=4)[
                                    :, v * m:v * m + m, g, :, :]
                                nc.scalar.activation(dst, src, ACT.Identity).then_inc(s["job_used"].sem, 1)
                    for k in range(2):
                        o = job(i, ("out", k))[:, 0:n]
                        hold(act)
                        dst = feat[:, k, bass.ds(n * i, n)]
                        if cfg.ob:
                            col = DATA_COLS.lo(cfg.ob) + k
                            ins = nc.scalar.activation(dst, o, ACT.Identity, bias=dat[:, col:col + 1])
                        else:
                            ins = nc.scalar.activation(dst, o, ACT.Identity)
                        ins.then_inc(s["job_used"].sem, 1)

            def vector(dve):
                with dve.Fori(0, NI) as i:
                    k = [0]

                    def link(ins):
                        ins.then_inc(s["it_dve"].sem, 1)
                        k[0] += 1
                        dve.wait_ge(s["it_dve"].sem, b["it_dve"] + C * i + k[0])

                    def spread(c):
                        for h in range(HCH):
                            x = c * HCH + h
                            ins = nc.vector.tensor_scalar(k_x[0:R, x * n:(x + 1) * n], k_t[0:R, c % 4, 0:n],
                                                          heads[:, h:h + 1], None, ALU.mult)
                        return ins

                    if cfg.kind == "causal":
                        dve.wait_ge(s["job_used"].sem, b["job_used"] + J * i + JQ)
                        cos = shp[0:R, SHAPE_COLS["cos"]].unsqueeze(1).to_broadcast([R, 4 * G, SLOT])
                        sin = shp[0:R, SHAPE_COLS["sin"]].unsqueeze(1).to_broadcast([R, 4 * G, SLOT])
                        for c in range(NC):
                            for x, xr in ((q_t[0:R, qcols(c)], o_f[0:R, n * c:n * c + n]),
                                          (k_t[0:R, c, 0:n], k_t[0:R, 2 + c, 0:n])):
                                x3, xr3 = (v.rearrange("p (m s) -> p m s", s=SLOT) for v in (x, xr))
                                nc.vector.tensor_tensor(x3, x3, cos, ALU.mult)
                                link(nc.vector.tensor_tensor(xr3, xr3, sin, ALU.mult))
                                link(nc.vector.tensor_tensor(x, x, xr, ALU.add))
                    if cfg.kind == "rel":
                        for c in range(NC):
                            dve.wait_ge(s["job_used"].sem, b["job_used"] + J * i + NC + c + 1)
                            ins = spread(c)
                            if c < 4:
                                ins.then_inc(s["act_step"].sem, 1)
                        ins.then_inc(s["k_done"].sem, 1)
                    else:
                        dve.wait_ge(s["job_used"].sem, b["job_used"] + J * i + JQ)
                        for c in range(NC):
                            ins = spread(c)
                        ins.then_inc(s["k_done"].sem, 1)

                    n3 = [128, H, SLOT]

                    def shift(g):
                        t = G * i + g
                        j = g % 2
                        sc = bank[4 + j][:, 0:H * SLOT].rearrange("p (h s) -> p h s", s=SLOT)
                        z = z_t[j][:, 0:H, :]
                        mx = m12[:, j, 0:H]
                        dve.wait_ge(s["s_full"].sem, b["s_full"] + t + 1)
                        if cfg.kind == "performer":
                            dve.wait_ge(s["px_full"].sem, b["px_full"] + t - 1)
                            nc.vector.tensor_scalar(p_t[j][:, 0:H, 0:SLOT], sc, 1.0 / (2 * d), None, ALU.mult)\
                                .then_inc(s["s_used"].sem, 1)
                            return
                        if cfg.kind == "log2":
                            link(nc.vector.tensor_reduce(mx, sc, AX.X, ALU.max))
                            link(nc.vector.tensor_scalar(mx, mx, LOG2E, None, ALU.mult))
                            nc.vector.scalar_tensor_tensor(z, sc, LOG2E, bc(mx.unsqueeze(2), n3), ALU.mult,
                                                           ALU.subtract).then_inc(s["s_used"].sem, 1)
                            dve.wait_ge(s["s_used"].sem, b["s_used"] + t + 1)
                            zf, zi = (k_t[:, 2 + v, 0:H * SLOT].rearrange("p (h s) -> p h s", s=SLOT)
                                      for v in range(2))
                            link(nc.vector.tensor_scalar(z, z, -127.0, None, ALU.max))
                            magic = 1.5 * 2.0 ** 23
                            link(nc.vector.tensor_scalar(zf, z, magic, magic, ALU.add, ALU.subtract))
                            link(nc.vector.tensor_tensor(zi, zf, z, ALU.is_gt))
                            link(nc.vector.tensor_tensor(zi, zf, zi, ALU.subtract))
                            nc.vector.tensor_tensor(zf, z, zi, ALU.subtract)
                            bits = rel_p[:, :, :, :].rearrange("p h a c -> p (h a c)")[:, 0:H * SLOT]\
                                .rearrange("p (h s) -> p h s", s=SLOT)
                            link(nc.vector.tensor_scalar(bits.bitcast(I32), zi, 2.0 ** 23, 127.0 * 2 ** 23,
                                                         ALU.mult, ALU.add))
                            dve.wait_ge(s["px_full"].sem, b["px_full"] + t - 1)
                            nc.vector.scalar_tensor_tensor(p_t[j][:, 0:H, 0:SLOT], zf, 1.0, bits, ALU.add,
                                                           ALU.mult).then_inc(s["p_full"].sem, 1)
                            return
                        dve.wait_ge(s["p_full"].sem, b["p_full"] + t - 1)
                        src = sc
                        if cfg.kind == "causal":
                            mask = shp[:, SHAPE_COLS["causal"]].unsqueeze(1).to_broadcast(n3)
                            nc.vector.tensor_tensor(z, sc, mask, ALU.add).then_inc(s["s_used"].sem, 1)
                            dve.wait_ge(s["s_used"].sem, b["s_used"] + t + 1)
                            src = z
                        if cfg.kind == "rel":
                            dve.wait_ge(s["job_used"].sem, b["job_used"] + J * i + at_job[("rel", g)] + 1)
                            rl = rel[j]
                            for v, ind in enumerate(("relv", "relh")):
                                pr = rel_p[:, :, :, :]
                                tb = rl[:, :, 10 * v:10 * v + 10].unsqueeze(2).to_broadcast([128, 12, 5, 10])
                                im = shp[:, SHAPE_COLS[ind]].rearrange("p (a r) -> p a r", r=10).unsqueeze(1)\
                                    .to_broadcast([128, 12, 5, 10])
                                link(nc.vector.tensor_tensor(pr, tb, im, ALU.mult))
                                link(nc.vector.tensor_reduce(rel_u[:, v, :, :], pr, AX.X, ALU.add))
                            g4 = [128, 12, 5, 5]
                            z4 = z[:, :, 1:SLOT].rearrange("p h (a c) -> p h a c", c=5)
                            s4 = sc[:, :, 1:SLOT].rearrange("p h (a c) -> p h a c", c=5)
                            m0 = m12[:, 2, :].unsqueeze(2)
                            link(nc.vector.tensor_tensor(m0, rl[:, :, 0:1], rl[:, :, 10:11], ALU.add))
                            nc.vector.tensor_tensor(z[:, :, 0:1], sc[:, :, 0:1], m0, ALU.add)
                            nc.vector.tensor_tensor(z4, s4, rel_u[:, 0, :, :].unsqueeze(3).to_broadcast(g4),
                                                    ALU.add).then_inc(s["s_used"].sem, 1)
                            dve.wait_ge(s["s_used"].sem, b["s_used"] + t + 1)
                            link(nc.vector.tensor_tensor(z4, z4, rel_u[:, 1, :, :].unsqueeze(2).to_broadcast(g4),
                                                         ALU.add))
                            src = z
                        link(nc.vector.tensor_reduce(mx, src, AX.X, ALU.max))
                        nc.vector.tensor_tensor(z, src, bc(mx.unsqueeze(2), n3), ALU.subtract)\
                            .then_inc(s["z_full"].sem, 1)

                    def normalise(g):
                        t = G * i + g
                        j = g % 2
                        p = p_t[j][:, 0:H, 0:SLOT]
                        sm = m12[:, 2 + j, 0:H]
                        if cfg.kind == "performer":
                            dve.wait_ge(s["s_used"].sem, b["s_used"] + t + 1)
                        else:
                            dve.wait_ge(s["p_full"].sem, b["p_full"] + t + 1)
                        link(nc.vector.tensor_reduce(sm, p, AX.X, ALU.add))
                        if cfg.kind == "performer":
                            link(nc.vector.tensor_scalar(sm, sm, 1e-12, None, ALU.max))
                        link(nc.vector.reciprocal(sm, sm))
                        link(nc.vector.tensor_tensor(p, p, bc(sm.unsqueeze(2), n3), ALU.mult))
                        if cfg.kind == "rel":
                            pk = p[:, :, 1:SLOT].rearrange("p h (a c) -> p h a c", c=5)
                            nc.vector.tensor_reduce(rel_u[:, 0, :, :], pk, AX.X, ALU.add)
                            link(nc.vector.tensor_reduce(rel_u[:, 1, :, :], pk.rearrange("p h a c -> p h c a"),
                                                         AX.X, ALU.add))
                            for v, ind in enumerate(("relv", "relh")):
                                pr = rel_p[:, :, :, :].rearrange("p h a c -> p h (a c)")\
                                    .rearrange("p h (r k) -> p h r k", k=5)
                                pu = rel_u[:, v, :, :].unsqueeze(2).to_broadcast([128, 12, 10, 5])
                                im = shp[:, SHAPE_COLS[ind]].rearrange("p (a r) -> p r a", r=10).unsqueeze(1)\
                                    .to_broadcast([128, 12, 10, 5])
                                link(nc.vector.tensor_tensor(pr, pu, im, ALU.mult))
                                link(nc.vector.tensor_reduce(rel_a[:, :, 10 * v:10 * v + 10], pr, AX.X, ALU.add))
                            for v in range(2):
                                link(nc.vector.tensor_tensor(rel_a[:, :, 10 * v:10 * v + 1],
                                                             rel_a[:, :, 10 * v:10 * v + 1], p[:, :, 0:1], ALU.add))
                        dve.wait_ge(s["av_full"].sem, b["av_full"] + halves * (t - (0 if cfg.kind == "rel" else 1)))
                        if cfg.kind == "rel":
                            nc.vector.transpose(rel_x[:, :, :].rearrange("p h s -> p (h s)"),
                                                rel_a[:, :, :].rearrange("p h s -> p (h s)"))
                        nc.vector.transpose(p_x[j][:, 0:H, :].rearrange("p h s -> p (h s)"),
                                            p_t[j][:, 0:H, :].rearrange("p h s -> p (h s)"))\
                            .then_inc(s["px_full"].sem, 1)

                    for step in range(G + 1):
                        if step < G:
                            shift(step)
                        if step >= 1:
                            normalise(step - 1)
                    dve.wait_ge(s["job_used"].sem, b["job_used"] + J * i + JT)
                    if cfg.mix:
                        of3 = o_f[:, 0:2 * n].rearrange("p (c n) -> p c n", c=2)
                        link(nc.vector.tensor_tensor(of3, of3, mask_b[:, bass.ds(n * i, n)].unsqueeze(1)
                                                     .to_broadcast([128, 2, n]), ALU.mult))
                        hold(dve)
                        nc.vector.tensor_copy(xs[:, 0, 0:n], feat[:, 0, bass.ds(n * i, n)])
                        link(nc.vector.tensor_copy(xs[:, 2, 0:n], feat[:, 1, bass.ds(n * i, n)]))
                        nc.vector.tensor_tensor(xs[:, 1, 0:n], feat[:, 0, bass.ds(n * i, n)],
                                                xs[:, 0, 0:n].bitcast(F32), ALU.subtract)
                        nc.vector.tensor_tensor(xs[64:128, 2, 0:n], feat[64:128, 1, bass.ds(n * i, n)],
                                                xs[64:128, 2, 0:n].bitcast(F32), ALU.subtract)
                    link(nc.vector.tensor_copy(o_hi[:, 0:no * n], o_f[:, 0:no * n]))
                    if no == 2:
                        nc.vector.tensor_tensor(o_hi[64:128, n:2 * n], o_f[64:128, n:2 * n],
                                                o_hi[64:128, n:2 * n].bitcast(F32), ALU.subtract)
                    m = n if no == 2 else no * n
                    nc.vector.tensor_tensor(o_lo[:, 0:m], o_f[:, 0:m], o_hi[:, 0:m].bitcast(F32), ALU.subtract)\
                        .then_inc(s["o_split"].sem, 1)
                    assert k[0] == C, (cfg.dram, k[0])
            for name, uses in (("s_used", cfg.kind != "softmax"), ("z_full", cfg.kind in ("softmax", "rel", "causal")),
                               ("p_full", cfg.kind != "performer"),
                               ("qk_ready", cfg.kind == "performer"), ("act_step", cfg.kind == "rel")):
                if not uses:
                    signals[name].at = b[name]
            phases.append(dict(tensor=tensor, scalar=scalar, vector=vector, gpsimd=gpsimd))

        qk4 = [("q", 0), ("q", 1), ("k", 0), ("k", 1)]
        std = dict(H=12, d=16, G=4, qk=qk4, qcol=lambda x: 96 * x, vcol=2 * D, C=3 * D)
        l0 = Attention("L0_att", "causal", 6, 32, 4, [(k, c) for k in ("q", "qr", "k", "kr") for c in range(2)],
                    lambda x: 96 * x, 4 * D, 5 * D, 25, scale=32 ** -0.5, low_rank=True)
        l1 = Attention("L1_att", "rel", 12, 64, 2, [(k, c) for k in ("q", "k") for c in range(6)],
                    lambda x: 128 * x, 12 * 128, 18 * 128, 35, scale=0.125, ob="L1_ob", no=6, R=128, NC=6)
        l2a = Attention("L2_att", "performer", dve_steps=17, ob="L2a_ob", NC=4, **std)
        l2f = Attention("L2_fat", "softmax", dve_steps=17, scale=0.25, bias="L2f", vb="L2f_vb", ob="L2f_ob", **std)
        l3a = Attention("L3_att", "log2", dve_steps=41, bias="L3a", vb="L3a_vb", ob="L3a_ob", **std)

        l3f = Attention("L3_fat", "softmax", dve_steps=19, scale=0.25, bias="L3f", vb="L3f_vb", ob="L3f_ob", mix=True,
                     **std)

        def attention(cfg, res, after):
            attention_weights_phase(cfg, after)
            attention_phase(cfg)
            add_back_phase(res)

        conv_phase()
        norm_phase(h_tok, n_tok)
        features_phase(n_tok)
        attention(l0, h_tok, 1)
        norm_phase(h_tok, n_tok)
        features_phase(n_tok)
        gates_phase(32, "L0_g", "L0_gb", "softmax")
        experts_phase(32, a["L0_exp"], "L0_b1", "L0_b2", h_tok, ACT.Gelu)
        free = len(phases)
        norm_phase(h_tok, n_tok)
        features_phase(n_tok)
        attention(l1, h_tok, free)
        norm_phase(h_tok, n_tok)
        features_phase(n_tok)
        gates_phase(8, "L1_g", None, "top1")
        experts_phase(8, a["L1_exp"], "L1_b1", "L1_b2", h_tok, ACT.Silu)
        free = len(phases)
        norm_phase(h_tok, n_tok)
        features_phase(n_tok)
        attention(l2a, h_tok, free)
        free = len(phases)
        norm_phase(h_tok, y_tok)
        norm_phase(y_tok, n_tok)
        features_phase(n_tok, "ln_L2f1")
        attention(l2f, y_tok, free)
        features_phase(y_tok)
        experts_phase(1, a["L2_mlp"], "L2m_b1", "L2m_b2", y_tok, ACT.Gelu)
        norm_phase(y_tok, n_tok)
        features_phase(n_tok, "ln_L2f2")
        gates_phase(4, "L2_g", "L2_gb", "top2")
        experts_phase(4, a["L2_exp"], "L2e_b1", "L2e_b2", y_tok, ACT.Gelu)
        add_phase(h_tok, y_tok)
        free = len(phases)
        norm_phase(h_tok, n_tok)
        quantise_phase(n_tok)
        features_phase(n_tok)
        attention(l3a, h_tok, free)
        norm_phase(h_tok, y_tok)
        norm_phase(y_tok, n_tok)
        features_phase(n_tok, "ln_L3f1")
        ROUTE[0] = len(phases)
        route_phase()
        attention(l3f, y_tok, len(phases))
        norm_phase(y_tok, n_tok)
        features_phase(n_tok, "ln_L3f2")
        experts_phase(1, a["L3_mlp"], "L3_b1", "L3_b2", y_tok, ACT.Gelu)
        add_phase(h_tok, y_tok)

        block = ctx.enter_context(nc.Block())
        loads = [(shp[:, :], a["shape_pack"]), (dat[:, :], a["data_pack"]), (row[:, :], a["row_pack"]),
                 (pix[:, :, :], a["pixels"]), (conv_w[:, :, :], a["conv_w"]), (tok0[:, :, :], a["tok0"]),
                 (conv_row[:, :], a["conv_row"])]
        CONSTS = len(loads)
        started = [n for n in names if signals[n] and n not in
                   ("consts_in", "w_in0", "w_in1", "att_in", "out_done", "bridge", "phase_done", "holds")]

        def run(eng, kind):
            for n, ph in enumerate(phases):
                if kind in ph:
                    ph[kind](eng)
                eng.drain().then_inc(s["phase_done"].sem, 1)
                eng.wait_ge(s["phase_done"].sem, 4 * (n + 1))

        @block.sync
        def _(sp):
            for dst, src in loads:
                sp.dma_start(dst, src).then_inc(s["consts_in"].sem, 16)
            for ph in phases:
                if "sync" in ph:
                    ph["sync"](sp)
            sp.wait_ge(s["phase_done"].sem, 4 * len(phases))
            sp.dma_start(out, h_tok[:, :, :]).then_inc(s["out_done"].sem, 16)
            sp.wait_ge(s["out_done"].sem, 16)

        @block.gpsimd
        def _(pool):
            for n in started:
                pool.sem_inc(signals[n].sem, START)
            run(pool, "gpsimd")

        @block.scalar
        def _(act):
            run(act, "scalar")

        @block.vector
        def _(dve):
            run(dve, "vector")

        @block.tensor
        def _(pe):
            run(pe, "tensor")


def pad2(w):
    o = np.zeros((128, 2, w.shape[1]), w.dtype)
    o[:, 0] = w[:DA]
    o[:DB, 1] = w[DA:]
    o[DB:, 1] = w[DA:]
    return o


def shape_pack():
    o = np.zeros((128, SHAPE_COLS.n), np.float32)
    p = np.arange(128)
    o[p, SHAPE_COLS.lo("ident") + p] = 1
    for name, d, rows in (("head16", 16, 96), ("head32", 32, 96), ("head64", 64, 128)):
        r = np.arange(rows)
        o[r, SHAPE_COLS.lo(name) + r // d] = 1
    inv = 1.0 / 10000.0 ** (np.arange(0, 32, 2, dtype=np.float32) / 32)
    f = np.outer(np.arange(SLOT, dtype=np.float32), inv).astype(np.float32)
    emb = np.concatenate([f, f], 1)
    r = np.arange(96)
    o[:96, SHAPE_COLS["cos"]] = np.cos(emb).T[r % 32]
    o[:96, SHAPE_COLS["sin"]] = (np.sin(emb).T * np.where(np.arange(32) < 16, -1, 1)[:, None])[r % 32]
    q = p % 32
    o[:, SHAPE_COLS["causal"]] = np.where(np.arange(SLOT)[None] > q[:, None], -BIG, 0)
    hn = np.zeros((128, D), np.float32)
    for k in range(2):
        for c in range(96):
            hn[(3 * k + c // 32) * 16:(3 * k + c // 32) * 16 + 16, 96 * k + c] = -0.5
    o[:, SHAPE_COLS["halfnorm"]] = hn
    for name, div in (("relv", True), ("relh", False)):
        ind = np.zeros((128, SIDE, 10), np.float32)
        for i in range(128):
            m = i % 32 - 1
            for k in range(SIDE):
                if m < 0 or m >= SIDE * SIDE:
                    ind[i, k, 0] = 1
                else:
                    ind[i, k, k - (m // SIDE if div else m % SIDE) + 5] = 1
        o[:, SHAPE_COLS["" + name]] = ind.reshape(128, 50)
    o[:, SHAPE_COLS["order8"]] = np.arange(8, 0, -1)[None]
    return o


def expert_pack(w1, w2):
    E = w1.shape[0]
    o = np.zeros((E, 128, RAW), w1.dtype)
    v = o[:, :, :2 * HID].reshape(E, 128, 2, HID)
    v[:, :, 0] = w1[:, :DA]
    v[:, :DB, 1] = w1[:, DA:]
    v[:, DB:, 1] = w1[:, DA:]
    o[:, :, :2 * HID] = v.reshape(E, 128, 2 * HID)
    o[:, :, 2 * HID:] = w2.reshape(E, HC, 128, D).transpose(0, 2, 1, 3).reshape(E, 128, HC * D)
    return o


def chunked_bias(b):
    return b.reshape(-1, HC, 128).transpose(2, 0, 1).reshape(128, -1)


def layout(i):
    g = {k: np.asarray(v) for k, v in i.items()}
    f = np.float32
    dat = np.zeros((128, DATA_COLS.n), f)
    row = np.zeros((1, ROW_COLS.n), f)

    def col(name, v):
        dat[:v.shape[0], DATA_COLS[name]] = v
    col("L0_b1", chunked_bias(g["L0_ffn_b1"]))
    col("L1_b1", chunked_bias(g["L1_ffn_b1"]))
    col("L2m_b1", chunked_bias(g["L2_ffn_mlp_b1"]))
    col("L2e_b1", chunked_bias(g["L2_ffn_exp_b1"]))
    col("L3_b1", chunked_bias(g["L3_ffn_bf1"]))
    for name, v in (("L2f_qb", g["L2_ffn_in_b"][:D]), ("L2f_kb", g["L2_ffn_in_b"][D:2 * D]),
                    ("L3a_qb", g["L3_attn_bq"]), ("L3a_kb", g["L3_attn_bk"]),
                    ("L3f_qb", g["L3_ffn_bq"]), ("L3f_kb", g["L3_ffn_bk"])):
        col(name, v.reshape(2, 96).T)
    for name, v in (("L1_ob", g["L1_attn_proj_b"]), ("L2a_ob", g["L2_attn_proj_b"]), ("L2f_ob", g["L2_ffn_out_b"]),
                    ("L3a_ob", g["L3_attn_bo"]), ("L3f_ob", g["L3_ffn_bm"])):
        col(name, np.stack([v[:128], v[64:]], 1))
    for name, gg, bb in (("ln_L2f1", g["L2_ffn_ln1_g"], g["L2_ffn_ln1_b"]), ("ln_L2f2", g["L2_ffn_ln2_g"], g["L2_ffn_ln2_b"]),
                         ("ln_L3f1", g["L3_ffn_g1"], g["L3_ffn_b1"]), ("ln_L3f2", g["L3_ffn_g2"], g["L3_ffn_b2"])):
        col(name, np.concatenate([pad2(gg[:, None])[:, :, 0], pad2(bb[:, None])[:, :, 0]], 1))
    col("L0_g", pad2(g["L0_ffn_gate_w"]).reshape(128, -1))
    col("L1_g", pad2(g["L1_ffn_Wg"]).reshape(128, -1))
    col("L2_g", pad2(g["L2_ffn_gate_w"].T).reshape(128, -1))
    wr = np.zeros((D, 2), f)
    wr[:, 0] = g["L3_ffn_Wr"]
    col("L3_r", pad2(wr).reshape(128, -1))
    col("L0_b2", g["L0_ffn_b2"])
    col("L1_b2", g["L1_ffn_b2"])
    col("L2e_b2", g["L2_ffn_exp_b2"])
    rand = np.zeros((96, 2, D), f)
    for h in range(12):
        rand[16 * (h % 6):16 * (h % 6) + 16, h // 6, 32 * (h % 6):32 * (h % 6) + 32] = g["L2_attn_rand_matrix"][h]
    col("rand", rand.reshape(96, -1))
    rows = [0] + list(range(11, 20))
    tk = np.zeros((128, 2, 20), f)
    for h in range(2):
        tk[64 * h:64 * h + 64, h, :10] = g["L1_attn_tab_kv"][rows].T
        tk[64 * h:64 * h + 64, h, 10:] = g["L1_attn_tab_kh"][rows].T
    col("tabk", tk.reshape(128, 40))
    tv = np.zeros((4, 32, 64), f)
    tv[:, :10] = g["L1_attn_tab_vv"][rows][None]
    tv[:, 10:20] = g["L1_attn_tab_vh"][rows][None]
    col("tabv", tv.reshape(128, 64))

    def rowset(name, v):
        row[0, ROW_COLS[name]] = v
    row[0, ROW_COLS["ones"]] = 1
    for name, v in (("L0_gb", g["L0_ffn_gate_b"]), ("L2_gb", g["L2_ffn_gate_b"]),
                    ("L2f_vb", g["L2_ffn_in_b"][2 * D:]), ("L3a_vb", g["L3_attn_bv"]), ("L3f_vb", g["L3_ffn_bv"]),
                    ("L2m_b2", g["L2_ffn_mlp_b2"]), ("L3_b2", g["L3_ffn_bf2"]),
                    ("L3_bo", g["L3_ffn_bo"]), ("L3_bm", g["L3_ffn_bm"])):
        rowset(name, v)
    row[0, ROW_COLS.lo("L3_br")] = g["L3_ffn_br"]
    x = g["x"][:, :, :80, :80].reshape(IMG, 3, SIDE, 16, SIDE, 16).transpose(1, 3, 5, 0, 2, 4)
    px = np.zeros((PIX, IMG, SLOT), f)
    px[:, :, 1:] = x.reshape(PIX, IMG, SIDE * SIDE)
    bounds = np.arange(1.0 / 32, 1.0, 1.0 / 32, dtype=f)
    frac = np.arange(0.0, 1.0 - 1e-06, 1.0 / SIDE, dtype=f)
    bins = np.searchsorted(bounds, frac, side="right")
    pos = g["L0_tok_pos_table"][(bins[:, None] * 32 + bins).reshape(-1)]
    tok0 = np.zeros((IMG, SLOT, D), f)
    tok0[:, 0] = g["cls_tok"][0, 0]
    tok0[:, 1:] = pos
    arrays = {
        "conv_row": np.concatenate([(np.arange(TOK) % SLOT != 0).astype(f), g["L0_tok_conv_b"]])[None],
        "shape_pack": shape_pack(), "data_pack": dat, "row_pack": row,
        "pixels": px.reshape(PIX // 128, 128, TOK).transpose(1, 0, 2),
        "conv_w": g["L0_tok_conv_w"].reshape(D, PIX).T.reshape(PIX // 128, 128, D).transpose(1, 0, 2),
        "tok0": tok0.reshape(TILES, 128, D).transpose(1, 0, 2),
        "L0_exp": expert_pack(g["L0_ffn_w1"], g["L0_ffn_w2"]),
        "L1_exp": expert_pack(g["L1_ffn_W1"], g["L1_ffn_W2"]),
        "L2_mlp": expert_pack(g["L2_ffn_mlp_w1"][None], g["L2_ffn_mlp_w2"][None]),
        "L2_exp": expert_pack(g["L2_ffn_exp_w1"], g["L2_ffn_exp_w2"]),
        "L3_mlp": expert_pack(g["L3_ffn_W1"][None], g["L3_ffn_W2"][None]),
    }

    def att(name, qkv, o):
        o = pad2(o).reshape(128, -1) if o.shape[0] == D else \
            o.reshape(-1, 128, D).transpose(1, 0, 2).reshape(128, -1)
        arrays[name] = np.concatenate([pad2(qkv).reshape(128, -1), o], 1) if qkv is not None else o

    def twice(m):
        m = m.T
        return [m[:, :DA], m[:, DA:], m[:, DA:]]
    turned = (np.arange(D) // 32) * 32 + (np.arange(D) % 32 + 16) % 32
    att("L0_att", None, g["L0_attn_o_w"])
    arrays["L0_att_low"] = np.concatenate(
        twice(g["L0_attn_qA"]) + twice(g["L0_attn_kA"]) + twice(g["L0_attn_vA"])
        + [g["L0_attn_qB"], g["L0_attn_qB"][:, turned], g["L0_attn_kB"], g["L0_attn_kB"][:, turned],
           g["L0_attn_vB"]], 1)
    att("L1_att", g["L1_attn_qkv_w"].T, g["L1_attn_proj_w"].T)
    att("L2_att", g["L2_attn_qkv_w"].T, g["L2_attn_proj_w"].T)
    att("L2_fat", g["L2_ffn_in_w"].T, g["L2_ffn_out_w"].T)
    att("L3_att", np.concatenate([g["L3_attn_Wq"], g["L3_attn_Wk"], g["L3_attn_Wv"]], 1), g["L3_attn_Wo"])
    att("L3_fat", np.concatenate([g["L3_ffn_Wq"], g["L3_ffn_Wk"], g["L3_ffn_Wv"]], 1), g["L3_ffn_Wo"])
    arrays["L3_fat"] = np.concatenate([arrays["L3_fat"], pad2(g["L3_ffn_Wm"]).reshape(128, -1)], 1)
    t = np.arange(SLOT)
    arrays["earlier"] = np.tile((t[None, :] < t[:, None]).astype(f).reshape(1, -1), (IMG, 1))
    return {k: np.ascontiguousarray(v) for k, v in arrays.items()}


def kernel(**inputs):
    import numpy as _np
    import concourse.bacc as _bacc
    from concourse import mybir as _mybir
    from concourse.bass_utils import run_bass_kernel_spmd as _run

    nc = _bacc.Bacc("TRN2", target_bir_lowering=False, num_devices=1)
    arrays = layout(inputs)
    args = {k: nc.dram_tensor("in_" + k, v.shape, _mybir.dt.from_np(v.dtype), kind="ExternalInput").ap()
            for k, v in arrays.items()}
    o = nc.dram_tensor("out_0", (128, TILES, D), _mybir.dt.float32, kind="ExternalOutput").ap()
    vit_tower(nc, args, o)
    r = _run(nc, [{"in_" + k: v for k, v in arrays.items()}], core_ids=[0])
    return _np.ascontiguousarray(r.results[0]["out_0"].transpose(1, 0, 2).reshape(IMG, SLOT, D))
```

```python
import numpy as np
import concourse.bass as bass
from concourse import mybir
from contextlib import ExitStack

F32 = mybir.dt.float32
F32R = mybir.dt.float32r
I32 = mybir.dt.int32
ALU = mybir.AluOpType
ACT = mybir.ActivationFunctionType
AX = mybir.AxisListType

D = 192
DA = 128
DB = D - DA
IMG, SLOT = 64, 26
SIDE = 5
TOK = IMG * SLOT
TILES = TOK // 128
HID = 768
HC = HID // 128
PIX = 768
BLOCKS = [(0, 3), (3, 3), (6, 3), (9, 4)]
RAW = 2 * HID + HC * D
START = 64
LN_EPS = 1e-5
LOG2E = 1.4426950408889634
BIG = 1.0e30


class Signal:

    def __init__(self, sem, at):
        self.sem, self.at = sem, at


class Attention:

    def __init__(self, dram, kind, H, d, G, qk, qcol, vcol, C, dve_steps, scale=1.0, bias=None, vb=None, ob=None,
                 no=2, R=96, NC=2, low_rank=False, mix=False):
        self.dram, self.kind, self.H, self.d, self.G = dram, kind, H, d, G
        self.qk, self.qcol, self.vcol, self.C, self.dve_steps = qk, qcol, vcol, C, dve_steps
        self.scale, self.bias, self.vb, self.ob, self.no = scale, bias, vb, ob, no
        self.R, self.NC, self.HCH, self.low_rank, self.mix = R, NC, H // NC, low_rank, mix




class Columns:

    def __init__(self, spec):
        self.at, self.n = {}, 0
        for name, width in spec:
            self.at[name] = (self.n, width)
            self.n += width

    def __getitem__(self, name):
        a, w = self.at[name]
        return slice(a, a + w)

    def lo(self, name):
        return self.at[name][0]


SHAPE_COLS = Columns([("ident", 128), ("head16", 6), ("head32", 3), ("head64", 2), ("cos", SLOT), ("sin", SLOT),
                      ("causal", SLOT), ("halfnorm", D), ("relv", 50), ("relh", 50), ("order8", 8)])
DATA_COLS = Columns([("L0_b1", 32 * HC), ("L1_b1", 8 * HC), ("L2m_b1", HC), ("L2e_b1", 4 * HC), ("L3_b1", HC),
                     ("L2f_qb", 2), ("L2f_kb", 2), ("L3a_qb", 2), ("L3a_kb", 2), ("L3f_qb", 2), ("L3f_kb", 2),
                     ("L1_ob", 2), ("L2a_ob", 2), ("L2f_ob", 2), ("L3a_ob", 2), ("L3f_ob", 2),
                     ("ln_L2f1", 4), ("ln_L2f2", 4), ("ln_L3f1", 4), ("ln_L3f2", 4),
                     ("L0_g", 64), ("L1_g", 16), ("L2_g", 8), ("L3_r", 4),
                     ("L0_b2", D), ("L1_b2", D), ("L2e_b2", D),
                     ("rand", 2 * D), ("tabk", 40), ("tabv", 64)])
ROW_COLS = Columns([("ones", 128), ("L0_gb", 32), ("L1_gb", 8), ("L2_gb", 4),
                    ("L3_br", 2), ("L2f_vb", D), ("L3a_vb", D), ("L3f_vb", D), ("L2m_b2", D), ("L3_b2", D),
                    ("L3_bo", D), ("L3_bm", D)])


def vit_tower(nc, a, out, stop=99):
    ctx = ExitStack()

    def sb(name, shape, dt=F32, scope=None):
        return (scope or ctx).enter_context(nc.sbuf_tensor(name, shape, dt))

    def pb(name):
        return ctx.enter_context(nc.psum_tensor(name, [128, 512], F32))

    signals = {}

    def signal(name, start=START):
        signals[name] = Signal(ctx.enter_context(nc.semaphore(name)), start)
        return signals[name]

    with ctx:
        h_tok = sb("h_tok", [128, TILES, D])
        y_tok = sb("y_tok", [128, TILES, D])
        n_tok = sb("n_tok", [128, TILES, D])
        feat = sb("feat", [128, 2, TOK])
        XP = TOK + 8
        xa_hi = sb("xa_hi", [128, XP], F32R)
        xa_lo = sb("xa_lo", [128, XP], F32R)
        xb = sb("xb", [128, XP], F32R)
        shp = sb("shp", [128, SHAPE_COLS.n])
        dat = sb("dat", [128, DATA_COLS.n])
        row = sb("row", [1, ROW_COLS.n])
        gate = sb("gate", [128, TILES, 32])
        gate_t = feat[0:32, 1, :]
        gsc = feat[:, 0, :].rearrange("p (k n) -> p k n", k=4)
        stats = sb("stats", [128, TILES, 6])
        mv = sb("mv", [128, TILES, 2])
        rstd = sb("rstd", [128, 4, TILES])
        sml = sb("sml", [128, 160])
        gw_hi = sb("gw_hi", [128, 2, 32], F32R)
        gw_lo = sb("gw_lo", [128, 2, 32], F32R)

        ex = ExitStack()
        raw = [sb(f"raw{j}", [128, RAW], scope=ex) for j in range(2)]
        w1_hi = [sb(f"w1_hi{j}", [128, 2, HID], F32R, ex) for j in range(2)]
        w1_lo = [sb(f"w1_lo{j}", [128, 2, HID], F32R, ex) for j in range(2)]
        w2 = [sb(f"w2_{j}", [128, HC, 2 * D], F32R, ex) for j in range(2)]
        hid = [sb(f"hid{j}", [128, 512], scope=ex) for j in range(3)]
        hid_hi = [sb(f"hid_hi{j}", [128, HC, 512], F32R, ex) for j in range(2)]
        hid_lo = [sb(f"hid_lo{j}", [128, HC, 512], F32R, ex) for j in range(2)]
        ex.close()

        cv = ExitStack()
        pix = sb("pix", [128, PIX // 128, TOK], scope=cv)
        conv_w = sb("conv_w", [128, PIX // 128, D], scope=cv)
        tok0 = sb("tok0", [128, TILES, D], scope=cv)
        conv_row = sb("conv_row", [1, TOK + D], scope=cv)
        cv.close()

        AW, NARROW = 5760, 2304
        nr = ExitStack()
        sb("wp_narrow", [128, NARROW], F32R, nr)
        spare = sb("spare", [128, AW - NARROW], scope=nr)
        nr.close()
        at = ExitStack()
        wp_hi = sb("wp_hi", [128, AW], F32R, at)
        wp_lo = sb("wp_lo", [128, AW], F32R, at)
        xs = sb("xs", [128, 3, 512], F32R, at)
        o_hi = sb("o_hi", [128, 6 * 208], F32R, at)
        o_lo = sb("o_lo", [128, 6 * 208], F32R, at)
        rw = ExitStack()
        wp_raw = sb("wp_raw", [128, AW], scope=rw)
        low = sb("low", [48, 3 * 256 + 5 * D], scope=rw)
        rw.close()
        q_t = sb("q_t", [128, 4 * 424], scope=at)
        k_t = sb("k_t", [128, 4, 416], scope=at)
        k_x = sb("k_x", [128, 12 * 416], scope=at)
        v_t = sb("v_t", [128, 4 * 384], scope=at)
        z_t = [sb(f"z_t{j}", [128, 12, SLOT], scope=at) for j in range(2)]
        p_t = [sb(f"p_t{j}", [128, 12, 32], scope=at) for j in range(2)]
        p_x = [sb(f"p_x{j}", [128, 12, 32], scope=at) for j in range(2)]
        o_t = [sb(f"o_t{j}", [128, HID], scope=at) for j in range(2)]
        o_f = sb("o_f", [128, 6 * 208], scope=at)
        m12 = sb("m12", [128, 4, 12], scope=at)
        rel = [sb(f"rel{j}", [128, 12, 20], scope=at) for j in range(2)]
        rel_p = sb("rel_p", [128, 12, 5, 10], scope=at)
        rel_u = sb("rel_u", [128, 2, 12, 5], scope=at)
        rel_a = sb("rel_a", [128, 12, 32], scope=at)
        rel_x = sb("rel_x", [128, 12, 32], scope=at)
        at.close()

        bank = [pb(f"bank{j}") for j in range(8)]

        names = ["consts_in", "phase_done", "dve_step", "act_step", "pool_step",
                 "w_in0", "w_in1", "w_split", "h_full", "h_act", "h_split", "y_full", "y_used", "att_in",
                 "job_full", "job_used", "staged", "qk_ready", "s_full", "s_used", "z_full", "p_full",
                 "px_full", "av_full", "av_used", "t_full", "t_used", "out_done", "bridge", "k_done",
                 "o_split", "it_dve", "holds"]
        s = {n: signal(n) for n in names}
        s["consts_in"].at = s["w_in0"].at = s["w_in1"].at = s["att_in"].at = s["out_done"].at = s["bridge"].at = 0
        s["phase_done"].at = 0

        phases = []

        def base(**adds):
            b = {k: signals[k].at for k in adds}
            for k, v in adds.items():
                signals[k].at += v
            return b

        def hold(eng):
            eng.sem_inc(s["holds"].sem, 1)

        def chain(eng, sig, n):
            def link(ins):
                ins.then_inc(sig.sem, 1)
                n[0] += 1
                eng.wait_ge(sig.sem, n[0])
            return link

        def bc(ap, shape):
            return ap.to_broadcast(shape)

        def conv_phase():
            b = base(job_full=TILES, job_used=TILES)

            def tensor(pe):
                pe.wait_ge(s["consts_in"].sem, 16 * CONSTS)
                for t in range(TILES):
                    o = bank[t % 8][:, 0:D]
                    if t >= 8:
                        pe.wait_ge(s["job_used"].sem, b["job_used"] + t - 7)
                    for c in range(PIX // 128):
                        nc.tensor.matmul(o, pix[:, c, 128 * t:128 * t + 128], conv_w[:, c, :],
                                         start=c == 0, stop=False)
                    nc.tensor.matmul(o, conv_row[0:1, 128 * t:128 * t + 128], conv_row[0:1, TOK:TOK + D],
                                     start=False, stop=True).then_inc(s["job_full"].sem, 1)

            def vector(dve):
                dve.wait_ge(s["consts_in"].sem, 16 * CONSTS)
                for t in range(TILES):
                    dve.wait_ge(s["job_full"].sem, b["job_full"] + t + 1)
                    nc.vector.tensor_tensor(h_tok[:, t, :], bank[t % 8][:, 0:D], tok0[:, t, :],
                                            ALU.add).then_inc(s["job_used"].sem, 1)
            phases.append(dict(tensor=tensor, vector=vector))

        def norm_phase(src, dst):
            b = base(dve_step=2 * TILES + 2, act_step=1)

            def vector(dve):
                for t in range(TILES):
                    nc.vector.bn_stats(stats[:, t, :], src[:, t, :]).then_inc(s["dve_step"].sem, 1)
                for t in range(TILES):
                    dve.wait_ge(s["dve_step"].sem, b["dve_step"] + t + 1)
                    nc.vector.bn_aggr(mv[:, t, :], stats[:, t, :]).then_inc(s["dve_step"].sem, 1)
                dve.wait_ge(s["dve_step"].sem, b["dve_step"] + 2 * TILES)
                nc.vector.tensor_scalar(rstd[:, 0, :], mv[:, :, 1], LN_EPS, None,
                                        ALU.add).then_inc(s["dve_step"].sem, 1)
                dve.wait_ge(s["act_step"].sem, b["act_step"] + 1)
                nc.vector.reciprocal(rstd[:, 2, :], rstd[:, 1, :]).then_inc(s["dve_step"].sem, 1)
                dve.wait_ge(s["dve_step"].sem, b["dve_step"] + 2 * TILES + 2)
                for t in range(TILES):
                    nc.vector.tensor_scalar(dst[:, t, :], src[:, t, :], mv[:, t, 0:1], rstd[:, 2, t:t + 1],
                                            ALU.subtract, ALU.mult)

            def scalar(act):
                act.wait_ge(s["dve_step"].sem, b["dve_step"] + 2 * TILES + 1)
                nc.scalar.activation(rstd[:, 1, :], rstd[:, 0, :], ACT.Sqrt).then_inc(s["act_step"].sem, 1)
            phases.append(dict(vector=vector, scalar=scalar))

        def transpose_b(o, x):
            ident = shp[:, SHAPE_COLS["ident"]]
            nc.tensor.transpose(o, x[:, DB:D], ident)
            return nc.tensor.transpose(o[0:DB, :], x[:, DA:D], ident)

        TBLK = [(0, 4), (4, 4), (8, 4), (12, 1)]

        def features_phase(src, ln=None):
            b = base(t_full=4, t_used=4, dve_step=8)
            ident = shp[:, SHAPE_COLS["ident"]]

            def tensor(pe):
                for i, (t0, n) in enumerate(TBLK):
                    pa, pbk = bank[2 * (i % 2)], bank[2 * (i % 2) + 1]
                    if i >= 2:
                        pe.wait_ge(s["t_used"].sem, b["t_used"] + i - 1)
                    for j in range(n):
                        x = src[:, t0 + j, :]
                        nc.tensor.transpose(pa[:, 128 * j:128 * j + 128], x[:, 0:DA], ident)
                        ins = transpose_b(pbk[:, 128 * j:128 * j + 128], x)
                    ins.then_inc(s["t_full"].sem, 1)

            def scalar(act):
                for i, (t0, n) in enumerate(TBLK):
                    act.wait_ge(s["t_full"].sem, b["t_full"] + i + 1)
                    for part in range(2):
                        p = bank[2 * (i % 2) + part][:, 0:128 * n]
                        o = feat[:, part, 128 * t0:128 * (t0 + n)]
                        if ln is None:
                            ins = nc.scalar.activation(o, p, ACT.Identity)
                        else:
                            g = DATA_COLS.lo(ln) + part
                            ins = nc.scalar.activation(o, p, ACT.Identity, bias=dat[:, g + 2:g + 3],
                                                       scale=dat[:, g:g + 1])
                    ins.then_inc(s["t_used"].sem, 1)

            def vector(dve):
                n_step = b["dve_step"]
                for i, (t0, n) in enumerate(TBLK):
                    dve.wait_ge(s["t_used"].sem, b["t_used"] + i + 1)
                    c = slice(128 * t0, 128 * (t0 + n))
                    nc.vector.tensor_copy(xa_hi[:, c], feat[:, 0, c])
                    nc.vector.tensor_copy(xb[:, c], feat[:, 1, c]).then_inc(s["dve_step"].sem, 1)
                    n_step += 1
                    dve.wait_ge(s["dve_step"].sem, n_step)
                    nc.vector.tensor_tensor(xa_lo[:, c], feat[:, 0, c], xa_hi[:, c].bitcast(F32), ALU.subtract)
                    nc.vector.tensor_tensor(xb[64:128, c], feat[64:128, 1, c], xb[64:128, c].bitcast(F32),
                                            ALU.subtract).then_inc(s["dve_step"].sem, 1)
                    n_step += 1
            phases.append(dict(tensor=tensor, scalar=scalar, vector=vector))

        def five(o, wh, wl, xh, xl, xbt, w_first, start=True, stop=True):
            parts = [(wh[0], xh), (wh[0], xl), (wl[0], xh), (wh[1], xbt), (wl[1], xbt)]
            for n, (w, x) in enumerate(parts):
                l, r = (w, x) if w_first else (x, w)
                ins = nc.tensor.matmul(o, l, r, start=start and n == 0, stop=stop and n == 4)
            return ins

        def gates_phase(E, g_col, gb_col, kind):
            steps = {"softmax": 8, "top1": 12, "top2": 24}[kind]
            b = base(dve_step=steps, job_full=2, t_full=TILES, t_used=TILES, act_step=1)
            n3 = [128, TILES, E]

            def v3(k):
                return gsc[:, k, 0:TILES * E].rearrange("p (t e) -> p t e", e=E)
            G = gate[:, :, 0:E]

            def tensor(pe):
                pe.wait_ge(s["dve_step"].sem, b["dve_step"] + 2)
                for t in range(TILES):
                    c = slice(128 * t, 128 * t + 128)
                    o = bank[0][:, E * t:E * t + E]
                    ins = five(o, [gw_hi[:, 0, 0:E], gw_hi[:, 1, 0:E]], [gw_lo[:, 0, 0:E], gw_lo[:, 1, 0:E]],
                               xa_hi[:, c], xa_lo[:, c], xb[:, c], False, stop=not gb_col)
                    if gb_col:
                        ins = nc.tensor.matmul(o, row[0:1, ROW_COLS["ones"]], row[0:1, ROW_COLS[gb_col]],
                                               start=False, stop=True)
                ins.then_inc(s["job_full"].sem, 1)
                pe.wait_ge(s["job_full"].sem, b["job_full"] + 2)
                for t in range(TILES):
                    if t >= 4:
                        pe.wait_ge(s["t_used"].sem, b["t_used"] + t - 3)
                    nc.tensor.transpose(bank[1 + t % 4][0:E, 0:128], gate[:, t, 0:E],
                                        shp[:, SHAPE_COLS["ident"]]).then_inc(s["t_full"].sem, 1)

            def scalar(act):
                act.wait_ge(s["dve_step"].sem, b["dve_step"] + (5 if kind != "top2" else 14))
                nc.scalar.activation(v3(1) if kind != "top2" else gsc[:, 1, 0:TILES],
                                     v3(0) if kind != "top2" else gsc[:, 0, 0:TILES], ACT.Exp)\
                    .then_inc(s["act_step"].sem, 1)
                for t in range(TILES):
                    act.wait_ge(s["t_full"].sem, b["t_full"] + t + 1)
                    nc.scalar.activation(gate_t[0:E, 128 * t:128 * t + 128], bank[1 + t % 4][0:E, 0:128],
                                         ACT.Identity).then_inc(s["t_used"].sem, 1)

            def vector(dve):
                n = [b["dve_step"]]
                link = chain(dve, s["dve_step"], n)
                w = dat[:, DATA_COLS[g_col]].rearrange("p (k e) -> p k e", k=2)
                link(nc.vector.tensor_copy(gw_hi[:, :, 0:E], w))
                link(nc.vector.tensor_tensor(gw_lo[:, :, 0:E], w, gw_hi[:, :, 0:E].bitcast(F32), ALU.subtract))
                dve.wait_ge(s["job_full"].sem, b["job_full"] + 1)
                lg = bank[0][:, 0:TILES * E].rearrange("p (t e) -> p t e", e=E)
                link(nc.vector.tensor_copy(v3(3), lg))
                mx = sml[:, 0:TILES]

                def first_of(eq_src, target, dst):
                    order = shp[:, SHAPE_COLS["order8"]][:, 0:E].unsqueeze(1).to_broadcast(n3)
                    link(nc.vector.tensor_tensor(dst, eq_src, bc(target.unsqueeze(2), n3), ALU.is_equal))
                    link(nc.vector.tensor_tensor(dst, dst, order, ALU.mult))
                    link(nc.vector.tensor_reduce(sml[:, 48:48 + TILES], dst, AX.X, ALU.max))
                    link(nc.vector.tensor_tensor(dst, dst, bc(sml[:, 48:48 + TILES].unsqueeze(2), n3),
                                                 ALU.is_equal))
                link(nc.vector.tensor_reduce(mx, v3(3), AX.X, ALU.max))
                if kind != "top2":
                    link(nc.vector.tensor_tensor(v3(0), v3(3), bc(mx.unsqueeze(2), n3), ALU.subtract))
                    dve.wait_ge(s["act_step"].sem, b["act_step"] + 1)
                    link(nc.vector.tensor_reduce(sml[:, 16:16 + TILES], v3(1), AX.X, ALU.add))
                    link(nc.vector.reciprocal(sml[:, 32:32 + TILES], sml[:, 16:16 + TILES]))
                    inv = bc(sml[:, 32:32 + TILES].unsqueeze(2), n3)
                    if kind == "softmax":
                        link(nc.vector.tensor_tensor(G, v3(1), inv, ALU.mult))
                    else:
                        first_of(v3(3), mx, v3(2))
                        link(nc.vector.tensor_tensor(G, v3(2), inv, ALU.mult))
                else:
                    m2 = sml[:, 64:64 + TILES]
                    first_of(v3(3), mx, v3(2))
                    link(nc.vector.tensor_scalar(v3(1), v3(2), -BIG, None, ALU.mult))
                    link(nc.vector.tensor_tensor(v3(1), v3(1), v3(3), ALU.add))
                    link(nc.vector.tensor_reduce(m2, v3(1), AX.X, ALU.max))
                    link(nc.vector.tensor_copy(v3(3), v3(1)))
                    first = gsc[:, 0, 256:256 + TILES * E].rearrange("p (t e) -> p t e", e=E)
                    link(nc.vector.tensor_copy(first, v3(2)))
                    link(nc.vector.tensor_tensor(gsc[:, 0, 0:TILES], m2, mx, ALU.subtract))
                    dve.wait_ge(s["act_step"].sem, b["act_step"] + 1)
                    e2 = gsc[:, 1, 0:TILES]
                    link(nc.vector.tensor_scalar(sml[:, 16:16 + TILES], e2, 1.0, None, ALU.add))
                    link(nc.vector.reciprocal(sml[:, 32:32 + TILES], sml[:, 16:16 + TILES]))
                    link(nc.vector.tensor_tensor(sml[:, 80:80 + TILES], e2, sml[:, 32:32 + TILES], ALU.mult))
                    first_of(v3(3), m2, v3(2))
                    link(nc.vector.tensor_tensor(v3(2), v3(2), bc(sml[:, 80:80 + TILES].unsqueeze(2), n3),
                                                 ALU.mult))
                    link(nc.vector.tensor_tensor(first, first, bc(sml[:, 32:32 + TILES].unsqueeze(2), n3),
                                                 ALU.mult))
                    link(nc.vector.tensor_tensor(G, first, v3(2), ALU.add))
                assert n[0] == b["dve_step"] + steps
                dve.sem_inc(s["job_full"].sem, 1)
            phases.append(dict(tensor=tensor, scalar=scalar, vector=vector))

        def experts_phase(E, dram, b1_col, b2_col, res, func):
            b = base(w_split=4 * E, h_full=24 * E, h_act=24 * E, h_split=24 * E, y_full=TILES * (E + 1),
                     y_used=TILES * (E + 1), dve_step=(24 + TILES) * E,
                     w_in0=16 * ((E + 1) // 2), w_in1=16 * (E // 2))
            w_in = [s["w_in0"], s["w_in1"]]
            w_in_at = [b["w_in0"], b["w_in1"]]
            STEPS = 24 + TILES
            barrier = len(phases)

            def over_experts(eng, body, first=0):
                if E == 1:
                    body(0, 0, 0)
                else:
                    with eng.Fori(0, E // 2) as i:
                        body(2 * i, 0, i)
                        body(2 * i + 1, 1, i)

            def sync(sp):
                sp.wait_ge(s["phase_done"].sem, 4 * barrier)
                for e in range(min(E, 2)):
                    sp.dma_start(raw[e][:, :], dram[e]).then_inc(w_in[e].sem, 16)
                if E > 2:
                    with sp.Fori(0, E // 2 - 1) as i:
                        for j in range(2):
                            sp.wait_ge(s["w_split"].sem, b["w_split"] + 4 * (2 * i + j + 1))
                            sp.dma_start(raw[j][:, :], dram[bass.ds(2 * i + j + 2, 1)]
                                         .rearrange("o p n -> p (o n)")).then_inc(w_in[j].sem, 16)

            def gpsimd(pool):
                def body(e, j, i):
                    pool.wait_ge(w_in[j].sem, w_in_at[j] + 16 * (i + 1))
                    pool.wait_ge(s["y_full"].sem, b["y_full"] + TILES + TILES * (e - 1))
                    hold(pool)
                    r1 = raw[j][:, 0:2 * HID].rearrange("p (k n) -> p k n", k=2)
                    r2 = raw[j][:, 2 * HID:RAW].rearrange("p (c n) -> p c n", c=HC)
                    nc.gpsimd.tensor_copy(w1_hi[j][:, :, :], r1).then_inc(s["w_split"].sem, 1)
                    nc.gpsimd.tensor_copy(w2[j][:, :, 0:D], r2).then_inc(s["w_split"].sem, 1)
                    pool.wait_ge(s["w_split"].sem, b["w_split"] + 4 * e + 1)
                    nc.gpsimd.tensor_tensor(w1_lo[j][:, :, :], r1, w1_hi[j][:, :, :].bitcast(F32),
                                            ALU.subtract).then_inc(s["w_split"].sem, 1)
                    pool.wait_ge(s["w_split"].sem, b["w_split"] + 4 * e + 2)
                    nc.gpsimd.tensor_tensor(w2[j][:, :, D:2 * D], r2, w2[j][:, :, 0:D].bitcast(F32),
                                            ALU.subtract).then_inc(s["w_split"].sem, 1)
                over_experts(pool, body)

            def tensor(pe):
                for t in range(TILES):
                    if t >= 4:
                        pe.wait_ge(s["y_used"].sem, b["y_used"] + t - 3)
                    if E == 1:
                        l, r = row[0:1, ROW_COLS["ones"]], row[0:1, ROW_COLS[b2_col]]
                    else:
                        l, r = gate_t[0:E, 128 * t:128 * t + 128], dat[0:E, DATA_COLS[b2_col]]
                    nc.tensor.matmul(bank[t % 4][:, 0:D], l, r, start=True, stop=True)\
                        .then_inc(s["y_full"].sem, 1)

                def up(e, j, k):
                    t0, nt = BLOCKS[k]
                    c = slice(128 * t0, 128 * (t0 + nt))
                    for m in range(HC):
                        n = 24 * e + 6 * k + m
                        pe.wait_ge(s["h_act"].sem, b["h_act"] + n - 3)
                        o = bank[4 + (6 * k + m) % 4][:, 0:128 * nt]
                        mc = slice(128 * m, 128 * m + 128)
                        five(o, [w1_hi[j][:, 0, mc], w1_hi[j][:, 1, mc]],
                             [w1_lo[j][:, 0, mc], w1_lo[j][:, 1, mc]],
                             xa_hi[:, c], xa_lo[:, c], xb[:, c], True).then_inc(s["h_full"].sem, 1)

                def down(e, j, k):
                    t0, nt = BLOCKS[k]
                    for t in range(nt):
                        n = TILES * (e + 1) + t0 + t
                        if t == 0:
                            pe.wait_ge(s["h_split"].sem, b["h_split"] + 24 * e + 6 * k + 6)
                        pe.wait_ge(s["y_used"].sem, b["y_used"] + n - (3 if t0 + t else 0))
                        o = bank[(t0 + t) % 4]
                        c = slice(128 * t, 128 * t + 128)
                        for m in range(HC):
                            nc.tensor.matmul(o[:, 0:2 * D], hid_hi[k % 2][:, m, c], w2[j][:, m, :],
                                             start=m == 0, stop=False)
                            ins = nc.tensor.matmul(o[:, 0:D], hid_lo[k % 2][:, m, c], w2[j][:, m, 0:D],
                                                   start=False, stop=m == HC - 1)
                        ins.then_inc(s["y_full"].sem, 1)

                def body(e, j, i):
                    pe.wait_ge(s["w_split"].sem, b["w_split"] + 4 * (e + 1))
                    up(e, j, 0)
                    for k in range(1, 4):
                        up(e, j, k)
                        down(e, j, k - 1)
                    down(e, j, 3)
                over_experts(pe, body)

            def scalar(act):
                def body(e, j, i):
                    for k, (t0, nt) in enumerate(BLOCKS):
                        for m in range(HC):
                            n = 24 * e + 6 * k + m
                            act.wait_ge(s["h_full"].sem, b["h_full"] + n + 1)
                            act.wait_ge(s["h_split"].sem, b["h_split"] + n - 2)
                            col = DATA_COLS.lo(b1_col) + m
                            hold(act)
                            bias = dat[:, col:col + 1] if E == 1 else dat[:, bass.ds(HC * e + col, 1)]
                            nc.scalar.activation(hid[(6 * k + m) % 3][:, 0:128 * nt],
                                                 bank[4 + (6 * k + m) % 4][:, 0:128 * nt], func,
                                                 bias=bias).then_inc(s["h_act"].sem, 1)
                over_experts(act, body)

            def vector(dve):
                for t in range(TILES):
                    dve.wait_ge(s["y_full"].sem, b["y_full"] + t + 1)
                    nc.vector.tensor_tensor(res[:, t, :], bank[t % 4][:, 0:D], res[:, t, :],
                                            ALU.add).then_inc(s["y_used"].sem, 1)

                def split(e, j, k):
                    t0, nt = BLOCKS[k]
                    w = 128 * nt
                    prev = [TILES * e + BLOCKS[3][0], TILES * (e + 1), TILES * (e + 1) + BLOCKS[1][0],
                            TILES * (e + 1) + BLOCKS[2][0]][k]
                    dve.wait_ge(s["y_full"].sem, b["y_full"] + prev)
                    for m in range(HC):
                        n = 24 * e + 6 * k + m
                        dve.wait_ge(s["h_act"].sem, b["h_act"] + n + 1)
                        h = hid[(6 * k + m) % 3][:, 0:w]
                        nc.vector.tensor_copy(hid_hi[k % 2][:, m, 0:w], h).then_inc(s["dve_step"].sem, 1)
                        dve.wait_ge(s["dve_step"].sem, b["dve_step"] + STEPS * e + 6 * k + m + 1
                                    + (BLOCKS[k - 1][0] if k > 1 else 0))
                        nc.vector.tensor_tensor(hid_lo[k % 2][:, m, 0:w], h,
                                                hid_hi[k % 2][:, m, 0:w].bitcast(F32),
                                                ALU.subtract).then_inc(s["h_split"].sem, 1)

                def gather(e, j, k):
                    t0, nt = BLOCKS[k]
                    for t in range(t0, t0 + nt):
                        n = TILES * (e + 1) + t
                        dve.wait_ge(s["y_full"].sem, b["y_full"] + n + 1)
                        o = bank[t % 4]
                        g = 1.0 if E == 1 else gate[:, t, bass.ds(e, 1)]
                        nc.vector.scalar_tensor_tensor(res[:, t, :], o[:, 0:D], g, res[:, t, :], ALU.mult,
                                                       ALU.add).then_inc(s["dve_step"].sem, 1)
                        done_splits = 6 * min(k + 2, 4)
                        dve.wait_ge(s["dve_step"].sem, b["dve_step"] + STEPS * e + done_splits + t + 1)
                        nc.vector.scalar_tensor_tensor(res[:, t, :], o[:, D:2 * D], g, res[:, t, :], ALU.mult,
                                                       ALU.add).then_inc(s["y_used"].sem, 1)

                def body(e, j, i):
                    split(e, j, 0)
                    for k in range(1, 4):
                        split(e, j, k)
                        gather(e, j, k - 1)
                    gather(e, j, 3)
                over_experts(dve, body)
            phases.append(dict(tensor=tensor, scalar=scalar, vector=vector, gpsimd=gpsimd, sync=sync))

        def add_back_phase(res):
            b = base(t_full=TILES, t_used=TILES)
            ident = shp[:, SHAPE_COLS["ident"]]

            def tensor(pe):
                for t in range(TILES):
                    if t >= 8:
                        pe.wait_ge(s["t_used"].sem, b["t_used"] + t - 7)
                    c = slice(128 * t, 128 * t + 128)
                    nc.tensor.transpose(bank[t % 8][:, 0:128], feat[:, 0, c], ident)
                    nc.tensor.transpose(bank[t % 8][:, 64:192], feat[:, 1, c], ident)\
                        .then_inc(s["t_full"].sem, 1)

            def vector(dve):
                for t in range(TILES):
                    dve.wait_ge(s["t_full"].sem, b["t_full"] + t + 1)
                    nc.vector.tensor_tensor(res[:, t, :], bank[t % 8][:, 0:D], res[:, t, :],
                                            ALU.add).then_inc(s["t_used"].sem, 1)
            phases.append(dict(tensor=tensor, vector=vector))

        def quantise_phase(x):
            b = base(dve_step=10, t_full=1, job_full=1)
            v = x[:, :, :].rearrange("p t d -> p (t d)")
            q = y_tok[:, :, :].rearrange("p t d -> p (t d)")
            top, one, sc, inv = (sml[:, 150 + j:151 + j] for j in range(4))

            def tensor(pe):
                pe.wait_ge(s["dve_step"].sem, b["dve_step"] + 1)
                nc.tensor.transpose(bank[0][0:1, 0:128], top, shp[:, SHAPE_COLS["ident"]])\
                    .then_inc(s["t_full"].sem, 1)
                pe.wait_ge(s["dve_step"].sem, b["dve_step"] + 4)
                nc.tensor.matmul(bank[1][:, 0:1], row[0:1, ROW_COLS["ones"]], one[0:1, :], start=True, stop=True)\
                    .then_inc(s["job_full"].sem, 1)

            def vector(dve):
                link = chain(dve, s["dve_step"], [b["dve_step"]])
                link(nc.vector.tensor_reduce(top, v, AX.X, ALU.max, apply_absolute_value=True))
                dve.wait_ge(s["t_full"].sem, b["t_full"] + 1)
                link(nc.vector.tensor_reduce(one[0:1, :], bank[0][0:1, 0:128], AX.X, ALU.max))
                link(nc.vector.tensor_scalar(one[0:1, :], one[0:1, :], 1.0 / 127.0, None, ALU.mult))
                link(nc.vector.tensor_scalar(one[0:1, :], one[0:1, :], 1e-8, None, ALU.max))
                dve.wait_ge(s["job_full"].sem, b["job_full"] + 1)
                link(nc.vector.tensor_copy(sc, bank[1][:, 0:1]))
                link(nc.vector.reciprocal(inv, sc))
                magic = 1.5 * 2.0 ** 23
                link(nc.vector.tensor_scalar(q, v, inv, magic, ALU.mult, ALU.add))
                link(nc.vector.tensor_scalar(q, q, magic, 127.0, ALU.subtract, ALU.min))
                link(nc.vector.tensor_scalar(q, q, -128.0, sc, ALU.max, ALU.mult))
                link(nc.vector.tensor_tensor(q, q, v, ALU.subtract))
                nc.vector.tensor_tensor(v, v, q, ALU.add)
            phases.append(dict(tensor=tensor, vector=vector))

        def route_phase():
            KEEP = max(1, int(round(0.15 * SLOT)))
            b = base(dve_step=9 + 4 * 2 + 4 * 4, job_full=4 + 12, job_used=4 + 12, bridge=112)
            turn_d = nc.dram_tensor("turn", (3, TOK), F32).ap()

            def by_image(k):
                return turn_d[k, :].rearrange("(m t) -> m t", t=SLOT)
            NJ = TOK // 4
            s_row, w_row, m_row = k_x[0:1, 0:TOK], k_t[0:1, :, :].rearrange("p c n -> p (c n)"), q_t[0:1, 0:TOK]
            s26, w26, m26 = (k_x[0:IMG, c:c + SLOT] for c in (1664, 1704, 1744))
            early, less, same = (k_x[0:IMG, c:c + SLOT * SLOT].rearrange("p (t u) -> p t u", u=SLOT)
                                 for c in (1800, 2500, 3200))
            total = k_x[0:IMG, 4000:4001]
            pool = sml[:, 0:2 * IMG].rearrange("p (c m) -> p c m", c=2)

            def sync(sp):
                sp.wait_ge(s["phase_done"].sem, 4 * ROUTE[0])
                sp.dma_start(k_x[0:IMG, 1800:1800 + SLOT * SLOT], a["earlier"]).then_inc(s["bridge"].sem, 16)
                sp.wait_ge(s["job_used"].sem, b["job_used"] + 4)
                sp.dma_start(turn_d[0:1, :], s_row).then_inc(s["bridge"].sem, 16)
                sp.wait_ge(s["bridge"].sem, b["bridge"] + 32)
                sp.dma_start(s26, by_image(0)).then_inc(s["bridge"].sem, 16)
                sp.wait_ge(s["dve_step"].sem, b["dve_step"] + 9)
                sp.dma_start(by_image(1), w26).then_inc(s["bridge"].sem, 16)
                sp.dma_start(by_image(2), m26).then_inc(s["bridge"].sem, 16)
                sp.wait_ge(s["bridge"].sem, b["bridge"] + 80)
                sp.dma_start(w_row, turn_d[1:2, :]).then_inc(s["bridge"].sem, 16)
                sp.dma_start(m_row, turn_d[2:3, :]).then_inc(s["bridge"].sem, 16)

            def tensor(pe):
                pe.wait_ge(s["dve_step"].sem, b["dve_step"] + 2)
                for j in range(4):
                    c = slice(NJ * j, NJ * (j + 1))
                    five(bank[j][0:2, 0:NJ], [gw_hi[:, 0, 0:2], gw_hi[:, 1, 0:2]],
                         [gw_lo[:, 0, 0:2], gw_lo[:, 1, 0:2]], xa_hi[:, c], xa_lo[:, c], xb[:, c], True)\
                        .then_inc(s["job_full"].sem, 1)
                pe.wait_ge(s["bridge"].sem, b["bridge"] + 112)
                for x in range(12):
                    r, j = BROADCAST[x]
                    pe.wait_ge(s["job_used"].sem, b["job_used"] + (4 if x < 4 else x + 1))
                    src = (w_row, s_row, m_row)[r]
                    nc.tensor.matmul(bank[4 + x % 4][:, 0:NJ], row[0:1, ROW_COLS["ones"]],
                                     src[:, NJ * j:NJ * (j + 1)], start=True, stop=True).then_inc(s["job_full"].sem, 1)

            def scalar(act):
                for j in range(4):
                    act.wait_ge(s["job_full"].sem, b["job_full"] + j + 1)
                    nc.scalar.activation(s_row[:, NJ * j:NJ * (j + 1)], bank[j][0:1, 0:NJ], ACT.Sigmoid,
                                         bias=row[0:1, ROW_COLS.lo("L3_br"):ROW_COLS.lo("L3_br") + 1])\
                        .then_inc(s["job_used"].sem, 1)

            def vector(dve):
                link = chain(dve, s["dve_step"], [b["dve_step"]])
                w = dat[:, DATA_COLS["L3_r"]].rearrange("p (k e) -> p k e", k=2)
                link(nc.vector.tensor_copy(gw_hi[:, :, 0:2], w))
                link(nc.vector.tensor_tensor(gw_lo[:, :, 0:2], w, gw_hi[:, :, 0:2].bitcast(F32), ALU.subtract))
                dve.wait_ge(s["bridge"].sem, b["bridge"] + 48)
                n3 = [IMG, SLOT, SLOT]
                su, st = s26.unsqueeze(1).to_broadcast(n3), s26.unsqueeze(2).to_broadcast(n3)
                nc.vector.tensor_tensor(less, su, st, ALU.is_lt)
                nc.vector.tensor_reduce(total, s26, AX.X, ALU.add)
                link(nc.vector.tensor_tensor(same, su, st, ALU.is_equal))
                nc.vector.tensor_scalar(row[0:1, ROW_COLS["L3_bm"]], row[0:1, ROW_COLS["L3_bm"]], -1.0, None,
                                        ALU.mult)
                link(nc.vector.tensor_tensor(same, same, early, ALU.mult))
                nc.vector.tensor_scalar(total, total, 1e-6, None, ALU.add)
                link(nc.vector.tensor_tensor(less, less, same, ALU.add))
                nc.vector.reciprocal(total, total)
                link(nc.vector.tensor_reduce(m26, less, AX.X, ALU.add))
                link(nc.vector.tensor_scalar(m26, m26, KEEP - 0.5, None, ALU.is_lt))
                link(nc.vector.tensor_scalar(w26, s26, total, None, ALU.mult))
                link(nc.vector.memset(sml[:, 140:141], 0.0))
                g3 = [128, NJ // SLOT, SLOT]
                for x in range(12):
                    r, j = BROADCAST[x]
                    dve.wait_ge(s["job_full"].sem, b["job_full"] + 4 + x + 1)
                    p = bank[4 + x % 4][:, 0:NJ]
                    c = slice(NJ * j, NJ * (j + 1))
                    mc = slice(NJ // SLOT * j, NJ // SLOT * (j + 1))
                    if r == 0:
                        nc.vector.tensor_tensor(o_f[:, 0:NJ], feat[:, 0, c], p, ALU.mult)
                        link(nc.vector.tensor_tensor(o_f[:, NJ:2 * NJ], feat[:, 1, c], p, ALU.mult))
                        nc.vector.tensor_reduce(pool[:, :, mc], o_f[:, 0:2 * NJ].rearrange(
                            "p (c m t) -> p c m t", c=2, t=SLOT), AX.X, ALU.add).then_inc(s["job_used"].sem, 1)
                        dve.wait_ge(s["job_used"].sem, b["job_used"] + 4 + x + 1)
                        link(nc.vector.memset(sml[:, 140:141], 0.0))
                    elif r == 1:
                        for k in range(2):
                            t = nc.vector.tensor_tensor(
                                o_f[:, NJ * k:NJ * (k + 1)].rearrange("p (m t) -> p m t", t=SLOT),
                                p.rearrange("p (m t) -> p m t", t=SLOT),
                                pool[:, k, mc].unsqueeze(2).to_broadcast(g3), ALU.mult)
                        t.then_inc(s["job_used"].sem, 1)
                        dve.wait_ge(s["job_used"].sem, b["job_used"] + 4 + x + 1)
                        link(nc.vector.tensor_tensor(feat[:, :, c], feat[:, :, c], o_f[:, 0:2 * NJ].rearrange(
                            "p (c n) -> p c n", c=2), ALU.add))
                    else:
                        nc.vector.tensor_copy(mask_b[:, c], p)
                        nc.vector.tensor_scalar(o_f[:, 0:NJ], p, -1.0, 1.0, ALU.mult, ALU.add)\
                            .then_inc(s["job_used"].sem, 1)
                        dve.wait_ge(s["job_used"].sem, b["job_used"] + 4 + x + 1)
                        link(nc.vector.tensor_tensor(feat[:, :, c], feat[:, :, c],
                                                     o_f[:, 0:NJ].unsqueeze(1).to_broadcast([128, 2, NJ]),
                                                     ALU.mult))
                for _ in range(8):
                    dve.sem_inc(s["dve_step"].sem, 1)
            BROADCAST = [(0, j) for j in range(4)] + [(r, j) for j in range(4) for r in (1, 2)]
            phases.append(dict(tensor=tensor, scalar=scalar, vector=vector, sync=sync))

        mask_b = n_tok[:, :, :].rearrange("p t d -> p (t d)")[:, 0:TOK]
        ROUTE = [0]

        def add_phase(dst, src):
            def vector(dve):
                nc.vector.tensor_tensor(dst[:, :, :], dst[:, :, :], src[:, :, :], ALU.add)
            phases.append(dict(vector=vector))

        def attention_weights_phase(cfg, after):
            cols = 2 * cfg.C + (cfg.no + (2 if cfg.mix else 0)) * D
            low_rank = cfg.low_rank
            b = base(att_in=32 if low_rank else 16, dve_step=1, job_full=10 if low_rank else 0,
                     job_used=10 if low_rank else 0)
            memsets = [xs[:, :, :], q_t[:, :]] + [p[:, :, :] for p in p_t] + [rel_a[:, :, :]]

            def sync(sp):
                sp.wait_ge(s["phase_done"].sem, 4 * after)
                if low_rank:
                    sp.dma_start(low[:, :], a[cfg.dram + "_low"]).then_inc(s["att_in"].sem, 16)
                    sp.dma_start(wp_raw[:, 2 * cfg.C:cols], a[cfg.dram]).then_inc(s["att_in"].sem, 16)
                else:
                    sp.dma_start(wp_raw[:, 0:cols], a[cfg.dram]).then_inc(s["att_in"].sem, 16)

            def tensor(pe):
                if not low_rank:
                    return
                pe.wait_ge(s["att_in"].sem, b["att_in"] + 32)
                for m in range(5):
                    f = (0, 0, 1, 1, 2)[m]
                    for k in range(2):
                        n = 2 * m + k
                        if n >= 4:
                            pe.wait_ge(s["job_used"].sem, b["job_used"] + n - 3)
                        nc.tensor.matmul(bank[n % 4][:, 0:D], low[:, 256 * f + 128 * k:256 * f + 128 * k + 128],
                                         low[:, 768 + D * m:768 + D * m + D], start=True, stop=True)\
                            .then_inc(s["job_full"].sem, 1)

            def scalar(act):
                if not low_rank:
                    return
                for m in range(5):
                    for k in range(2):
                        n = 2 * m + k
                        act.wait_ge(s["job_full"].sem, b["job_full"] + n + 1)
                        c = k * cfg.C + D * m
                        nc.scalar.activation(wp_raw[:, c:c + D], bank[n % 4][:, 0:D], ACT.Identity)\
                            .then_inc(s["job_used"].sem, 1)

            def vector(dve):
                dve.wait_ge(s["att_in"].sem, b["att_in"] + (32 if low_rank else 16))
                if low_rank:
                    dve.wait_ge(s["job_used"].sem, b["job_used"] + 10)
                nc.vector.tensor_copy(wp_hi[:, 0:cols], wp_raw[:, 0:cols]).then_inc(s["dve_step"].sem, 1)
                dve.wait_ge(s["dve_step"].sem, b["dve_step"] + 1)
                nc.vector.tensor_tensor(wp_lo[:, 0:cols], wp_raw[:, 0:cols], wp_hi[:, 0:cols].bitcast(F32),
                                        ALU.subtract)
            phases.append(dict(sync=sync, tensor=tensor, scalar=scalar, vector=vector))

            def clear(dve):
                for m in memsets:
                    nc.vector.memset(m.bitcast(F32) if m.dtype == F32R else m, 0.0)
            phases.append(dict(vector=clear))

        def attention_phase(cfg):
            G, R, NC, HCH, H, d, no = cfg.G, cfg.R, cfg.NC, cfg.HCH, cfg.H, cfg.d, cfg.no
            NI, n = IMG // (4 * G), 4 * G * SLOT
            QW = n + 8
            W = H * d
            halves = 2 if W > 512 else 1
            HH, WH = H // halves, W // halves
            qk = cfg.qk
            rel_kind = cfg.kind == "rel"
            if cfg.kind == "performer":
                order = ["+qk", ("scores", 2), ("values", 0), ("exp", 2), "+fk", ("scores", 3), "+fq"]
            elif G == 4:
                order = [("scores", 2), ("values", 0), ("exp", 2), ("scores", 3), "+qk"]
            else:
                order = ["+qk", ("values", 0)]
            order += [("values", 1)]
            for g in range(2, G):
                order += [("exp", 3)] if g == 2 else []
                order += [("turn", g - 2), ("values", g)]
            order += ["+v", ("turn", G - 2), ("+scores", 0), ("+scores", 1), ("turn", G - 1), ("+exp", 0), "out",
                      ("+exp", 1)]
            dve_order = [("normalise", 0), ("shift", 2), ("normalise", 1), ("shift", 3), ("normalise", 2), "+spread",
                         ("normalise", 3)] if G == 4 else [("normalise", 0), ("normalise", 1), "+spread"]
            dve_order += [("+shift", 0), "split", ("+shift", 1)]

            def jobs_of(steps):
                jobs = []
                for step in steps:
                    name, g = (step, 0) if isinstance(step, str) else step
                    if name == "+qk":
                        jobs += [("qk", y) for y in range(len(qk))]
                    elif name in ("+fq", "+fk"):
                        jobs += [(name[1:], c) for c in range(4)]
                    elif name == "+v":
                        jobs += [("v", (h, v)) for h in range(G) for v in range(halves)]
                    elif name == "+scores" and rel_kind:
                        jobs.append(("rel", g))
                    elif name == "turn":
                        jobs += [("t", (g, v)) for v in range(halves)]
                    elif name == "out":
                        jobs += [("out", 0), ("out", 1)]
                return jobs

            def is_next(step):
                return (step if isinstance(step, str) else step[0])[0] == "+"
            first_steps = [step for step in order if is_next(step)]
            last_steps = [step for step in order if not is_next(step)]
            J, JA = len(jobs_of(order)), len(jobs_of(first_steps))
            assert J % 2 == 0 and JA % 2 == 0

            class Body:

                def __init__(self, steps, i, j0):
                    self.steps, self.i, self.j0 = steps, i, j0
                    self.first, self.last = steps is first_steps, steps is last_steps
                    self.at = {job: y for y, job in enumerate(jobs_of(steps))}

                def nth(self, name):
                    return self.j0 + self.at[name]

            def bodies(eng, run):
                run(Body(first_steps, -1, 0))
                with eng.Fori(0, NI - 1) as i:
                    run(Body(order, i, JA + J * i))
                run(Body(last_steps, NI - 1, JA + J * (NI - 1)))
            C = cfg.dve_steps
            b = base(job_full=J * NI, job_used=J * NI, staged=3 * NI, k_done=NI, s_full=16, s_used=16, z_full=16,
                     p_full=16, px_full=16, av_full=16 * halves, av_used=16 * halves, o_split=NI, it_dve=C * NI,
                     qk_ready=2 * NI)
            s_free, s_free_at = (s["z_full"], b["z_full"]) if cfg.kind == "softmax" else (s["s_used"], b["s_used"])
            heads = shp[0:R, SHAPE_COLS[{16: "head16", 32: "head32", 64: "head64"}[cfg.R // HCH]]]

            def w_part(w, k, c0, m):
                return w[:, k * cfg.C + c0:k * cfg.C + c0 + m]

            def w_pair(w, c0, m):
                return [w_part(w, 0, c0, m), w_part(w, 1, c0, m)]

            def qcols(c):
                return slice(c * QW, c * QW + n)

            def wo(w, k, c0):
                return w[:, 2 * cfg.C + k * D + c0:2 * cfg.C + k * D + c0 + 128]

            def bank_of(x):
                return bank[6 + x % 2]

            q_turned = spare[0:R, 0:2 * n]
            k_feat = spare[0:R, 0:4 * n]
            squares = spare[0:R, 4 * n:8 * n]
            mixed = wp_hi[:, NARROW:NARROW + 3 * n].rearrange("p (c n) -> p c n", c=3)
            k_flat = k_feat if cfg.kind == "performer" else k_t[0:R, :, :].rearrange("p c n -> p (c n)")
            rel_xs = [rel_x, k_x[:, 4000:4384].rearrange("p (h s) -> p h s", s=32)]

            def k_chunk(c):
                return k_flat[:, n * c:n * c + n]

            def gpsimd(pool):
                def stage(i):
                    for p, y in enumerate((xa_hi, xa_lo, xb)):
                        o = xs_v(p, G)[:, :, 0:SLOT]
                        nc.gpsimd.tensor_copy(o, y[:, bass.ds(n * i, n)].rearrange("p (m s) -> p m s", s=SLOT))\
                            .then_inc(s["staged"].sem, 1)
                stage(0)
                pool.wait_ge(s["job_full"].sem, b["job_full"] + JA)
                stage(1)
                with pool.Fori(0, NI - 2) as i:
                    last_v = Body(order, i, JA + J * i).nth(("v", (G - 1, halves - 1)))
                    pool.wait_ge(s["job_full"].sem, b["job_full"] + last_v + 1)
                    hold(pool)
                    stage(i + 2)

            def xs_v(p, G):
                return xs[:, p, 0:128 * G].rearrange("p (m s) -> p m s", s=32)

            def tensor(pe):
                def job(body, name):
                    pe.wait_ge(s["job_used"].sem, b["job_used"] + body.nth(name) - 1)
                    return bank_of(body.at[name])

                def xm(p):
                    return xs_v(p, G)[:, :, 0:SLOT]

                def scores(body, i, g):
                    t = G * i + g
                    pe.wait_ge(s_free.sem, s_free_at + t - 1)
                    if g == 0:
                        pe.wait_ge(s["k_done"].sem, b["k_done"] + i + 1)
                        last = ("fq", 3) if cfg.kind == "performer" else ("qk", len(qk) - 1)
                        pe.wait_ge(s["job_used"].sem, b["job_used"] + body.nth(last) + 1)
                    o = bank[4 + g % 2]
                    for im in range(4):
                        m = SLOT * (4 * g + im)
                        for c in range(NC):
                            kx = k_x[0:R, c * HCH * n:(c + 1) * HCH * n].rearrange("p (h n) -> p h n", n=n)
                            w = HCH * SLOT
                            ins = nc.tensor.matmul(o[32 * im:32 * im + 32, c * w:(c + 1) * w],
                                                   q_t[0:R, c * QW + m:c * QW + m + 32], kx[:, :, m:m + SLOT],
                                                   start=True, stop=True)
                    ins.then_inc(s["s_full"].sem, 1)

                def rel_scores(body, g):
                    o = job(body, ("rel", g))
                    for im in range(4):
                        m = SLOT * (4 * g + im)
                        for c in range(NC):
                            ins = nc.tensor.matmul(o[32 * im:32 * im + 32, 40 * c:40 * c + 40],
                                                   q_t[0:R, c * QW + m:c * QW + m + 32],
                                                   dat[0:R, DATA_COLS["tabk"]], start=True, stop=True)
                    ins.then_inc(s["job_full"].sem, 1)

                def values(body, g):
                    t = G * body.i + g
                    pe.wait_ge(s["px_full"].sem, b["px_full"] + t + 1)
                    if g == 0:
                        pe.wait_ge(s["job_used"].sem, b["job_used"] + body.j0)
                    hold(pe)
                    for v in range(halves):
                        pe.wait_ge(s["av_used"].sem, b["av_used"] + halves * t + v)
                        hold(pe)
                        for im in range(4):
                            p0 = 32 * im
                            for h in range(v * HH, v * HH + HH):
                                o = bank[im][p0:p0 + 32, (h - v * HH) * d:(h - v * HH) * d + d]
                                ins = nc.tensor.matmul(o, p_x[g % 2][p0:p0 + SLOT, h, :],
                                                       v_t[p0:p0 + SLOT, g * W + h * d:g * W + h * d + d],
                                                       start=True, stop=cfg.kind != "rel")
                                if cfg.kind == "rel":
                                    ins = nc.tensor.matmul(o, rel_xs[g % 2][p0:p0 + 20, h, :],
                                                           dat[p0:p0 + 20, DATA_COLS["tabv"]],
                                                           start=False, stop=True)
                        ins.then_inc(s["av_full"].sem, 1)

                def turn(body, g):
                    t = G * body.i + g
                    pe.wait_ge(s["av_used"].sem, b["av_used"] + halves * (t + 1))
                    x = o_t[g % 2]
                    if no == 2:
                        o = job(body, ("t", (g, 0)))
                        nc.tensor.transpose(o[:, 0:128], x[:, 0:128], shp[:, SHAPE_COLS["ident"]])
                        transpose_b(o[:, 128:256], x[:, 0:D]).then_inc(s["job_full"].sem, 1)
                    else:
                        for v in range(2):
                            o = job(body, ("t", (g, v)))
                            for k in range(3):
                                ins = nc.tensor.transpose(o[:, 128 * k:128 * k + 128],
                                                          x[:, 128 * (3 * v + k):128 * (3 * v + k) + 128],
                                                          shp[:, SHAPE_COLS["ident"]])
                            ins.then_inc(s["job_full"].sem, 1)

                def projections(body):
                    pe.wait_ge(s["staged"].sem, b["staged"] + 3 * (body.i + 2))
                    for y in range(len(qk)):
                        o = job(body, ("qk", y))
                        c0 = cfg.qcol(y)
                        five(o[0:R, 0:n], w_pair(wp_hi, c0, R), w_pair(wp_lo, c0, R), xm(0), xm(1), xm(2),
                             True).then_inc(s["job_full"].sem, 1)

                def features(body, f):
                    first = 0 if f == "fq" else 2
                    pe.wait_ge(s["qk_ready"].sem, b["qk_ready"] + 2 * (body.i + 1) + (1 if f == "fk" else 2))
                    for c in range(4):
                        o = job(body, (f, c))[0:96, 0:n]
                        r0 = DATA_COLS.lo("rand") + D * (c // 2) + 96 * (c % 2)
                        h0 = SHAPE_COLS.lo("halfnorm") + 96 * (c % 2)
                        nc.tensor.matmul(o, dat[0:96, r0:r0 + 96], k_t[0:96, first + c // 2, 0:n],
                                         start=True, stop=False)
                        q0 = n * (first + c // 2)
                        nc.tensor.matmul(o, shp[0:96, h0:h0 + 96], squares[:, q0:q0 + n],
                                         start=False, stop=True).then_inc(s["job_full"].sem, 1)

                def value_projections(body):
                    for g in range(G):
                        for v in range(halves):
                            o = job(body, ("v", (g, v)))[:, 0:WH]
                            c0 = cfg.vcol + WH * v
                            gc = slice(128 * g, 128 * g + 128)
                            ins = five(o, w_pair(wp_hi, c0, WH), w_pair(wp_lo, c0, WH), xs[:, 0, gc],
                                       xs[:, 1, gc], xs[:, 2, gc], False, stop=not cfg.vb)
                            if cfg.vb:
                                ins = nc.tensor.matmul(o, row[0:1, ROW_COLS["ones"]], row[0:1, ROW_COLS[cfg.vb]],
                                                       start=False, stop=True)
                            ins.then_inc(s["job_full"].sem, 1)

                def project_out(body):
                    pe.wait_ge(s["o_split"].sem, b["o_split"] + body.i + 1)
                    for k in range(2):
                        o = job(body, ("out", k))[:, 0:n]
                        c0 = 64 * k
                        if no == 2:
                            ins = five(o, [wo(wp_hi, 0, c0), wo(wp_hi, 1, c0)], [wo(wp_lo, 0, c0), wo(wp_lo, 1, c0)],
                                       o_hi[:, 0:n], o_lo[:, 0:n], o_hi[:, n:2 * n], True, stop=not cfg.mix)
                            if cfg.mix:
                                five(o, [wo(wp_hi, 2, c0), wo(wp_hi, 3, c0)], [wo(wp_lo, 2, c0), wo(wp_lo, 3, c0)],
                                     mixed[:, 0, :], mixed[:, 1, :], mixed[:, 2, :], True, start=False, stop=False)
                                for y, name in enumerate(("L3_bo", "L3_bm")):
                                    r0 = ROW_COLS.lo(name) + c0
                                    ins = nc.tensor.matmul(o, row[0:1, r0:r0 + 128], mask_b[0:1, bass.ds(n * body.i, n)],
                                                           start=False, stop=y == 1)
                        else:
                            for f in range(no):
                                fc = slice(n * f, n * f + n)
                                nc.tensor.matmul(o, wo(wp_hi, f, c0), o_hi[:, fc], start=f == 0, stop=False)
                                nc.tensor.matmul(o, wo(wp_hi, f, c0), o_lo[:, fc], start=False, stop=False)
                                ins = nc.tensor.matmul(o, wo(wp_lo, f, c0), o_hi[:, fc], start=False,
                                                       stop=f == no - 1)
                        ins.then_inc(s["job_full"].sem, 1)

                def steps(body):
                    for step in body.steps:
                        name, g = (step, 0) if isinstance(step, str) else step
                        if name == "+qk":
                            projections(body)
                        elif name in ("+fq", "+fk"):
                            features(body, name[1:])
                        elif name == "+v":
                            value_projections(body)
                        elif name == "+scores":
                            scores(body, body.i + 1, g)
                            if rel_kind:
                                rel_scores(body, g)
                        elif name == "scores":
                            scores(body, body.i, g)
                        elif name == "values":
                            values(body, g)
                        elif name == "turn":
                            turn(body, g)
                        elif name == "out":
                            project_out(body)
                bodies(pe, steps)

            def scalar(act):
                def job(body, name):
                    act.wait_ge(s["job_full"].sem, b["job_full"] + body.nth(name) + 1)
                    return bank_of(body.at[name])

                def projections(body):
                    if cfg.kind != "performer":
                        act.wait_ge(s["k_done"].sem, b["k_done"] + body.i + 1)
                    for y, (kind, c) in enumerate(qk):
                        p = job(body, ("qk", y))[0:R, 0:n]
                        if cfg.kind == "performer":
                            ins = nc.scalar.activation(k_t[0:R, y, 0:n], p, ACT.Identity,
                                                       scale=float(cfg.d) ** -0.25)
                            ins.then_inc(s["job_used"].sem, 1)
                            continue
                        dst = {"q": q_t[0:R, qcols(c)], "k": k_chunk(c), "qr": q_turned[:, n * (c % 2):n * (c % 2) + n],
                               "kr": k_t[0:R, (2 + c) % 4, 0:n]}[kind]
                        if cfg.bias:
                            col = DATA_COLS.lo(cfg.bias + {"q": "_qb", "k": "_kb"}[kind]) + c
                            ins = nc.scalar.activation(dst, p, ACT.Identity, bias=dat[0:R, col:col + 1])
                        else:
                            ins = nc.scalar.activation(dst, p, ACT.Identity)
                        ins.then_inc(s["job_used"].sem, 1)
                    if cfg.kind == "performer":
                        act.wait_ge(s["job_used"].sem, b["job_used"] + body.nth(("qk", 3)) + 1)
                        for y in (2, 3, 0, 1):
                            ins = nc.scalar.activation(squares[:, n * y:n * y + n], k_t[0:R, y, 0:n], ACT.Square)
                            if y in (3, 1):
                                ins.then_inc(s["qk_ready"].sem, 1)

                def features(body, f):
                    if f == "fk":
                        act.wait_ge(s["k_done"].sem, b["k_done"] + body.i + 1)
                    for c in range(4):
                        dst = q_t[0:96, qcols(c)] if f == "fq" else k_chunk(c)
                        nc.scalar.activation(dst, job(body, (f, c))[0:96, 0:n], ACT.Exp)\
                            .then_inc(s["job_used"].sem, 1)

                def value_projections(body):
                    for g in range(G):
                        for v in range(halves):
                            nc.scalar.activation(v_t[:, g * W + WH * v:g * W + WH * v + WH],
                                                 job(body, ("v", (g, v)))[:, 0:WH], ACT.Identity)\
                                .then_inc(s["job_used"].sem, 1)

                def rel_scores(body, g):
                    nc.scalar.activation(rel[g][:, :, :].rearrange("p h r -> p (h r)"),
                                         job(body, ("rel", g))[:, 0:240], ACT.Identity)\
                        .then_inc(s["job_used"].sem, 1)

                def exponents(i, g):
                    t = G * i + g
                    act.wait_ge(s["z_full"].sem, b["z_full"] + t + 1)
                    act.wait_ge(s["px_full"].sem, b["px_full"] + t - 1)
                    nc.scalar.activation(p_t[g % 2][:, 0:H, 0:SLOT], z_t[g % 2][:, 0:H, :],
                                         ACT.Exp, scale=cfg.scale).then_inc(s["p_full"].sem, 1)

                def values(body, g):
                    t = G * body.i + g
                    for v in range(halves):
                        act.wait_ge(s["av_full"].sem, b["av_full"] + halves * t + v + 1)
                        for im in range(4):
                            ins = nc.scalar.activation(o_t[g % 2][32 * im:32 * im + 32, v * WH:v * WH + WH],
                                                       bank[im][32 * im:32 * im + 32, 0:WH], ACT.Identity)
                        ins.then_inc(s["av_used"].sem, 1)

                def turn(body, g):
                    if g == 0:
                        act.wait_ge(s["o_split"].sem, b["o_split"] + body.i)
                    for v in range(halves):
                        o = job(body, ("t", (g, v)))
                        m = no // halves
                        src = o[:, 0:128 * m].rearrange("p (c b s) -> p c b s", c=m, b=4)[:, :, :, 0:SLOT]
                        dst = o_f[:, 0:no * n].rearrange("p (c g b s) -> p c g b s", c=no, g=G, b=4)[
                            :, v * m:v * m + m, g, :, :]
                        nc.scalar.activation(dst, src, ACT.Identity).then_inc(s["job_used"].sem, 1)

                def project_out(body):
                    for k in range(2):
                        o = job(body, ("out", k))[:, 0:n]
                        hold(act)
                        dst = feat[:, k, bass.ds(n * body.i, n)]
                        if cfg.ob:
                            col = DATA_COLS.lo(cfg.ob) + k
                            ins = nc.scalar.activation(dst, o, ACT.Identity, bias=dat[:, col:col + 1])
                        else:
                            ins = nc.scalar.activation(dst, o, ACT.Identity)
                        ins.then_inc(s["job_used"].sem, 1)

                def steps(body):
                    exps = cfg.kind in ("softmax", "rel", "causal")
                    for step in body.steps:
                        name, g = (step, 0) if isinstance(step, str) else step
                        if name == "+qk":
                            projections(body)
                        elif name in ("+fq", "+fk"):
                            features(body, name[1:])
                        elif name == "+v":
                            value_projections(body)
                        elif name == "+scores" and rel_kind:
                            rel_scores(body, g)
                        elif name == "values":
                            values(body, g)
                        elif name == "exp" and exps:
                            exponents(body.i, g)
                        elif name == "+exp" and exps:
                            exponents(body.i + 1, g)
                        elif name == "turn":
                            turn(body, g)
                        elif name == "out":
                            project_out(body)
                bodies(act, steps)

            def vector(dve):
                def link(ins):
                    ins.then_inc(s["it_dve"].sem, 1)
                    k[1] += 1
                    dve.wait_ge(s["it_dve"].sem, b["it_dve"] + k[0] + k[1])

                def spread(body):
                    if cfg.kind == "causal":
                        dve.wait_ge(s["job_used"].sem, b["job_used"] + body.nth(("qk", 7)) + 1)
                        cos = shp[0:R, SHAPE_COLS["cos"]].unsqueeze(1).to_broadcast([R, 4 * G, SLOT])
                        sin = shp[0:R, SHAPE_COLS["sin"]].unsqueeze(1).to_broadcast([R, 4 * G, SLOT])
                        for c in range(NC):
                            for x, xr in ((q_t[0:R, qcols(c)], q_turned[:, n * c:n * c + n]),
                                          (k_chunk(c), k_t[0:R, 2 + c, 0:n])):
                                x3, xr3 = (v.rearrange("p (m s) -> p m s", s=SLOT) for v in (x, xr))
                                nc.vector.tensor_tensor(x3, x3, cos, ALU.mult)
                                link(nc.vector.tensor_tensor(xr3, xr3, sin, ALU.mult))
                                link(nc.vector.tensor_tensor(x, x, xr, ALU.add))
                    for c in range(NC):
                        last = ("fk", c) if cfg.kind == "performer" else ("qk", qk.index(("k", c)))
                        dve.wait_ge(s["job_used"].sem, b["job_used"] + body.nth(last) + 1)
                        for h in range(HCH):
                            x = c * HCH + h
                            ins = nc.vector.tensor_scalar(k_x[0:R, x * n:(x + 1) * n], k_chunk(c),
                                                          heads[:, h:h + 1], None, ALU.mult)
                    ins.then_inc(s["k_done"].sem, 1)

                n3 = [128, H, SLOT]

                def shift(body, i, g):
                    t = G * i + g
                    j = g % 2
                    sc = bank[4 + j][:, 0:H * SLOT].rearrange("p (h s) -> p h s", s=SLOT)
                    z = z_t[j][:, 0:H, :]
                    mx = m12[:, j, 0:H]
                    dve.wait_ge(s["s_full"].sem, b["s_full"] + t + 1)
                    if cfg.kind == "performer":
                        dve.wait_ge(s["px_full"].sem, b["px_full"] + t - 1)
                        nc.vector.tensor_scalar(p_t[j][:, 0:H, 0:SLOT], sc, 1.0 / (2 * d), None, ALU.mult)\
                            .then_inc(s["s_used"].sem, 1)
                        return
                    if cfg.kind == "log2":
                        link(nc.vector.tensor_reduce(mx, sc, AX.X, ALU.max))
                        link(nc.vector.tensor_scalar(mx, mx, LOG2E, None, ALU.mult))
                        nc.vector.scalar_tensor_tensor(z, sc, LOG2E, bc(mx.unsqueeze(2), n3), ALU.mult,
                                                       ALU.subtract).then_inc(s["s_used"].sem, 1)
                        dve.wait_ge(s["s_used"].sem, b["s_used"] + t + 1)
                        zf, zi = (k_t[:, 2 + v, 0:H * SLOT].rearrange("p (h s) -> p h s", s=SLOT)
                                  for v in range(2))
                        link(nc.vector.tensor_scalar(z, z, -127.0, None, ALU.max))
                        magic = 1.5 * 2.0 ** 23
                        link(nc.vector.tensor_scalar(zf, z, magic, magic, ALU.add, ALU.subtract))
                        link(nc.vector.tensor_tensor(zi, zf, z, ALU.is_gt))
                        link(nc.vector.tensor_tensor(zi, zf, zi, ALU.subtract))
                        nc.vector.tensor_tensor(zf, z, zi, ALU.subtract)
                        bits = rel_p[:, :, :, :].rearrange("p h a c -> p (h a c)")[:, 0:H * SLOT]\
                            .rearrange("p (h s) -> p h s", s=SLOT)
                        link(nc.vector.tensor_scalar(bits.bitcast(I32), zi, 2.0 ** 23, 127.0 * 2 ** 23,
                                                     ALU.mult, ALU.add))
                        dve.wait_ge(s["px_full"].sem, b["px_full"] + t - 1)
                        nc.vector.scalar_tensor_tensor(p_t[j][:, 0:H, 0:SLOT], zf, 1.0, bits, ALU.add,
                                                       ALU.mult).then_inc(s["p_full"].sem, 1)
                        return
                    dve.wait_ge(s["p_full"].sem, b["p_full"] + t - 1)
                    src = sc
                    if cfg.kind == "causal":
                        mask = shp[:, SHAPE_COLS["causal"]].unsqueeze(1).to_broadcast(n3)
                        nc.vector.tensor_tensor(z, sc, mask, ALU.add).then_inc(s["s_used"].sem, 1)
                        dve.wait_ge(s["s_used"].sem, b["s_used"] + t + 1)
                        src = z
                    if cfg.kind == "rel":
                        dve.wait_ge(s["job_used"].sem, b["job_used"] + body.nth(("rel", g)) + 1)
                        rl = rel[j]
                        for v, ind in enumerate(("relv", "relh")):
                            pr = rel_p[:, :, :, :]
                            tb = rl[:, :, 10 * v:10 * v + 10].unsqueeze(2).to_broadcast([128, 12, 5, 10])
                            im = shp[:, SHAPE_COLS[ind]].rearrange("p (a r) -> p a r", r=10).unsqueeze(1)\
                                .to_broadcast([128, 12, 5, 10])
                            link(nc.vector.tensor_tensor(pr, tb, im, ALU.mult))
                            link(nc.vector.tensor_reduce(rel_u[:, v, :, :], pr, AX.X, ALU.add))
                        g4 = [128, 12, 5, 5]
                        z4 = z[:, :, 1:SLOT].rearrange("p h (a c) -> p h a c", c=5)
                        s4 = sc[:, :, 1:SLOT].rearrange("p h (a c) -> p h a c", c=5)
                        m0 = m12[:, 2, :].unsqueeze(2)
                        link(nc.vector.tensor_tensor(m0, rl[:, :, 0:1], rl[:, :, 10:11], ALU.add))
                        nc.vector.tensor_tensor(z[:, :, 0:1], sc[:, :, 0:1], m0, ALU.add)
                        nc.vector.tensor_tensor(z4, s4, rel_u[:, 0, :, :].unsqueeze(3).to_broadcast(g4),
                                                ALU.add).then_inc(s["s_used"].sem, 1)
                        dve.wait_ge(s["s_used"].sem, b["s_used"] + t + 1)
                        link(nc.vector.tensor_tensor(z4, z4, rel_u[:, 1, :, :].unsqueeze(2).to_broadcast(g4),
                                                     ALU.add))
                        src = z
                    link(nc.vector.tensor_reduce(mx, src, AX.X, ALU.max))
                    nc.vector.tensor_tensor(z, src, bc(mx.unsqueeze(2), n3), ALU.subtract)\
                        .then_inc(s["z_full"].sem, 1)

                def normalise(i, g):
                    t = G * i + g
                    j = g % 2
                    p = p_t[j][:, 0:H, 0:SLOT]
                    sm = m12[:, 2 + j, 0:H]
                    if cfg.kind == "performer":
                        dve.wait_ge(s["s_used"].sem, b["s_used"] + t + 1)
                    else:
                        dve.wait_ge(s["p_full"].sem, b["p_full"] + t + 1)
                    link(nc.vector.tensor_reduce(sm, p, AX.X, ALU.add))
                    if cfg.kind == "performer":
                        link(nc.vector.tensor_scalar(sm, sm, 1e-12, None, ALU.max))
                    link(nc.vector.reciprocal(sm, sm))
                    link(nc.vector.tensor_tensor(p, p, bc(sm.unsqueeze(2), n3), ALU.mult))
                    if cfg.kind == "rel":
                        pk = p[:, :, 1:SLOT].rearrange("p h (a c) -> p h a c", c=5)
                        nc.vector.tensor_reduce(rel_u[:, 0, :, :], pk, AX.X, ALU.add)
                        link(nc.vector.tensor_reduce(rel_u[:, 1, :, :], pk.rearrange("p h a c -> p h c a"),
                                                     AX.X, ALU.add))
                        for v, ind in enumerate(("relv", "relh")):
                            pr = rel_p[:, :, :, :].rearrange("p h a c -> p h (a c)")\
                                .rearrange("p h (r k) -> p h r k", k=5)
                            pu = rel_u[:, v, :, :].unsqueeze(2).to_broadcast([128, 12, 10, 5])
                            im = shp[:, SHAPE_COLS[ind]].rearrange("p (a r) -> p r a", r=10).unsqueeze(1)\
                                .to_broadcast([128, 12, 10, 5])
                            link(nc.vector.tensor_tensor(pr, pu, im, ALU.mult))
                            link(nc.vector.tensor_reduce(rel_a[:, :, 10 * v:10 * v + 10], pr, AX.X, ALU.add))
                        for v in range(2):
                            link(nc.vector.tensor_tensor(rel_a[:, :, 10 * v:10 * v + 1],
                                                         rel_a[:, :, 10 * v:10 * v + 1], p[:, :, 0:1], ALU.add))
                    dve.wait_ge(s["av_full"].sem, b["av_full"] + halves * (t - 1))
                    if cfg.kind == "rel":
                        nc.vector.transpose(rel_xs[j][:, :, :].rearrange("p h s -> p (h s)"),
                                            rel_a[:, :, :].rearrange("p h s -> p (h s)"))
                    nc.vector.transpose(p_x[j][:, 0:H, :].rearrange("p h s -> p (h s)"),
                                        p_t[j][:, 0:H, :].rearrange("p h s -> p (h s)"))\
                        .then_inc(s["px_full"].sem, 1)

                def split_result(body):
                    i = body.i
                    dve.wait_ge(s["job_used"].sem, b["job_used"] + body.nth(("t", (G - 1, halves - 1))) + 1)
                    if cfg.mix:
                        of3 = o_f[:, 0:2 * n].rearrange("p (c n) -> p c n", c=2)
                        link(nc.vector.tensor_tensor(of3, of3, mask_b[:, bass.ds(n * i, n)].unsqueeze(1)
                                                     .to_broadcast([128, 2, n]), ALU.mult))
                        hold(dve)
                        nc.vector.tensor_copy(mixed[:, 0, :], feat[:, 0, bass.ds(n * i, n)])
                        link(nc.vector.tensor_copy(mixed[:, 2, :], feat[:, 1, bass.ds(n * i, n)]))
                        nc.vector.tensor_tensor(mixed[:, 1, :], feat[:, 0, bass.ds(n * i, n)],
                                                mixed[:, 0, :].bitcast(F32), ALU.subtract)
                        nc.vector.tensor_tensor(mixed[64:128, 2, :], feat[64:128, 1, bass.ds(n * i, n)],
                                                mixed[64:128, 2, :].bitcast(F32), ALU.subtract)
                    link(nc.vector.tensor_copy(o_hi[:, 0:no * n], o_f[:, 0:no * n]))
                    if no == 2:
                        nc.vector.tensor_tensor(o_hi[64:128, n:2 * n], o_f[64:128, n:2 * n],
                                                o_hi[64:128, n:2 * n].bitcast(F32), ALU.subtract)
                    m = n if no == 2 else no * n
                    nc.vector.tensor_tensor(o_lo[:, 0:m], o_f[:, 0:m], o_hi[:, 0:m].bitcast(F32), ALU.subtract)\
                        .then_inc(s["o_split"].sem, 1)

                def steps(body):
                    if not body.first:
                        k[0], k[1] = k[2] + C * body.i, 0
                    for step in dve_order:
                        name, g = (step, 0) if isinstance(step, str) else step
                        if is_next(step):
                            if body.last:
                                continue
                            if name == "+spread":
                                spread(body)
                            else:
                                shift(body, body.i + 1, g)
                        elif body.first:
                            continue
                        elif name == "normalise":
                            normalise(body.i, g)
                        elif name == "shift":
                            shift(body, body.i, g)
                        else:
                            split_result(body)
                    if body.first:
                        k[2] = k[1]
                    assert body.first or body.last or k[1] == C, (cfg.dram, k)
                k = [0, 0, 0]
                bodies(dve, steps)
            for name, uses in (("s_used", cfg.kind != "softmax"), ("z_full", cfg.kind in ("softmax", "rel", "causal")),
                               ("p_full", cfg.kind != "performer"),
                               ("qk_ready", cfg.kind == "performer")):
                if not uses:
                    signals[name].at = b[name]
            phases.append(dict(tensor=tensor, scalar=scalar, vector=vector, gpsimd=gpsimd))

        qk4 = [("q", 0), ("q", 1), ("k", 0), ("k", 1)]
        std = dict(H=12, d=16, G=4, qk=qk4, qcol=lambda x: 96 * x, vcol=2 * D, C=3 * D)
        l0 = Attention("L0_att", "causal", 6, 32, 4, [(k, c) for k in ("q", "qr", "k", "kr") for c in range(2)],
                    lambda x: 96 * x, 4 * D, 5 * D, 25, scale=32 ** -0.5, low_rank=True)
        l1 = Attention("L1_att", "rel", 12, 64, 2, [(k, c) for k in ("q", "k") for c in range(6)],
                    lambda x: 128 * x, 12 * 128, 18 * 128, 35, scale=0.125, ob="L1_ob", no=6, R=128, NC=6)
        l2a = Attention("L2_att", "performer", dve_steps=17, ob="L2a_ob", NC=4, **std)
        l2f = Attention("L2_fat", "softmax", dve_steps=17, scale=0.25, bias="L2f", vb="L2f_vb", ob="L2f_ob", **std)
        l3a = Attention("L3_att", "log2", dve_steps=41, bias="L3a", vb="L3a_vb", ob="L3a_ob", **std)

        l3f = Attention("L3_fat", "softmax", dve_steps=19, scale=0.25, bias="L3f", vb="L3f_vb", ob="L3f_ob", mix=True,
                     **std)

        def attention(cfg, res, after):
            attention_weights_phase(cfg, after)
            attention_phase(cfg)
            add_back_phase(res)

        conv_phase()
        norm_phase(h_tok, n_tok)
        features_phase(n_tok)
        attention(l0, h_tok, 1)
        norm_phase(h_tok, n_tok)
        features_phase(n_tok)
        gates_phase(32, "L0_g", "L0_gb", "softmax")
        experts_phase(32, a["L0_exp"], "L0_b1", "L0_b2", h_tok, ACT.Gelu)
        free = len(phases)
        norm_phase(h_tok, n_tok)
        features_phase(n_tok)
        attention(l1, h_tok, free)
        norm_phase(h_tok, n_tok)
        features_phase(n_tok)
        gates_phase(8, "L1_g", None, "top1")
        experts_phase(8, a["L1_exp"], "L1_b1", "L1_b2", h_tok, ACT.Silu)
        free = len(phases)
        norm_phase(h_tok, n_tok)
        features_phase(n_tok)
        attention(l2a, h_tok, free)
        free = len(phases)
        norm_phase(h_tok, y_tok)
        norm_phase(y_tok, n_tok)
        features_phase(n_tok, "ln_L2f1")
        attention(l2f, y_tok, free)
        features_phase(y_tok)
        experts_phase(1, a["L2_mlp"], "L2m_b1", "L2m_b2", y_tok, ACT.Gelu)
        norm_phase(y_tok, n_tok)
        features_phase(n_tok, "ln_L2f2")
        gates_phase(4, "L2_g", "L2_gb", "top2")
        experts_phase(4, a["L2_exp"], "L2e_b1", "L2e_b2", y_tok, ACT.Gelu)
        add_phase(h_tok, y_tok)
        free = len(phases)
        norm_phase(h_tok, n_tok)
        quantise_phase(n_tok)
        features_phase(n_tok)
        attention(l3a, h_tok, free)
        norm_phase(h_tok, y_tok)
        norm_phase(y_tok, n_tok)
        features_phase(n_tok, "ln_L3f1")
        ROUTE[0] = len(phases)
        route_phase()
        attention(l3f, y_tok, len(phases))
        norm_phase(y_tok, n_tok)
        features_phase(n_tok, "ln_L3f2")
        experts_phase(1, a["L3_mlp"], "L3_b1", "L3_b2", y_tok, ACT.Gelu)
        add_phase(h_tok, y_tok)

        block = ctx.enter_context(nc.Block())
        loads = [(shp[:, :], a["shape_pack"]), (dat[:, :], a["data_pack"]), (row[:, :], a["row_pack"]),
                 (pix[:, :, :], a["pixels"]), (conv_w[:, :, :], a["conv_w"]), (tok0[:, :, :], a["tok0"]),
                 (conv_row[:, :], a["conv_row"])]
        CONSTS = len(loads)
        started = [n for n in names if signals[n] and n not in
                   ("consts_in", "w_in0", "w_in1", "att_in", "out_done", "bridge", "phase_done", "holds")]

        def run(eng, kind):
            for n, ph in enumerate(phases):
                if kind in ph:
                    ph[kind](eng)
                eng.drain().then_inc(s["phase_done"].sem, 1)
                eng.wait_ge(s["phase_done"].sem, 4 * (n + 1))

        @block.sync
        def _(sp):
            for dst, src in loads:
                sp.dma_start(dst, src).then_inc(s["consts_in"].sem, 16)
            for ph in phases:
                if "sync" in ph:
                    ph["sync"](sp)
            sp.wait_ge(s["phase_done"].sem, 4 * len(phases))
            sp.dma_start(out, h_tok[:, :, :]).then_inc(s["out_done"].sem, 16)
            sp.wait_ge(s["out_done"].sem, 16)

        @block.gpsimd
        def _(pool):
            for n in started:
                pool.sem_inc(signals[n].sem, START)
            run(pool, "gpsimd")

        @block.scalar
        def _(act):
            run(act, "scalar")

        @block.vector
        def _(dve):
            run(dve, "vector")

        @block.tensor
        def _(pe):
            run(pe, "tensor")


def pad2(w):
    o = np.zeros((128, 2, w.shape[1]), w.dtype)
    o[:, 0] = w[:DA]
    o[:DB, 1] = w[DA:]
    o[DB:, 1] = w[DA:]
    return o


def shape_pack():
    o = np.zeros((128, SHAPE_COLS.n), np.float32)
    p = np.arange(128)
    o[p, SHAPE_COLS.lo("ident") + p] = 1
    for name, d, rows in (("head16", 16, 96), ("head32", 32, 96), ("head64", 64, 128)):
        r = np.arange(rows)
        o[r, SHAPE_COLS.lo(name) + r // d] = 1
    inv = 1.0 / 10000.0 ** (np.arange(0, 32, 2, dtype=np.float32) / 32)
    f = np.outer(np.arange(SLOT, dtype=np.float32), inv).astype(np.float32)
    emb = np.concatenate([f, f], 1)
    r = np.arange(96)
    o[:96, SHAPE_COLS["cos"]] = np.cos(emb).T[r % 32]
    o[:96, SHAPE_COLS["sin"]] = (np.sin(emb).T * np.where(np.arange(32) < 16, -1, 1)[:, None])[r % 32]
    q = p % 32
    o[:, SHAPE_COLS["causal"]] = np.where(np.arange(SLOT)[None] > q[:, None], -BIG, 0)
    hn = np.zeros((128, D), np.float32)
    for k in range(2):
        for c in range(96):
            hn[(3 * k + c // 32) * 16:(3 * k + c // 32) * 16 + 16, 96 * k + c] = -0.5
    o[:, SHAPE_COLS["halfnorm"]] = hn
    for name, div in (("relv", True), ("relh", False)):
        ind = np.zeros((128, SIDE, 10), np.float32)
        for i in range(128):
            m = i % 32 - 1
            for k in range(SIDE):
                if m < 0 or m >= SIDE * SIDE:
                    ind[i, k, 0] = 1
                else:
                    ind[i, k, k - (m // SIDE if div else m % SIDE) + 5] = 1
        o[:, SHAPE_COLS["" + name]] = ind.reshape(128, 50)
    o[:, SHAPE_COLS["order8"]] = np.arange(8, 0, -1)[None]
    return o


def expert_pack(w1, w2):
    E = w1.shape[0]
    o = np.zeros((E, 128, RAW), w1.dtype)
    v = o[:, :, :2 * HID].reshape(E, 128, 2, HID)
    v[:, :, 0] = w1[:, :DA]
    v[:, :DB, 1] = w1[:, DA:]
    v[:, DB:, 1] = w1[:, DA:]
    o[:, :, :2 * HID] = v.reshape(E, 128, 2 * HID)
    o[:, :, 2 * HID:] = w2.reshape(E, HC, 128, D).transpose(0, 2, 1, 3).reshape(E, 128, HC * D)
    return o


def chunked_bias(b):
    return b.reshape(-1, HC, 128).transpose(2, 0, 1).reshape(128, -1)


def layout(i):
    g = {k: np.asarray(v) for k, v in i.items()}
    f = np.float32
    dat = np.zeros((128, DATA_COLS.n), f)
    row = np.zeros((1, ROW_COLS.n), f)

    def col(name, v):
        dat[:v.shape[0], DATA_COLS[name]] = v
    col("L0_b1", chunked_bias(g["L0_ffn_b1"]))
    col("L1_b1", chunked_bias(g["L1_ffn_b1"]))
    col("L2m_b1", chunked_bias(g["L2_ffn_mlp_b1"]))
    col("L2e_b1", chunked_bias(g["L2_ffn_exp_b1"]))
    col("L3_b1", chunked_bias(g["L3_ffn_bf1"]))
    for name, v in (("L2f_qb", g["L2_ffn_in_b"][:D]), ("L2f_kb", g["L2_ffn_in_b"][D:2 * D]),
                    ("L3a_qb", g["L3_attn_bq"]), ("L3a_kb", g["L3_attn_bk"]),
                    ("L3f_qb", g["L3_ffn_bq"]), ("L3f_kb", g["L3_ffn_bk"])):
        col(name, v.reshape(2, 96).T)
    for name, v in (("L1_ob", g["L1_attn_proj_b"]), ("L2a_ob", g["L2_attn_proj_b"]), ("L2f_ob", g["L2_ffn_out_b"]),
                    ("L3a_ob", g["L3_attn_bo"]), ("L3f_ob", g["L3_ffn_bm"])):
        col(name, np.stack([v[:128], v[64:]], 1))
    for name, gg, bb in (("ln_L2f1", g["L2_ffn_ln1_g"], g["L2_ffn_ln1_b"]), ("ln_L2f2", g["L2_ffn_ln2_g"], g["L2_ffn_ln2_b"]),
                         ("ln_L3f1", g["L3_ffn_g1"], g["L3_ffn_b1"]), ("ln_L3f2", g["L3_ffn_g2"], g["L3_ffn_b2"])):
        col(name, np.concatenate([pad2(gg[:, None])[:, :, 0], pad2(bb[:, None])[:, :, 0]], 1))
    col("L0_g", pad2(g["L0_ffn_gate_w"]).reshape(128, -1))
    col("L1_g", pad2(g["L1_ffn_Wg"]).reshape(128, -1))
    col("L2_g", pad2(g["L2_ffn_gate_w"].T).reshape(128, -1))
    wr = np.zeros((D, 2), f)
    wr[:, 0] = g["L3_ffn_Wr"]
    col("L3_r", pad2(wr).reshape(128, -1))
    col("L0_b2", g["L0_ffn_b2"])
    col("L1_b2", g["L1_ffn_b2"])
    col("L2e_b2", g["L2_ffn_exp_b2"])
    rand = np.zeros((96, 2, D), f)
    for h in range(12):
        rand[16 * (h % 6):16 * (h % 6) + 16, h // 6, 32 * (h % 6):32 * (h % 6) + 32] = g["L2_attn_rand_matrix"][h]
    col("rand", rand.reshape(96, -1))
    rows = [0] + list(range(11, 20))
    tk = np.zeros((128, 2, 20), f)
    for h in range(2):
        tk[64 * h:64 * h + 64, h, :10] = g["L1_attn_tab_kv"][rows].T
        tk[64 * h:64 * h + 64, h, 10:] = g["L1_attn_tab_kh"][rows].T
    col("tabk", tk.reshape(128, 40))
    tv = np.zeros((4, 32, 64), f)
    tv[:, :10] = g["L1_attn_tab_vv"][rows][None]
    tv[:, 10:20] = g["L1_attn_tab_vh"][rows][None]
    col("tabv", tv.reshape(128, 64))

    def rowset(name, v):
        row[0, ROW_COLS[name]] = v
    row[0, ROW_COLS["ones"]] = 1
    for name, v in (("L0_gb", g["L0_ffn_gate_b"]), ("L2_gb", g["L2_ffn_gate_b"]),
                    ("L2f_vb", g["L2_ffn_in_b"][2 * D:]), ("L3a_vb", g["L3_attn_bv"]), ("L3f_vb", g["L3_ffn_bv"]),
                    ("L2m_b2", g["L2_ffn_mlp_b2"]), ("L3_b2", g["L3_ffn_bf2"]),
                    ("L3_bo", g["L3_ffn_bo"]), ("L3_bm", g["L3_ffn_bm"])):
        rowset(name, v)
    row[0, ROW_COLS.lo("L3_br")] = g["L3_ffn_br"]
    x = g["x"][:, :, :80, :80].reshape(IMG, 3, SIDE, 16, SIDE, 16).transpose(1, 3, 5, 0, 2, 4)
    px = np.zeros((PIX, IMG, SLOT), f)
    px[:, :, 1:] = x.reshape(PIX, IMG, SIDE * SIDE)
    bounds = np.arange(1.0 / 32, 1.0, 1.0 / 32, dtype=f)
    frac = np.arange(0.0, 1.0 - 1e-06, 1.0 / SIDE, dtype=f)
    bins = np.searchsorted(bounds, frac, side="right")
    pos = g["L0_tok_pos_table"][(bins[:, None] * 32 + bins).reshape(-1)]
    tok0 = np.zeros((IMG, SLOT, D), f)
    tok0[:, 0] = g["cls_tok"][0, 0]
    tok0[:, 1:] = pos
    arrays = {
        "conv_row": np.concatenate([(np.arange(TOK) % SLOT != 0).astype(f), g["L0_tok_conv_b"]])[None],
        "shape_pack": shape_pack(), "data_pack": dat, "row_pack": row,
        "pixels": px.reshape(PIX // 128, 128, TOK).transpose(1, 0, 2),
        "conv_w": g["L0_tok_conv_w"].reshape(D, PIX).T.reshape(PIX // 128, 128, D).transpose(1, 0, 2),
        "tok0": tok0.reshape(TILES, 128, D).transpose(1, 0, 2),
        "L0_exp": expert_pack(g["L0_ffn_w1"], g["L0_ffn_w2"]),
        "L1_exp": expert_pack(g["L1_ffn_W1"], g["L1_ffn_W2"]),
        "L2_mlp": expert_pack(g["L2_ffn_mlp_w1"][None], g["L2_ffn_mlp_w2"][None]),
        "L2_exp": expert_pack(g["L2_ffn_exp_w1"], g["L2_ffn_exp_w2"]),
        "L3_mlp": expert_pack(g["L3_ffn_W1"][None], g["L3_ffn_W2"][None]),
    }

    def att(name, qkv, o):
        o = pad2(o).reshape(128, -1) if o.shape[0] == D else \
            o.reshape(-1, 128, D).transpose(1, 0, 2).reshape(128, -1)
        arrays[name] = np.concatenate([pad2(qkv).reshape(128, -1), o], 1) if qkv is not None else o

    def twice(m):
        m = m.T
        return [m[:, :DA], m[:, DA:], m[:, DA:]]
    turned = (np.arange(D) // 32) * 32 + (np.arange(D) % 32 + 16) % 32
    att("L0_att", None, g["L0_attn_o_w"])
    arrays["L0_att_low"] = np.concatenate(
        twice(g["L0_attn_qA"]) + twice(g["L0_attn_kA"]) + twice(g["L0_attn_vA"])
        + [g["L0_attn_qB"], g["L0_attn_qB"][:, turned], g["L0_attn_kB"], g["L0_attn_kB"][:, turned],
           g["L0_attn_vB"]], 1)
    att("L1_att", g["L1_attn_qkv_w"].T, g["L1_attn_proj_w"].T)
    att("L2_att", g["L2_attn_qkv_w"].T, g["L2_attn_proj_w"].T)
    att("L2_fat", g["L2_ffn_in_w"].T, g["L2_ffn_out_w"].T)
    att("L3_att", np.concatenate([g["L3_attn_Wq"], g["L3_attn_Wk"], g["L3_attn_Wv"]], 1), g["L3_attn_Wo"])
    att("L3_fat", np.concatenate([g["L3_ffn_Wq"], g["L3_ffn_Wk"], g["L3_ffn_Wv"]], 1), g["L3_ffn_Wo"])
    arrays["L3_fat"] = np.concatenate([arrays["L3_fat"], pad2(g["L3_ffn_Wm"]).reshape(128, -1)], 1)
    t = np.arange(SLOT)
    arrays["earlier"] = np.tile((t[None, :] < t[:, None]).astype(f).reshape(1, -1), (IMG, 1))
    return {k: np.ascontiguousarray(v) for k, v in arrays.items()}


def kernel(**inputs):
    import numpy as _np
    import concourse.bacc as _bacc
    from concourse import mybir as _mybir
    from concourse.bass_utils import run_bass_kernel_spmd as _run

    nc = _bacc.Bacc("TRN2", target_bir_lowering=False, num_devices=1)
    arrays = layout(inputs)
    args = {k: nc.dram_tensor("in_" + k, v.shape, _mybir.dt.from_np(v.dtype), kind="ExternalInput").ap()
            for k, v in arrays.items()}
    o = nc.dram_tensor("out_0", (128, TILES, D), _mybir.dt.float32, kind="ExternalOutput").ap()
    vit_tower(nc, args, o)
    r = _run(nc, [{"in_" + k: v for k, v in arrays.items()}], core_ids=[0])
    return _np.ascontiguousarray(r.results[0]["out_0"].transpose(1, 0, 2).reshape(IMG, SLOT, D))
```

```python
import numpy as np
import concourse.bass as bass
from concourse import mybir
from contextlib import ExitStack

F32 = mybir.dt.float32
F32R = mybir.dt.float32r
I32 = mybir.dt.int32
ALU = mybir.AluOpType
ACT = mybir.ActivationFunctionType
AX = mybir.AxisListType

D = 192
DA = 128
DB = D - DA
IMG, SLOT = 64, 26
SIDE = 5
TOK = IMG * SLOT
TILES = TOK // 128
HID = 768
HC = HID // 128
PIX = 768
BLOCKS = [(0, 3), (3, 3), (6, 3), (9, 4)]
RAW = 2 * HID + HC * D
START = 64
LN_EPS = 1e-5
LOG2E = 1.4426950408889634
BIG = 1.0e30


class Signal:

    def __init__(self, sem, at):
        self.sem, self.at = sem, at


class Attention:

    def __init__(self, dram, kind, H, d, G, qk, qcol, vcol, C, dve_steps, scale=1.0, bias=None, vb=None, ob=None,
                 no=2, R=96, NC=2, low_rank=False, mix=False):
        self.dram, self.kind, self.H, self.d, self.G = dram, kind, H, d, G
        self.qk, self.qcol, self.vcol, self.C, self.dve_steps = qk, qcol, vcol, C, dve_steps
        self.scale, self.bias, self.vb, self.ob, self.no = scale, bias, vb, ob, no
        self.no_q = 4 if kind == "performer" else NC
        self.R, self.NC, self.HCH, self.low_rank, self.mix = R, NC, H // NC, low_rank, mix




class Columns:

    def __init__(self, spec):
        self.at, self.n = {}, 0
        for name, width in spec:
            self.at[name] = (self.n, width)
            self.n += width

    def __getitem__(self, name):
        a, w = self.at[name]
        return slice(a, a + w)

    def lo(self, name):
        return self.at[name][0]


SHAPE_COLS = Columns([("ident", 128), ("head16", 6), ("head32", 3), ("head64", 2), ("cos", SLOT), ("sin", SLOT),
                      ("causal", SLOT), ("halfnorm", D), ("relv", 50), ("relh", 50), ("order8", 8)])
DATA_COLS = Columns([("L0_b1", 32 * HC), ("L1_b1", 8 * HC), ("L2m_b1", HC), ("L2e_b1", 4 * HC), ("L3_b1", HC),
                     ("L2f_qb", 2), ("L2f_kb", 2), ("L3a_qb", 2), ("L3a_kb", 2), ("L3f_qb", 2), ("L3f_kb", 2),
                     ("L1_ob", 2), ("L2a_ob", 2), ("L2f_ob", 2), ("L3a_ob", 2), ("L3f_ob", 2),
                     ("ln_L2f1", 4), ("ln_L2f2", 4), ("ln_L3f1", 4), ("ln_L3f2", 4),
                     ("L0_g", 64), ("L1_g", 16), ("L2_g", 8), ("L3_r", 4),
                     ("L0_b2", D), ("L1_b2", D), ("L2e_b2", D),
                     ("rand", 2 * D), ("tabk", 40), ("tabv", 64)])
ROW_COLS = Columns([("ones", 128), ("L0_gb", 32), ("L1_gb", 8), ("L2_gb", 4),
                    ("L3_br", 2), ("L2f_vb", D), ("L3a_vb", D), ("L3f_vb", D), ("L2m_b2", D), ("L3_b2", D),
                    ("L3_bo", D), ("L3_bm", D)])


def vit_tower(nc, a, out, stop=99):
    ctx = ExitStack()

    def sb(name, shape, dt=F32, scope=None):
        return (scope or ctx).enter_context(nc.sbuf_tensor(name, shape, dt))

    def pb(name):
        return ctx.enter_context(nc.psum_tensor(name, [128, 512], F32))

    signals = {}

    def signal(name, start=START):
        signals[name] = Signal(ctx.enter_context(nc.semaphore(name)), start)
        return signals[name]

    with ctx:
        h_tok = sb("h_tok", [128, TILES, D])
        y_tok = sb("y_tok", [128, TILES, D])
        n_tok = sb("n_tok", [128, TILES, D])
        feat = sb("feat", [128, 2, TOK])
        XP = TOK + 8
        xa_hi = sb("xa_hi", [128, XP], F32R)
        xa_lo = sb("xa_lo", [128, XP], F32R)
        xb = sb("xb", [128, XP], F32R)
        shp = sb("shp", [128, SHAPE_COLS.n])
        dat = sb("dat", [128, DATA_COLS.n])
        row = sb("row", [1, ROW_COLS.n])
        gate = sb("gate", [128, TILES, 32])
        gate_t = feat[0:32, 1, :]
        gsc = feat[:, 0, :].rearrange("p (k n) -> p k n", k=4)
        stats = sb("stats", [128, TILES, 6])
        mv = sb("mv", [128, TILES, 2])
        rstd = sb("rstd", [128, 4, TILES])
        sml = sb("sml", [128, 160])
        gw_hi = sb("gw_hi", [128, 2, 32], F32R)
        gw_lo = sb("gw_lo", [128, 2, 32], F32R)

        ex = ExitStack()
        raw = [sb(f"raw{j}", [128, RAW], scope=ex) for j in range(2)]
        w1_hi = [sb(f"w1_hi{j}", [128, 2, HID], F32R, ex) for j in range(2)]
        w1_lo = [sb(f"w1_lo{j}", [128, 2, HID], F32R, ex) for j in range(2)]
        w2 = [sb(f"w2_{j}", [128, HC, 2 * D], F32R, ex) for j in range(2)]
        hid = [sb(f"hid{j}", [128, 512], scope=ex) for j in range(3)]
        hid_hi = [sb(f"hid_hi{j}", [128, HC, 512], F32R, ex) for j in range(2)]
        hid_lo = [sb(f"hid_lo{j}", [128, HC, 512], F32R, ex) for j in range(2)]
        ex.close()

        cv = ExitStack()
        pix = sb("pix", [128, PIX // 128, TOK], scope=cv)
        conv_w = sb("conv_w", [128, PIX // 128, D], scope=cv)
        tok0 = sb("tok0", [128, TILES, D], scope=cv)
        conv_row = sb("conv_row", [1, TOK + D], scope=cv)
        cv.close()

        AW, NARROW = 5760, 2304
        nr = ExitStack()
        sb("wp_narrow", [128, NARROW], F32R, nr)
        spare = sb("spare", [128, AW - NARROW], scope=nr)
        nr.close()
        at = ExitStack()
        wp_hi = sb("wp_hi", [128, AW], F32R, at)
        wp_lo = sb("wp_lo", [128, AW], F32R, at)
        xs = sb("xs", [128, 3, 512], F32R, at)
        o_hi = sb("o_hi", [128, 6 * 208], F32R, at)
        o_lo = sb("o_lo", [128, 6 * 208], F32R, at)
        rw = ExitStack()
        wp_raw = sb("wp_raw", [128, AW], scope=rw)
        low = sb("low", [48, 3 * 256 + 5 * D], scope=rw)
        rw.close()
        q_t = sb("q_t", [128, 4 * 424], scope=at)
        k_t = sb("k_t", [128, 4, 416], scope=at)
        k_x = sb("k_x", [128, 12 * 416], scope=at)
        v_t = sb("v_t", [128, 4 * 384], scope=at)
        z_t = [sb(f"z_t{j}", [128, 12, SLOT], scope=at) for j in range(2)]
        p_t = [sb(f"p_t{j}", [128, 12, 32], scope=at) for j in range(2)]
        p_x = [sb(f"p_x{j}", [128, 12, 32], scope=at) for j in range(2)]
        o_t = [sb(f"o_t{j}", [128, HID], scope=at) for j in range(2)]
        o_f = sb("o_f", [128, 6 * 208], scope=at)
        m12 = sb("m12", [128, 4, 12], scope=at)
        rel = [sb(f"rel{j}", [128, 12, 20], scope=at) for j in range(2)]
        rel_p = sb("rel_p", [128, 12, 5, 10], scope=at)
        rel_u = sb("rel_u", [128, 2, 12, 5], scope=at)
        rel_a = sb("rel_a", [128, 12, 32], scope=at)
        at.close()

        bank = [pb(f"bank{j}") for j in range(8)]

        pix_in = [ctx.enter_context(nc.semaphore(f"pix_in{c}")) for c in range(PIX // 128)]
        names = ["consts_in", "conv_in", "phase_done", "dve_step", "act_step", "pool_step",
                 "w_in0", "w_in1", "w_split", "h_full", "h_act", "h_split", "y_full", "y_used", "att_in",
                 "job_full", "job_used", "staged", "qk_ready", "s_full", "s_used", "z_full", "p_full",
                 "px_full", "av_full", "av_used", "t_full", "t_used", "out_done", "bridge", "k_done",
                 "o_split", "it_dve", "holds", "root", "normed", "hi_full", "scale_full", "lo_full", "hi_step", "rel_table", "att_hi", "att_ready"]
        s = {n: signal(n) for n in names}
        s["consts_in"].at = s["w_in0"].at = s["w_in1"].at = s["att_in"].at = s["out_done"].at = s["bridge"].at = 0
        s["phase_done"].at = s["conv_in"].at = 0

        phases = []

        def base(**adds):
            b = {k: signals[k].at for k in adds}
            for k, v in adds.items():
                signals[k].at += v
            return b

        def hold(eng):
            eng.sem_inc(s["holds"].sem, 1)

        def chain(eng, sig, n):
            def link(ins):
                ins.then_inc(sig.sem, 1)
                n[0] += 1
                eng.wait_ge(sig.sem, n[0])
            return link

        def beside(phase, *others):
            def in_turn(parts):
                def run_parts(eng):
                    for part in parts:
                        part(eng)
                return run_parts
            all_of = (phase,) + others
            return {kind: in_turn([ph[kind] for ph in all_of if kind in ph]) for kind in
                    ("sync", "tensor", "scalar", "vector", "gpsimd") if any(kind in ph for ph in all_of)}

        def preload(func):
            c = 156 + (ACT.Sqrt, ACT.Exp).index(func) if func in (ACT.Sqrt, ACT.Exp) else 158
            nc.scalar.activation(sml[:, c:c + 1], shp[:, 0:1], func)

        def bc(ap, shape):
            return ap.to_broadcast(shape)

        def conv_phase():
            b = base(job_full=TILES, job_used=TILES)

            def tensor(pe):
                pe.wait_ge(s["conv_in"].sem, 32)
                PC = PIX // 128

                def product(t, c):
                    nc.tensor.matmul(bank[t % 8][:, 0:D], pix[:, c, 128 * t:128 * t + 128], conv_w[:, c, :],
                                     start=c == 0, stop=False)

                def bias(t):
                    nc.tensor.matmul(bank[t % 8][:, 0:D], conv_row[0:1, 128 * t:128 * t + 128],
                                     conv_row[0:1, TOK:TOK + D], start=False, stop=True)\
                        .then_inc(s["job_full"].sem, 1)
                for c in range(PC):
                    pe.wait_ge(pix_in[c], 16)
                    for t in range(8):
                        product(t, c)
                for t in range(8):
                    bias(t)
                for t in range(8, TILES):
                    pe.wait_ge(s["job_used"].sem, b["job_used"] + t - 7)
                    for c in range(PC):
                        product(t, c)
                    bias(t)

            def vector(dve):
                dve.wait_ge(s["consts_in"].sem, 16 * CONSTS)
                for t in range(TILES):
                    dve.wait_ge(s["job_full"].sem, b["job_full"] + t + 1)
                    nc.vector.tensor_tensor(h_tok[:, t, :], bank[t % 8][:, 0:D], tok0[:, t, :],
                                            ALU.add).then_inc(s["job_used"].sem, 1)
            phases.append(dict(tensor=tensor, vector=vector))

        def norm_phase(src, dst, *others):
            b = base(dve_step=2 * TILES + 2, act_step=1, scale_full=1)
            ON_DVE = 7

            def vector(dve):
                for t in range(TILES):
                    nc.vector.bn_stats(stats[:, t, :], src[:, t, :]).then_inc(s["dve_step"].sem, 1)
                for t in range(TILES):
                    dve.wait_ge(s["dve_step"].sem, b["dve_step"] + t + 1)
                    nc.vector.bn_aggr(mv[:, t, :], stats[:, t, :]).then_inc(s["dve_step"].sem, 1)
                dve.wait_ge(s["dve_step"].sem, b["dve_step"] + 2 * TILES)
                nc.vector.tensor_scalar(rstd[:, 0, :], mv[:, :, 1], LN_EPS, None,
                                        ALU.add).then_inc(s["dve_step"].sem, 1)
                dve.wait_ge(s["act_step"].sem, b["act_step"] + 1)
                nc.vector.reciprocal(rstd[:, 2, :], rstd[:, 1, :]).then_inc(s["dve_step"].sem, 1)
                dve.wait_ge(s["dve_step"].sem, b["dve_step"] + 2 * TILES + 2)
                nc.vector.scalar_tensor_tensor(rstd[:, 3, :], mv[:, :, 0], -1.0, rstd[:, 2, :], ALU.mult,
                                               ALU.mult).then_inc(s["scale_full"].sem, 1)
                for t in range(ON_DVE):
                    nc.vector.tensor_scalar(dst[:, t, :], src[:, t, :], mv[:, t, 0:1], rstd[:, 2, t:t + 1],
                                            ALU.subtract, ALU.mult)

            def scalar(act):
                preload(ACT.Sqrt)
                act.wait_ge(s["dve_step"].sem, b["dve_step"] + 2 * TILES + 1)
                nc.scalar.activation(rstd[:, 1, :], rstd[:, 0, :], ACT.Sqrt).then_inc(s["act_step"].sem, 1)
                act.wait_ge(s["scale_full"].sem, b["scale_full"] + 1)
                for t in range(ON_DVE, TILES):
                    nc.scalar.activation(dst[:, t, :], src[:, t, :], ACT.Identity, bias=rstd[:, 3, t:t + 1],
                                         scale=rstd[:, 2, t:t + 1])
            phases.append(beside(dict(vector=vector, scalar=scalar), *others))

        def transpose_b(o, x):
            ident = shp[:, SHAPE_COLS["ident"]]
            nc.tensor.transpose(o, x[:, DB:D], ident)
            return nc.tensor.transpose(o[0:DB, :], x[:, DA:D], ident)

        TBLK = [(0, 2), (2, 4), (6, 4), (10, 3)]

        def features_phase(src, *others, ln=None, norm_of=None):
            b = base(t_full=4, t_used=4, dve_step=2 * TILES + 4, root=4, normed=4, hi_full=4, scale_full=4, lo_full=4, hi_step=8 if ln else 0)
            ident = shp[:, SHAPE_COLS["ident"]]

            def banks(i, n):
                return bank[2 * i][:, 0:128 * n], bank[2 * i + 1][:, 0:128 * n]

            def tensor(pe):
                for i, (t0, n) in enumerate(TBLK):
                    if norm_of is not None:
                        pe.wait_ge(s["normed"].sem, b["normed"] + i + 1)
                    pa, pbk = banks(i, n)
                    for j in range(n):
                        y = src[:, t0 + j, :]
                        nc.tensor.transpose(pa[:, 128 * j:128 * j + 128], y[:, 0:DA], ident)
                        ins = transpose_b(pbk[:, 128 * j:128 * j + 128], y)
                    ins.then_inc(s["t_full"].sem, 1)

            def scalar(act):
                def root(i):
                    t0, n = TBLK[i]
                    act.wait_ge(s["dve_step"].sem, b["dve_step"] + 2 * (t0 + n) + i + 1)
                    nc.scalar.activation(rstd[:, 1, t0:t0 + n], rstd[:, 0, t0:t0 + n], ACT.Sqrt)\
                        .then_inc(s["root"].sem, 1)

                def normalise(i):
                    t0, n = TBLK[i]
                    act.wait_ge(s["scale_full"].sem, b["scale_full"] + i + 1)
                    for t in range(t0, t0 + n):
                        ins = nc.scalar.activation(src[:, t, :], norm_of[:, t, :], ACT.Identity,
                                                   bias=rstd[:, 3, t:t + 1], scale=rstd[:, 2, t:t + 1])
                    ins.then_inc(s["normed"].sem, 1)

                def high(i):
                    t0, n = TBLK[i]
                    act.wait_ge(s["t_full"].sem, b["t_full"] + i + 1)
                    for part in range(2):
                        src_p = banks(i, n)[part]
                        c = slice(128 * t0, 128 * (t0 + n))
                        for o in ((feat[:, part, c],) if ln else ((xa_hi, xb)[part][:, c],)):
                            if ln:
                                g = DATA_COLS.lo(ln) + part
                                ins = nc.scalar.activation(o, src_p, ACT.Identity, bias=dat[:, g + 2:g + 3],
                                                           scale=dat[:, g:g + 1])
                            else:
                                ins = nc.scalar.activation(o, src_p, ACT.Identity)
                    ins.then_inc(s["hi_full"].sem, 1)

                if norm_of is not None:
                    preload(ACT.Sqrt)
                    root(0)
                    root(1)
                    normalise(0)
                    root(2)
                    normalise(1)
                    root(3)
                    high(0)
                    normalise(2)
                    normalise(3)
                else:
                    high(0)
                for i in range(1, 4):
                    high(i)

            def vector(dve):
                def statistics(i):
                    t0, n = TBLK[i]
                    first = b["dve_step"] + 2 * t0 + i
                    for t in range(t0, t0 + n):
                        nc.vector.bn_stats(stats[:, t, :], norm_of[:, t, :]).then_inc(s["dve_step"].sem, 1)
                    for t in range(t0, t0 + n):
                        dve.wait_ge(s["dve_step"].sem, first + t - t0 + 1)
                        nc.vector.bn_aggr(mv[:, t, :], stats[:, t, :]).then_inc(s["dve_step"].sem, 1)
                    dve.wait_ge(s["dve_step"].sem, first + 2 * n)
                    nc.vector.tensor_scalar(rstd[:, 0, t0:t0 + n], mv[:, t0:t0 + n, 1], LN_EPS, None,
                                            ALU.add).then_inc(s["dve_step"].sem, 1)

                def scales(i):
                    t0, n = TBLK[i]
                    dve.wait_ge(s["root"].sem, b["root"] + i + 1)
                    nc.vector.reciprocal(rstd[:, 2, t0:t0 + n], rstd[:, 1, t0:t0 + n])\
                        .then_inc(s["t_used"].sem, 1)
                    dve.wait_ge(s["t_used"].sem, b["t_used"] + i + 1)
                    nc.vector.scalar_tensor_tensor(rstd[:, 3, t0:t0 + n], mv[:, t0:t0 + n, 0], -1.0,
                                                   rstd[:, 2, t0:t0 + n], ALU.mult, ALU.mult)\
                        .then_inc(s["scale_full"].sem, 1)

                if norm_of is not None:
                    statistics(0)
                    statistics(1)
                    scales(0)
                    statistics(2)
                    scales(1)
                    statistics(3)
                    scales(2)
                    scales(3)
                for i, (t0, n) in enumerate(TBLK):
                    dve.wait_ge(s["hi_full"].sem, b["hi_full"] + i + 1)
                    c = slice(128 * t0, 128 * (t0 + n))
                    pa, pbk = banks(i, n)
                    va, vb = (feat[:, 0, c], feat[64:128, 1, c]) if ln else (pa, pbk[64:128, :])
                    if ln:
                        nc.vector.tensor_copy(xa_hi[:, c], feat[:, 0, c]).then_inc(s["hi_step"].sem, 1)
                        nc.vector.tensor_copy(xb[:, c], feat[:, 1, c]).then_inc(s["hi_step"].sem, 1)
                        dve.wait_ge(s["hi_step"].sem, b["hi_step"] + 2 * i + 2)
                    nc.vector.tensor_tensor(xa_lo[:, c], va, xa_hi[:, c].bitcast(F32), ALU.subtract)
                    nc.vector.tensor_tensor(xb[64:128, c], vb, xb[64:128, c].bitcast(F32), ALU.subtract)\
                        .then_inc(s["lo_full"].sem, 1)
            if norm_of is None:
                for name in ("dve_step", "root", "normed", "scale_full", "t_used"):
                    signals[name].at = b[name]
            phases.append(beside(dict(tensor=tensor, scalar=scalar, vector=vector), *others))

        def five(o, wh, wl, xh, xl, xbt, w_first, start=True, stop=True):
            parts = [(wh[0], xh), (wh[0], xl), (wl[0], xh), (wh[1], xbt), (wl[1], xbt)]
            for n, (w, x) in enumerate(parts):
                l, r = (w, x) if w_first else (x, w)
                ins = nc.tensor.matmul(o, l, r, start=start and n == 0, stop=stop and n == 4)
            return ins

        def gates(E, g_col, gb_col, kind):
            steps = {"softmax": 8, "top1": 12, "top2": 24}[kind]
            b = base(dve_step=steps, job_full=6, job_used=4, t_full=TILES, t_used=TILES, act_step=1)
            n3 = [128, TILES, E]

            def v3(k):
                return gsc[:, k, 0:TILES * E].rearrange("p (t e) -> p t e", e=E)
            G = gate[:, :, 0:E]

            def logits(pe):
                pe.wait_ge(s["dve_step"].sem, b["dve_step"] + 2)
                NJ = TOK // 4
                for j in range(4):
                    c = slice(NJ * j, NJ * (j + 1))
                    five(bank[j][0:E, 0:NJ], [gw_hi[:, 0, 0:E], gw_hi[:, 1, 0:E]],
                         [gw_lo[:, 0, 0:E], gw_lo[:, 1, 0:E]], xa_hi[:, c], xa_lo[:, c], xb[:, c], True)\
                        .then_inc(s["job_full"].sem, 1)
                pe.wait_ge(s["job_used"].sem, b["job_used"] + 4)
                for t in range(TILES):
                    o = bank[0][:, E * t:E * t + E]
                    ins = nc.tensor.matmul(o, gate_t[0:E, 128 * t:128 * t + 128],
                                           shp[0:E, SHAPE_COLS.lo("ident"):SHAPE_COLS.lo("ident") + E],
                                           start=True, stop=not gb_col)
                    if gb_col:
                        ins = nc.tensor.matmul(o, row[0:1, ROW_COLS["ones"]], row[0:1, ROW_COLS[gb_col]],
                                               start=False, stop=True)
                ins.then_inc(s["job_full"].sem, 1)

            def turn(pe):
                pe.wait_ge(s["job_full"].sem, b["job_full"] + 6)
                for t in range(TILES):
                    if t >= 3:
                        pe.wait_ge(s["t_used"].sem, b["t_used"] + t - 2)
                    nc.tensor.transpose(bank[1 + t % 3][0:E, 0:128], gate[:, t, 0:E],
                                        shp[:, SHAPE_COLS["ident"]]).then_inc(s["t_full"].sem, 1)
                pe.wait_ge(s["t_used"].sem, b["t_used"] + TILES)

            def exponents(act):
                NJ = TOK // 4
                for j in range(4):
                    act.wait_ge(s["job_full"].sem, b["job_full"] + j + 1)
                    nc.scalar.activation(gate_t[0:E, NJ * j:NJ * (j + 1)], bank[j][0:E, 0:NJ], ACT.Identity)\
                        .then_inc(s["job_used"].sem, 1)
                preload(ACT.Exp)
                act.wait_ge(s["dve_step"].sem, b["dve_step"] + (5 if kind != "top2" else 14))
                nc.scalar.activation(v3(1) if kind != "top2" else gsc[:, 1, 0:TILES],
                                     v3(0) if kind != "top2" else gsc[:, 0, 0:TILES], ACT.Exp)\
                    .then_inc(s["act_step"].sem, 1)

            def keep_turned(act):
                for t in range(TILES):
                    act.wait_ge(s["t_full"].sem, b["t_full"] + t + 1)
                    nc.scalar.activation(gate_t[0:E, 128 * t:128 * t + 128], bank[1 + t % 3][0:E, 0:128],
                                         ACT.Identity).then_inc(s["t_used"].sem, 1)

            def vector(dve):
                n = [b["dve_step"]]
                link = chain(dve, s["dve_step"], n)
                w = dat[:, DATA_COLS[g_col]].rearrange("p (k e) -> p k e", k=2)
                link(nc.vector.tensor_copy(gw_hi[:, :, 0:E], w))
                link(nc.vector.tensor_tensor(gw_lo[:, :, 0:E], w, gw_hi[:, :, 0:E].bitcast(F32), ALU.subtract))
                dve.wait_ge(s["job_full"].sem, b["job_full"] + 5)
                lg = bank[0][:, 0:TILES * E].rearrange("p (t e) -> p t e", e=E)
                link(nc.vector.tensor_copy(v3(3), lg))
                mx = sml[:, 0:TILES]

                def first_of(eq_src, target, dst):
                    order = shp[:, SHAPE_COLS["order8"]][:, 0:E].unsqueeze(1).to_broadcast(n3)
                    link(nc.vector.tensor_tensor(dst, eq_src, bc(target.unsqueeze(2), n3), ALU.is_equal))
                    link(nc.vector.tensor_tensor(dst, dst, order, ALU.mult))
                    link(nc.vector.tensor_reduce(sml[:, 48:48 + TILES], dst, AX.X, ALU.max))
                    link(nc.vector.tensor_tensor(dst, dst, bc(sml[:, 48:48 + TILES].unsqueeze(2), n3),
                                                 ALU.is_equal))
                link(nc.vector.tensor_reduce(mx, v3(3), AX.X, ALU.max))
                if kind != "top2":
                    link(nc.vector.tensor_tensor(v3(0), v3(3), bc(mx.unsqueeze(2), n3), ALU.subtract))
                    dve.wait_ge(s["act_step"].sem, b["act_step"] + 1)
                    link(nc.vector.tensor_reduce(sml[:, 16:16 + TILES], v3(1), AX.X, ALU.add))
                    link(nc.vector.reciprocal(sml[:, 32:32 + TILES], sml[:, 16:16 + TILES]))
                    inv = bc(sml[:, 32:32 + TILES].unsqueeze(2), n3)
                    if kind == "softmax":
                        link(nc.vector.tensor_tensor(G, v3(1), inv, ALU.mult))
                    else:
                        first_of(v3(3), mx, v3(2))
                        link(nc.vector.tensor_tensor(G, v3(2), inv, ALU.mult))
                else:
                    m2 = sml[:, 64:64 + TILES]
                    first_of(v3(3), mx, v3(2))
                    link(nc.vector.tensor_scalar(v3(1), v3(2), -BIG, None, ALU.mult))
                    link(nc.vector.tensor_tensor(v3(1), v3(1), v3(3), ALU.add))
                    link(nc.vector.tensor_reduce(m2, v3(1), AX.X, ALU.max))
                    link(nc.vector.tensor_copy(v3(3), v3(1)))
                    first = gsc[:, 0, 256:256 + TILES * E].rearrange("p (t e) -> p t e", e=E)
                    link(nc.vector.tensor_copy(first, v3(2)))
                    link(nc.vector.tensor_tensor(gsc[:, 0, 0:TILES], m2, mx, ALU.subtract))
                    dve.wait_ge(s["act_step"].sem, b["act_step"] + 1)
                    e2 = gsc[:, 1, 0:TILES]
                    link(nc.vector.tensor_scalar(sml[:, 16:16 + TILES], e2, 1.0, None, ALU.add))
                    link(nc.vector.reciprocal(sml[:, 32:32 + TILES], sml[:, 16:16 + TILES]))
                    link(nc.vector.tensor_tensor(sml[:, 80:80 + TILES], e2, sml[:, 32:32 + TILES], ALU.mult))
                    first_of(v3(3), m2, v3(2))
                    link(nc.vector.tensor_tensor(v3(2), v3(2), bc(sml[:, 80:80 + TILES].unsqueeze(2), n3),
                                                 ALU.mult))
                    link(nc.vector.tensor_tensor(first, first, bc(sml[:, 32:32 + TILES].unsqueeze(2), n3),
                                                 ALU.mult))
                    link(nc.vector.tensor_tensor(G, first, v3(2), ALU.add))
                assert n[0] == b["dve_step"] + steps
                dve.sem_inc(s["job_full"].sem, 1)
            return dict(tensor=(logits, turn), scalar=(exponents, keep_turned), vector=vector)

        def expert_weights(E, dram, after):
            b = base(w_split=4 * E, w_in0=16 * ((E + 1) // 2), w_in1=16 * (E // 2))

            def sync(sp):
                sp.wait_ge(s["phase_done"].sem, 3 * after)
                for e in range(min(E, 2)):
                    sp.dma_start(raw[e][:, :], dram[e]).then_inc((s["w_in0"], s["w_in1"])[e].sem, 16)

            def gpsimd(pool):
                split_weights(pool, b, 0, 0, 0)
            return dict(sync=sync), dict(gpsimd=gpsimd), b

        def split_weights(pool, b, e, j, i):
            w_in, at = ((s["w_in0"], b["w_in0"]), (s["w_in1"], b["w_in1"]))[j]
            pool.wait_ge(w_in.sem, at + 16 * (i + 1))
            hold(pool)
            r1 = raw[j][:, 0:2 * HID].rearrange("p (k n) -> p k n", k=2)
            r2 = raw[j][:, 2 * HID:RAW].rearrange("p (c n) -> p c n", c=HC)
            nc.gpsimd.tensor_copy(w1_hi[j][:, :, :], r1).then_inc(s["w_split"].sem, 1)
            nc.gpsimd.tensor_copy(w2[j][:, :, 0:D], r2).then_inc(s["w_split"].sem, 1)
            pool.wait_ge(s["w_split"].sem, b["w_split"] + 4 * e + 1)
            nc.gpsimd.tensor_tensor(w1_lo[j][:, :, :], r1, w1_hi[j][:, :, :].bitcast(F32),
                                    ALU.subtract).then_inc(s["w_split"].sem, 1)
            pool.wait_ge(s["w_split"].sem, b["w_split"] + 4 * e + 2)
            nc.gpsimd.tensor_tensor(w2[j][:, :, D:2 * D], r2, w2[j][:, :, 0:D].bitcast(F32),
                                    ALU.subtract).then_inc(s["w_split"].sem, 1)

        def experts_phase(E, dram, b1_col, b2_col, res, func, weights, gating=None):
            b = base(h_full=24 * E, h_act=24 * E, h_split=24 * E, y_full=TILES * (E + 1),
                     y_used=TILES * (E + 1), dve_step=(24 + TILES) * E)
            b.update(weights)
            w_in = [s["w_in0"], s["w_in1"]]
            STEPS = 24 + TILES

            def is_first(e):
                return isinstance(e, int) and e == 0

            def over_experts(eng, body, first=0):
                body(0, 0, 0)
                if E > 1:
                    body(1, 1, 0)
                    with eng.Fori(0, E // 2 - 1) as i:
                        body(2 * i + 2, 0, i + 1)
                        body(2 * i + 3, 1, i + 1)

            def sync(sp):
                if E > 2:
                    with sp.Fori(0, E // 2 - 1) as i:
                        for j in range(2):
                            sp.wait_ge(s["w_split"].sem, b["w_split"] + 4 * (2 * i + j + 1))
                            sp.dma_start(raw[j][:, :], dram[bass.ds(2 * i + j + 2, 1)]
                                         .rearrange("o p n -> p (o n)")).then_inc(w_in[j].sem, 16)

            def gpsimd(pool):
                if E > 1:
                    split_weights(pool, b, 1, 1, 0)
                    with pool.Fori(0, E // 2 - 1) as i:
                        for j in range(2):
                            pool.wait_ge(s["y_full"].sem, b["y_full"] + TILES * (2 * i + j + 2))
                            hold(pool)
                            split_weights(pool, b, 2 * i + 2 + j, j, i + 1)

            def tensor(pe):
                if gating:
                    gating["tensor"][0](pe)

                def second_biases():
                    if gating:
                        gating["tensor"][1](pe)
                    for t in range(TILES):
                        if t >= 4:
                            pe.wait_ge(s["y_used"].sem, b["y_used"] + t - 3)
                        if E == 1:
                            l, r = row[0:1, ROW_COLS["ones"]], row[0:1, ROW_COLS[b2_col]]
                        else:
                            l, r = gate_t[0:E, 128 * t:128 * t + 128], dat[0:E, DATA_COLS[b2_col]]
                        nc.tensor.matmul(bank[t % 4][:, 0:D], l, r, start=True, stop=True)\
                            .then_inc(s["y_full"].sem, 1)

                def up(e, j, k):
                    t0, nt = BLOCKS[k]
                    c = slice(128 * t0, 128 * (t0 + nt))
                    for m in range(HC):
                        n = 24 * e + 6 * k + m
                        pe.wait_ge(s["h_act"].sem, b["h_act"] + n - 3)
                        o = bank[4 + (6 * k + m) % 4][:, 0:128 * nt]
                        mc = slice(128 * m, 128 * m + 128)
                        five(o, [w1_hi[j][:, 0, mc], w1_hi[j][:, 1, mc]],
                             [w1_lo[j][:, 0, mc], w1_lo[j][:, 1, mc]],
                             xa_hi[:, c], xa_lo[:, c], xb[:, c], True).then_inc(s["h_full"].sem, 1)

                def down(e, j, k):
                    t0, nt = BLOCKS[k]
                    for t in range(nt):
                        n = TILES * (e + 1) + t0 + t
                        if t == 0:
                            pe.wait_ge(s["h_split"].sem, b["h_split"] + 24 * e + 6 * k + 6)
                        pe.wait_ge(s["y_used"].sem, b["y_used"] + n - (3 if t0 + t else 0))
                        o = bank[(t0 + t) % 4]
                        c = slice(128 * t, 128 * t + 128)
                        for m in range(HC):
                            nc.tensor.matmul(o[:, 0:2 * D], hid_hi[k % 2][:, m, c], w2[j][:, m, :],
                                             start=m == 0, stop=False)
                            ins = nc.tensor.matmul(o[:, 0:D], hid_lo[k % 2][:, m, c], w2[j][:, m, 0:D],
                                                   start=False, stop=m == HC - 1)
                        ins.then_inc(s["y_full"].sem, 1)

                def body(e, j, i):
                    pe.wait_ge(s["w_split"].sem, b["w_split"] + 4 * (e + 1))
                    up(e, j, 0)
                    if is_first(e):
                        second_biases()
                    for k in range(1, 4):
                        up(e, j, k)
                        down(e, j, k - 1)
                    down(e, j, 3)
                over_experts(pe, body)

            def scalar(act):
                if gating:
                    gating["scalar"][0](act)
                preload(func)

                def body(e, j, i):
                    for k, (t0, nt) in enumerate(BLOCKS):
                        for m in range(HC):
                            n = 24 * e + 6 * k + m
                            act.wait_ge(s["h_full"].sem, b["h_full"] + n + 1)
                            act.wait_ge(s["h_split"].sem, b["h_split"] + n - 2)
                            col = DATA_COLS.lo(b1_col) + m
                            hold(act)
                            bias = dat[:, col:col + 1] if E == 1 else dat[:, bass.ds(HC * e + col, 1)]
                            nc.scalar.activation(hid[(6 * k + m) % 3][:, 0:128 * nt],
                                                 bank[4 + (6 * k + m) % 4][:, 0:128 * nt], func,
                                                 bias=bias).then_inc(s["h_act"].sem, 1)
                        if gating and k == 0 and is_first(e):
                            gating["scalar"][1](act)
                over_experts(act, body)

            def vector(dve):
                if gating:
                    gating["vector"](dve)

                def add_second_biases():
                    for t in range(TILES):
                        dve.wait_ge(s["y_full"].sem, b["y_full"] + t + 1)
                        nc.vector.tensor_tensor(res[:, t, :], bank[t % 4][:, 0:D], res[:, t, :],
                                                ALU.add).then_inc(s["y_used"].sem, 1)

                def split(e, j, k):
                    t0, nt = BLOCKS[k]
                    w = 128 * nt
                    prev = [TILES * e + BLOCKS[3][0], TILES * (e + 1), TILES * (e + 1) + BLOCKS[1][0],
                            TILES * (e + 1) + BLOCKS[2][0]][k]
                    if not (is_first(e) and k == 0):
                        dve.wait_ge(s["y_full"].sem, b["y_full"] + prev)
                    for m in range(HC):
                        n = 24 * e + 6 * k + m
                        dve.wait_ge(s["h_act"].sem, b["h_act"] + n + 1)
                        h = hid[(6 * k + m) % 3][:, 0:w]
                        nc.vector.tensor_copy(hid_hi[k % 2][:, m, 0:w], h).then_inc(s["dve_step"].sem, 1)
                        dve.wait_ge(s["dve_step"].sem, b["dve_step"] + STEPS * e + 6 * k + m + 1
                                    + (BLOCKS[k - 1][0] if k > 1 else 0))
                        nc.vector.tensor_tensor(hid_lo[k % 2][:, m, 0:w], h,
                                                hid_hi[k % 2][:, m, 0:w].bitcast(F32),
                                                ALU.subtract).then_inc(s["h_split"].sem, 1)

                def gather(e, j, k):
                    t0, nt = BLOCKS[k]
                    for t in range(t0, t0 + nt):
                        n = TILES * (e + 1) + t
                        dve.wait_ge(s["y_full"].sem, b["y_full"] + n + 1)
                        o = bank[t % 4]
                        g = 1.0 if E == 1 else gate[:, t, bass.ds(e, 1)]
                        nc.vector.scalar_tensor_tensor(res[:, t, :], o[:, 0:D], g, res[:, t, :], ALU.mult,
                                                       ALU.add).then_inc(s["dve_step"].sem, 1)
                        done_splits = 6 * min(k + 2, 4)
                        dve.wait_ge(s["dve_step"].sem, b["dve_step"] + STEPS * e + done_splits + t + 1)
                        nc.vector.scalar_tensor_tensor(res[:, t, :], o[:, D:2 * D], g, res[:, t, :], ALU.mult,
                                                       ALU.add).then_inc(s["y_used"].sem, 1)

                def body(e, j, i):
                    split(e, j, 0)
                    if is_first(e):
                        add_second_biases()
                    for k in range(1, 4):
                        split(e, j, k)
                        gather(e, j, k - 1)
                    gather(e, j, 3)
                over_experts(dve, body)
            phases.append(dict(tensor=tensor, scalar=scalar, vector=vector, gpsimd=gpsimd, sync=sync))

        def add_back_phase(res, *others):
            b = base(t_full=TILES, t_used=TILES)
            ident = shp[:, SHAPE_COLS["ident"]]

            def tensor(pe):
                for t in range(TILES):
                    if t >= 8:
                        pe.wait_ge(s["t_used"].sem, b["t_used"] + t - 7)
                    c = slice(128 * t, 128 * t + 128)
                    nc.tensor.transpose(bank[t % 8][:, 0:128], feat[:, 0, c], ident)
                    nc.tensor.transpose(bank[t % 8][:, 64:192], feat[:, 1, c], ident)\
                        .then_inc(s["t_full"].sem, 1)

            def vector(dve):
                for t in range(TILES):
                    dve.wait_ge(s["t_full"].sem, b["t_full"] + t + 1)
                    nc.vector.tensor_tensor(res[:, t, :], bank[t % 8][:, 0:D], res[:, t, :],
                                            ALU.add).then_inc(s["t_used"].sem, 1)
            phases.append(beside(dict(tensor=tensor, vector=vector), *others))

        def quantise_phase(x):
            b = base(dve_step=10, t_full=1, job_full=1)
            v = x[:, :, :].rearrange("p t d -> p (t d)")
            q = y_tok[:, :, :].rearrange("p t d -> p (t d)")
            top, one, sc, inv = (sml[:, 150 + j:151 + j] for j in range(4))

            def tensor(pe):
                pe.wait_ge(s["dve_step"].sem, b["dve_step"] + 1)
                nc.tensor.transpose(bank[0][0:1, 0:128], top, shp[:, SHAPE_COLS["ident"]])\
                    .then_inc(s["t_full"].sem, 1)
                pe.wait_ge(s["dve_step"].sem, b["dve_step"] + 4)
                nc.tensor.matmul(bank[1][:, 0:1], row[0:1, ROW_COLS["ones"]], one[0:1, :], start=True, stop=True)\
                    .then_inc(s["job_full"].sem, 1)

            def vector(dve):
                link = chain(dve, s["dve_step"], [b["dve_step"]])
                link(nc.vector.tensor_reduce(top, v, AX.X, ALU.max, apply_absolute_value=True))
                dve.wait_ge(s["t_full"].sem, b["t_full"] + 1)
                link(nc.vector.tensor_reduce(one[0:1, :], bank[0][0:1, 0:128], AX.X, ALU.max))
                link(nc.vector.tensor_scalar(one[0:1, :], one[0:1, :], 1.0 / 127.0, None, ALU.mult))
                link(nc.vector.tensor_scalar(one[0:1, :], one[0:1, :], 1e-8, None, ALU.max))
                dve.wait_ge(s["job_full"].sem, b["job_full"] + 1)
                link(nc.vector.tensor_copy(sc, bank[1][:, 0:1]))
                link(nc.vector.reciprocal(inv, sc))
                magic = 1.5 * 2.0 ** 23
                link(nc.vector.tensor_scalar(q, v, inv, magic, ALU.mult, ALU.add))
                link(nc.vector.tensor_scalar(q, q, magic, 127.0, ALU.subtract, ALU.min))
                link(nc.vector.tensor_scalar(q, q, -128.0, sc, ALU.max, ALU.mult))
                link(nc.vector.tensor_tensor(q, q, v, ALU.subtract))
                nc.vector.tensor_tensor(v, v, q, ALU.add)
            phases.append(dict(tensor=tensor, vector=vector))

        def route_phase():
            KEEP = max(1, int(round(0.15 * SLOT)))
            b = base(dve_step=9 + 4 * 2 + 4 * 4, job_full=4 + 12, job_used=4 + 12, bridge=112)
            turn_d = nc.dram_tensor("turn", (3, TOK), F32).ap()

            def by_image(k):
                return turn_d[k, :].rearrange("(m t) -> m t", t=SLOT)
            NJ = TOK // 4
            s_row, w_row, m_row = k_x[0:1, 0:TOK], k_t[0:1, :, :].rearrange("p c n -> p (c n)"), q_t[0:1, 0:TOK]
            s26, w26, m26 = (k_x[0:IMG, c:c + SLOT] for c in (1664, 1704, 1744))
            early, less, same = (k_x[0:IMG, c:c + SLOT * SLOT].rearrange("p (t u) -> p t u", u=SLOT)
                                 for c in (1800, 2500, 3200))
            total = k_x[0:IMG, 4000:4001]
            pool = sml[:, 0:2 * IMG].rearrange("p (c m) -> p c m", c=2)

            def sync(sp):
                sp.wait_ge(s["phase_done"].sem, 3 * ROUTE[0])
                sp.dma_start(k_x[0:IMG, 1800:1800 + SLOT * SLOT], a["earlier"]).then_inc(s["bridge"].sem, 16)
                sp.wait_ge(s["job_used"].sem, b["job_used"] + 4)
                sp.dma_start(turn_d[0:1, :], s_row).then_inc(s["bridge"].sem, 16)
                sp.wait_ge(s["bridge"].sem, b["bridge"] + 32)
                sp.dma_start(s26, by_image(0)).then_inc(s["bridge"].sem, 16)
                sp.wait_ge(s["dve_step"].sem, b["dve_step"] + 9)
                sp.dma_start(by_image(1), w26).then_inc(s["bridge"].sem, 16)
                sp.dma_start(by_image(2), m26).then_inc(s["bridge"].sem, 16)
                sp.wait_ge(s["bridge"].sem, b["bridge"] + 80)
                sp.dma_start(w_row, turn_d[1:2, :]).then_inc(s["bridge"].sem, 16)
                sp.dma_start(m_row, turn_d[2:3, :]).then_inc(s["bridge"].sem, 16)

            def tensor(pe):
                pe.wait_ge(s["dve_step"].sem, b["dve_step"] + 2)
                for j in range(4):
                    c = slice(NJ * j, NJ * (j + 1))
                    five(bank[j][0:2, 0:NJ], [gw_hi[:, 0, 0:2], gw_hi[:, 1, 0:2]],
                         [gw_lo[:, 0, 0:2], gw_lo[:, 1, 0:2]], xa_hi[:, c], xa_lo[:, c], xb[:, c], True)\
                        .then_inc(s["job_full"].sem, 1)
                pe.wait_ge(s["bridge"].sem, b["bridge"] + 112)
                for x in range(12):
                    r, j = BROADCAST[x]
                    pe.wait_ge(s["job_used"].sem, b["job_used"] + (4 if x < 4 else x + 1))
                    src = (w_row, s_row, m_row)[r]
                    nc.tensor.matmul(bank[4 + x % 4][:, 0:NJ], row[0:1, ROW_COLS["ones"]],
                                     src[:, NJ * j:NJ * (j + 1)], start=True, stop=True).then_inc(s["job_full"].sem, 1)

            def scalar(act):
                for j in range(4):
                    act.wait_ge(s["job_full"].sem, b["job_full"] + j + 1)
                    nc.scalar.activation(s_row[:, NJ * j:NJ * (j + 1)], bank[j][0:1, 0:NJ], ACT.Sigmoid,
                                         bias=row[0:1, ROW_COLS.lo("L3_br"):ROW_COLS.lo("L3_br") + 1])\
                        .then_inc(s["job_used"].sem, 1)

            def vector(dve):
                link = chain(dve, s["dve_step"], [b["dve_step"]])
                w = dat[:, DATA_COLS["L3_r"]].rearrange("p (k e) -> p k e", k=2)
                link(nc.vector.tensor_copy(gw_hi[:, :, 0:2], w))
                link(nc.vector.tensor_tensor(gw_lo[:, :, 0:2], w, gw_hi[:, :, 0:2].bitcast(F32), ALU.subtract))
                dve.wait_ge(s["bridge"].sem, b["bridge"] + 48)
                n3 = [IMG, SLOT, SLOT]
                su, st = s26.unsqueeze(1).to_broadcast(n3), s26.unsqueeze(2).to_broadcast(n3)
                nc.vector.tensor_tensor(less, su, st, ALU.is_lt)
                nc.vector.tensor_reduce(total, s26, AX.X, ALU.add)
                link(nc.vector.tensor_tensor(same, su, st, ALU.is_equal))
                nc.vector.tensor_scalar(row[0:1, ROW_COLS["L3_bm"]], row[0:1, ROW_COLS["L3_bm"]], -1.0, None,
                                        ALU.mult)
                link(nc.vector.tensor_tensor(same, same, early, ALU.mult))
                nc.vector.tensor_scalar(total, total, 1e-6, None, ALU.add)
                link(nc.vector.tensor_tensor(less, less, same, ALU.add))
                nc.vector.reciprocal(total, total)
                link(nc.vector.tensor_reduce(m26, less, AX.X, ALU.add))
                link(nc.vector.tensor_scalar(m26, m26, KEEP - 0.5, None, ALU.is_lt))
                link(nc.vector.tensor_scalar(w26, s26, total, None, ALU.mult))
                link(nc.vector.memset(sml[:, 140:141], 0.0))
                g3 = [128, NJ // SLOT, SLOT]
                for x in range(12):
                    r, j = BROADCAST[x]
                    dve.wait_ge(s["job_full"].sem, b["job_full"] + 4 + x + 1)
                    p = bank[4 + x % 4][:, 0:NJ]
                    c = slice(NJ * j, NJ * (j + 1))
                    mc = slice(NJ // SLOT * j, NJ // SLOT * (j + 1))
                    if r == 0:
                        nc.vector.tensor_tensor(o_f[:, 0:NJ], feat[:, 0, c], p, ALU.mult)
                        link(nc.vector.tensor_tensor(o_f[:, NJ:2 * NJ], feat[:, 1, c], p, ALU.mult))
                        nc.vector.tensor_reduce(pool[:, :, mc], o_f[:, 0:2 * NJ].rearrange(
                            "p (c m t) -> p c m t", c=2, t=SLOT), AX.X, ALU.add).then_inc(s["job_used"].sem, 1)
                        dve.wait_ge(s["job_used"].sem, b["job_used"] + 4 + x + 1)
                        link(nc.vector.memset(sml[:, 140:141], 0.0))
                    elif r == 1:
                        for k in range(2):
                            t = nc.vector.tensor_tensor(
                                o_f[:, NJ * k:NJ * (k + 1)].rearrange("p (m t) -> p m t", t=SLOT),
                                p.rearrange("p (m t) -> p m t", t=SLOT),
                                pool[:, k, mc].unsqueeze(2).to_broadcast(g3), ALU.mult)
                        t.then_inc(s["job_used"].sem, 1)
                        dve.wait_ge(s["job_used"].sem, b["job_used"] + 4 + x + 1)
                        link(nc.vector.tensor_tensor(feat[:, :, c], feat[:, :, c], o_f[:, 0:2 * NJ].rearrange(
                            "p (c n) -> p c n", c=2), ALU.add))
                    else:
                        nc.vector.tensor_copy(mask_b[:, c], p)
                        nc.vector.tensor_scalar(o_f[:, 0:NJ], p, -1.0, 1.0, ALU.mult, ALU.add)\
                            .then_inc(s["job_used"].sem, 1)
                        dve.wait_ge(s["job_used"].sem, b["job_used"] + 4 + x + 1)
                        link(nc.vector.tensor_tensor(feat[:, :, c], feat[:, :, c],
                                                     o_f[:, 0:NJ].unsqueeze(1).to_broadcast([128, 2, NJ]),
                                                     ALU.mult))
                for _ in range(8):
                    dve.sem_inc(s["dve_step"].sem, 1)
            BROADCAST = [(0, j) for j in range(4)] + [(r, j) for j in range(4) for r in (1, 2)]
            phases.append(dict(tensor=tensor, scalar=scalar, vector=vector, sync=sync))

        mask_b = n_tok[:, :, :].rearrange("p t d -> p (t d)")[:, 0:TOK]
        ROUTE = [0]

        def add_phase(dst, src):
            def vector(dve):
                nc.vector.tensor_tensor(dst[:, :, :], dst[:, :, :], src[:, :, :], ALU.add)
            phases.append(dict(vector=vector))

        def attention_weights(cfg, after):
            cols = 2 * cfg.C + (cfg.no + (2 if cfg.mix else 0)) * D
            low_rank = cfg.low_rank
            b = base(att_in=32 if low_rank else 16, att_hi=1, att_ready=1, pool_step=1, lo_full=0, job_full=10 if low_rank else 0,
                     job_used=10 if low_rank else 0)
            n, QW = 4 * cfg.G * SLOT, 4 * cfg.G * SLOT + 8
            pads = [xs[:, p, :].rearrange("p (m s) -> p m s", s=32)[:, :, SLOT:32] for p in range(3)]
            pads += [p[:, :, SLOT:32] for p in p_t]
            pads += [q_t[:, 0:cfg.no_q * QW].rearrange("p (c n) -> p c n", n=QW)[:, :, n:QW], rel_a[:, :, 20:32]]

            def sync(sp):
                sp.wait_ge(s["phase_done"].sem, 3 * after)
                if low_rank:
                    sp.dma_start(low[:, :], a[cfg.dram + "_low"]).then_inc(s["att_in"].sem, 16)
                    sp.dma_start(wp_raw[:, 2 * cfg.C:cols], a[cfg.dram]).then_inc(s["att_in"].sem, 16)
                else:
                    sp.dma_start(wp_raw[:, 0:cols], a[cfg.dram]).then_inc(s["att_in"].sem, 16)

            def tensor(pe):
                if not low_rank:
                    return
                pe.wait_ge(s["att_in"].sem, b["att_in"] + 32)
                pe.wait_ge(s["lo_full"].sem, b["lo_full"] + 4)
                for m in range(5):
                    f = (0, 0, 1, 1, 2)[m]
                    for k in range(2):
                        n = 2 * m + k
                        if n >= 4:
                            pe.wait_ge(s["job_used"].sem, b["job_used"] + n - 3)
                        nc.tensor.matmul(bank[n % 4][:, 0:D], low[:, 256 * f + 128 * k:256 * f + 128 * k + 128],
                                         low[:, 768 + D * m:768 + D * m + D], start=True, stop=True)\
                            .then_inc(s["job_full"].sem, 1)

            def scalar(act):
                for m in range(5 if low_rank else 0):
                    for k in range(2):
                        n = 2 * m + k
                        act.wait_ge(s["job_full"].sem, b["job_full"] + n + 1)
                        c = k * cfg.C + D * m
                        nc.scalar.activation(wp_raw[:, c:c + D], bank[n % 4][:, 0:D], ACT.Identity)\
                            .then_inc(s["job_used"].sem, 1)

                act.wait_ge(s["att_in"].sem, b["att_in"] + (32 if low_rank else 16))
                if low_rank:
                    act.wait_ge(s["job_used"].sem, b["job_used"] + 10)
                nc.scalar.activation(wp_hi[:, 0:cols], wp_raw[:, 0:cols], ACT.Identity)\
                    .then_inc(s["att_hi"].sem, 1)

            def gpsimd(pool):
                pool.wait_ge(s["att_hi"].sem, b["att_hi"] + 1)
                nc.gpsimd.tensor_tensor(wp_lo[:, 0:cols], wp_raw[:, 0:cols], wp_hi[:, 0:cols].bitcast(F32),
                                        ALU.subtract).then_inc(s["pool_step"].sem, 1)
                pool.wait_ge(s["pool_step"].sem, b["pool_step"] + 1)
                for m in pads:
                    ins = nc.gpsimd.memset(m.bitcast(F32) if m.dtype == F32R else m, 0.0)
                ins.then_inc(s["att_ready"].sem, 1)
            return dict(sync=sync, tensor=tensor, scalar=scalar, gpsimd=gpsimd)

        def attention_phase(cfg):
            G, R, NC, HCH, H, d, no = cfg.G, cfg.R, cfg.NC, cfg.HCH, cfg.H, cfg.d, cfg.no
            NI, n = IMG // (4 * G), 4 * G * SLOT
            QW = n + 8
            W = H * d
            halves = 2 if W > 512 else 1
            HH, WH = H // halves, W // halves
            qk = cfg.qk
            qk_order = sorted(range(len(qk)), key=lambda y: qk[y][0][0] != "k")
            rel_kind = cfg.kind == "rel"
            if cfg.kind == "performer":
                order = ["+qk", ("scores", 2), ("values", 0), ("exp", 2), "+fk", ("scores", 3), "+fq"]
            elif G == 4:
                order = [("scores", 2), ("values", 0), ("exp", 2), ("scores", 3)]
                order += ["+qk"] if cfg.kind == "causal" else ["+k"]
            if G == 4:
                order += [("values", 1), ("exp", 3)]
                order += ["+q"] if "+k" in order else []
                order += [("turn", 0), ("values", 2), ("turn", 1), ("+scores", 0),
                          ("values", 3), ("+scores", 1), ("turn", 2)]
                dve_order = [("normalise", 0), ("shift", 2), ("normalise", 1), ("shift", 3), ("normalise", 2),
                             "+spread", ("normalise", 3)]
            else:
                order = ["+qk", ("+scores", 0), ("values", 0), ("+scores", 1), ("values", 1), ("turn", 0)]
                dve_order = [("normalise", 0), "+spread", ("normalise", 1)]
            order += [("turn", G - 1), "+v", ("+exp", 0), "out", ("+exp", 1)]
            dve_order += [("+shift", 0), ("+shift", 1), "split"]

            half = len(qk) // 2
            PROJECTED = {"+qk": qk_order, "+k": qk_order[:half], "+q": qk_order[half:]}

            def jobs_of(steps):
                jobs = []
                for step in steps:
                    name, g = (step, 0) if isinstance(step, str) else step
                    if name in PROJECTED:
                        jobs += [("qk", y) for y in PROJECTED[name]]
                    elif name in ("+fq", "+fk"):
                        jobs += [(name[1:], c) for c in range(4)]
                    elif name == "+v":
                        jobs += [("v", (h, v)) for h in range(G) for v in range(halves)]
                    elif name == "+scores" and rel_kind:
                        jobs.append(("rel", g))
                    elif name == "values" and rel_kind:
                        jobs.append(("mass", g))
                    elif name == "turn":
                        jobs += [("t", (g, v)) for v in range(halves)]
                    elif name == "out":
                        jobs += [("out", 0), ("out", 1)]
                return jobs

            def is_next(step):
                return (step if isinstance(step, str) else step[0])[0] == "+"
            first_steps = [step for step in order if is_next(step)]
            last_steps = [step for step in order if not is_next(step)]
            J, JA = len(jobs_of(order)), len(jobs_of(first_steps))
            assert J % 2 == 0 and JA % 2 == 0

            class Body:

                def __init__(self, steps, i, j0):
                    self.steps, self.i, self.j0 = steps, i, j0
                    self.first, self.last = steps is first_steps, steps is last_steps
                    self.at = {job: y for y, job in enumerate(jobs_of(steps))}

                def nth(self, name):
                    return self.j0 + self.at[name]

            def bodies(eng, run):
                run(Body(first_steps, -1, 0))
                with eng.Fori(0, NI - 1) as i:
                    run(Body(order, i, JA + J * i))
                run(Body(last_steps, NI - 1, JA + J * (NI - 1)))
            C = cfg.dve_steps
            b = base(job_full=J * NI, job_used=J * NI, staged=3 * NI, k_done=NI, s_full=16, s_used=16, z_full=16,
                     p_full=16, px_full=16, av_full=16 * halves, av_used=16 * halves, o_split=NI, it_dve=C * NI,
                     qk_ready=2 * NI, rel_table=5 * rel_kind)
            s_free, s_free_at = (s["z_full"], b["z_full"]) if cfg.kind == "softmax" else (s["s_used"], b["s_used"])
            heads = shp[0:R, SHAPE_COLS[{16: "head16", 32: "head32", 64: "head64"}[cfg.R // HCH]]]

            def w_part(w, k, c0, m):
                return w[:, k * cfg.C + c0:k * cfg.C + c0 + m]

            def w_pair(w, c0, m):
                return [w_part(w, 0, c0, m), w_part(w, 1, c0, m)]

            def qcols(c):
                return slice(c * QW, c * QW + n)

            def wo(w, k, c0):
                return w[:, 2 * cfg.C + k * D + c0:2 * cfg.C + k * D + c0 + 128]

            def bank_of(x):
                return bank[6 + x % 2]

            q_turned = spare[0:R, 0:2 * n]
            k_feat = spare[0:R, 0:4 * n]
            squares = spare[0:R, 4 * n:8 * n]
            mixed = wp_hi[:, NARROW:NARROW + 3 * n].rearrange("p (c n) -> p c n", c=3)
            k_flat = k_feat if cfg.kind == "performer" else k_t[0:R, :, :].rearrange("p c n -> p (c n)")
            rel_table = k_x[:, 2560:2816]
            rel_mass = [k_x[:, 2816 + 384 * j:3200 + 384 * j] for j in range(2)]

            def k_chunk(c):
                return k_flat[:, n * c:n * c + n]

            def gpsimd(pool):
                def stage(i):
                    for p, y in enumerate((xa_hi, xa_lo, xb)):
                        o = xs_v(p, G)[:, :, 0:SLOT]
                        nc.gpsimd.tensor_copy(o, y[:, bass.ds(n * i, n)].rearrange("p (m s) -> p m s", s=SLOT))\
                            .then_inc(s["staged"].sem, 1)
                stage(0)
                if rel_kind:
                    nc.gpsimd.memset(rel_table, 0.0).then_inc(s["rel_table"].sem, 1)
                    pool.wait_ge(s["rel_table"].sem, b["rel_table"] + 1)
                    for k in range(4):
                        nc.gpsimd.tensor_copy(rel_table[32 * k:32 * k + 20, 64 * k:64 * k + 64],
                                              dat[32 * k:32 * k + 20, DATA_COLS["tabv"]])\
                            .then_inc(s["rel_table"].sem, 1)
                    pool.wait_ge(s["rel_table"].sem, b["rel_table"] + 5)
                pool.wait_ge(s["job_full"].sem, b["job_full"] + JA)
                stage(1)
                with pool.Fori(0, NI - 2) as i:
                    last_v = Body(order, i, JA + J * i).nth(("v", (G - 1, halves - 1)))
                    pool.wait_ge(s["job_full"].sem, b["job_full"] + last_v + 1)
                    hold(pool)
                    stage(i + 2)

            def xs_v(p, G):
                return xs[:, p, 0:128 * G].rearrange("p (m s) -> p m s", s=32)

            ready = s["att_ready"].at

            def tensor(pe):
                pe.wait_ge(s["att_ready"].sem, ready)

                def job(body, name):
                    pe.wait_ge(s["job_used"].sem, b["job_used"] + body.nth(name) - 1)
                    return bank_of(body.at[name])

                def scores(body, i, g):
                    t = G * i + g
                    pe.wait_ge(s_free.sem, s_free_at + t - 1)
                    if g == 0:
                        pe.wait_ge(s["k_done"].sem, b["k_done"] + i + 1)
                        last = ("fq", 3) if cfg.kind == "performer" else ("qk", qk_order[-1])
                        pe.wait_ge(s["job_used"].sem, b["job_used"] + body.nth(last) + 1)
                    o = bank[4 + g % 2]
                    for im in range(4):
                        m = SLOT * (4 * g + im)
                        for c in range(NC):
                            kx = k_x[0:R, c * HCH * n:(c + 1) * HCH * n].rearrange("p (h n) -> p h n", n=n)
                            w = HCH * SLOT
                            ins = nc.tensor.matmul(o[32 * im:32 * im + 32, c * w:(c + 1) * w],
                                                   q_t[0:R, c * QW + m:c * QW + m + 32], kx[:, :, m:m + SLOT],
                                                   start=True, stop=True)
                    ins.then_inc(s["s_full"].sem, 1)

                def rel_scores(body, g):
                    o = job(body, ("rel", g))
                    for im in range(4):
                        m = SLOT * (4 * g + im)
                        for c in range(NC):
                            ins = nc.tensor.matmul(o[32 * im:32 * im + 32, 40 * c:40 * c + 40],
                                                   q_t[0:R, c * QW + m:c * QW + m + 32],
                                                   dat[0:R, DATA_COLS["tabk"]], start=True, stop=True)
                    ins.then_inc(s["job_full"].sem, 1)

                def values(body, g):
                    t = G * body.i + g
                    pe.wait_ge(s["px_full"].sem, b["px_full"] + t + 1)
                    if g == 0:
                        pe.wait_ge(s["job_used"].sem, b["job_used"] + body.j0)
                    hold(pe)
                    if rel_kind:
                        o = job(body, ("mass", g))
                        hold(pe)
                        for k in range(3):
                            ins = nc.tensor.transpose(o[:, 128 * k:128 * k + 128],
                                                      rel_a[:, 4 * k:4 * k + 4, :].rearrange("p h s -> p (h s)"),
                                                      shp[:, SHAPE_COLS["ident"]])
                        ins.then_inc(s["job_full"].sem, 1)
                    for v in range(halves):
                        pe.wait_ge(s["av_used"].sem, b["av_used"] + halves * t + v - 3)
                        hold(pe)
                        ob = bank[halves * g + v]
                        for im in range(4):
                            p0 = 32 * im
                            for h in range(v * HH, v * HH + HH):
                                o = ob[p0:p0 + 32, (h - v * HH) * d:(h - v * HH) * d + d]
                                ins = nc.tensor.matmul(o, p_x[g % 2][p0:p0 + SLOT, h, :],
                                                       v_t[p0:p0 + SLOT, g * W + h * d:g * W + h * d + d],
                                                       start=True, stop=True)
                        ins.then_inc(s["av_full"].sem, 1)

                def turn(body, g):
                    t = G * body.i + g
                    pe.wait_ge(s["av_used"].sem, b["av_used"] + halves * (t + 1))
                    x = o_t[g % 2]
                    if no == 2:
                        o = job(body, ("t", (g, 0)))
                        nc.tensor.transpose(o[:, 0:128], x[:, 0:128], shp[:, SHAPE_COLS["ident"]])
                        transpose_b(o[:, 128:256], x[:, 0:D]).then_inc(s["job_full"].sem, 1)
                    else:
                        for v in range(2):
                            o = job(body, ("t", (g, v)))
                            if v == 0:
                                pe.wait_ge(s["rel_table"].sem, b["rel_table"] + 5)
                            for k in range(3):
                                c, p = divmod(3 * v + k, 2)
                                nc.tensor.matmul(o[:, 128 * k:128 * k + 128], rel_table[:, 128 * p:128 * p + 128],
                                                 rel_mass[g][:, 128 * c:128 * c + 128], start=True, stop=False)
                                ins = nc.tensor.matmul(o[:, 128 * k:128 * k + 128],
                                                       x[:, 128 * (3 * v + k):128 * (3 * v + k) + 128],
                                                       shp[:, SHAPE_COLS["ident"]], start=False, stop=True)
                            ins.then_inc(s["job_full"].sem, 1)

                def projections(body, ys):
                    m = bass.ds(n * (body.i + 1), n)
                    for y in ys:
                        o = job(body, ("qk", y))
                        c0 = cfg.qcol(y)
                        hold(pe)
                        five(o[0:R, 0:n], w_pair(wp_hi, c0, R), w_pair(wp_lo, c0, R), xa_hi[:, m], xa_lo[:, m],
                             xb[:, m], True).then_inc(s["job_full"].sem, 1)

                def features(body, f):
                    first = 0 if f == "fq" else 2
                    pe.wait_ge(s["qk_ready"].sem, b["qk_ready"] + 2 * (body.i + 1) + (1 if f == "fk" else 2))
                    for c in range(4):
                        o = job(body, (f, c))[0:96, 0:n]
                        r0 = DATA_COLS.lo("rand") + D * (c // 2) + 96 * (c % 2)
                        h0 = SHAPE_COLS.lo("halfnorm") + 96 * (c % 2)
                        nc.tensor.matmul(o, dat[0:96, r0:r0 + 96], k_t[0:96, first + c // 2, 0:n],
                                         start=True, stop=False)
                        q0 = n * (first + c // 2)
                        nc.tensor.matmul(o, shp[0:96, h0:h0 + 96], squares[:, q0:q0 + n],
                                         start=False, stop=True).then_inc(s["job_full"].sem, 1)

                def value_projections(body):
                    pe.wait_ge(s["staged"].sem, b["staged"] + 3 * (body.i + 2))
                    hold(pe)
                    for g in range(G):
                        for v in range(halves):
                            o = job(body, ("v", (g, v)))[:, 0:WH]
                            c0 = cfg.vcol + WH * v
                            gc = slice(128 * g, 128 * g + 128)
                            ins = five(o, w_pair(wp_hi, c0, WH), w_pair(wp_lo, c0, WH), xs[:, 0, gc],
                                       xs[:, 1, gc], xs[:, 2, gc], False, stop=not cfg.vb)
                            if cfg.vb:
                                ins = nc.tensor.matmul(o, row[0:1, ROW_COLS["ones"]], row[0:1, ROW_COLS[cfg.vb]],
                                                       start=False, stop=True)
                            ins.then_inc(s["job_full"].sem, 1)

                def project_out(body):
                    pe.wait_ge(s["o_split"].sem, b["o_split"] + body.i + 1)
                    for k in range(2):
                        o = job(body, ("out", k))[:, 0:n]
                        c0 = 64 * k
                        if no == 2:
                            ins = five(o, [wo(wp_hi, 0, c0), wo(wp_hi, 1, c0)], [wo(wp_lo, 0, c0), wo(wp_lo, 1, c0)],
                                       o_hi[:, 0:n], o_lo[:, 0:n], o_hi[:, n:2 * n], True, stop=not cfg.mix)
                            if cfg.mix:
                                five(o, [wo(wp_hi, 2, c0), wo(wp_hi, 3, c0)], [wo(wp_lo, 2, c0), wo(wp_lo, 3, c0)],
                                     mixed[:, 0, :], mixed[:, 1, :], mixed[:, 2, :], True, start=False, stop=False)
                                for y, name in enumerate(("L3_bo", "L3_bm")):
                                    r0 = ROW_COLS.lo(name) + c0
                                    ins = nc.tensor.matmul(o, row[0:1, r0:r0 + 128], mask_b[0:1, bass.ds(n * body.i, n)],
                                                           start=False, stop=y == 1)
                        else:
                            for f in range(no):
                                fc = slice(n * f, n * f + n)
                                nc.tensor.matmul(o, wo(wp_hi, f, c0), o_hi[:, fc], start=f == 0, stop=False)
                                nc.tensor.matmul(o, wo(wp_hi, f, c0), o_lo[:, fc], start=False, stop=False)
                                ins = nc.tensor.matmul(o, wo(wp_lo, f, c0), o_hi[:, fc], start=False,
                                                       stop=f == no - 1)
                        ins.then_inc(s["job_full"].sem, 1)

                def steps(body):
                    for step in body.steps:
                        name, g = (step, 0) if isinstance(step, str) else step
                        if name in PROJECTED:
                            projections(body, PROJECTED[name])
                        elif name in ("+fq", "+fk"):
                            features(body, name[1:])
                        elif name == "+v":
                            value_projections(body)
                        elif name == "+scores":
                            scores(body, body.i + 1, g)
                            if rel_kind:
                                rel_scores(body, g)
                        elif name == "scores":
                            scores(body, body.i, g)
                        elif name == "values":
                            values(body, g)
                        elif name == "turn":
                            turn(body, g)
                        elif name == "out":
                            project_out(body)
                bodies(pe, steps)

            def scalar(act):
                act.wait_ge(s["att_ready"].sem, ready)

                def job(body, name):
                    act.wait_ge(s["job_full"].sem, b["job_full"] + body.nth(name) + 1)
                    return bank_of(body.at[name])

                def projections(body, ys):
                    if cfg.kind != "performer":
                        act.wait_ge(s["k_done"].sem, b["k_done"] + body.i + 1)
                    for y in ys:
                        kind, c = qk[y]
                        p = job(body, ("qk", y))[0:R, 0:n]
                        if cfg.kind == "performer":
                            ins = nc.scalar.activation(k_t[0:R, y, 0:n], p, ACT.Identity,
                                                       scale=float(cfg.d) ** -0.25)
                            ins.then_inc(s["job_used"].sem, 1)
                            continue
                        dst = {"q": q_t[0:R, qcols(c)], "k": k_chunk(c), "qr": q_turned[:, n * (c % 2):n * (c % 2) + n],
                               "kr": k_t[0:R, (2 + c) % 4, 0:n]}[kind]
                        if cfg.bias:
                            col = DATA_COLS.lo(cfg.bias + {"q": "_qb", "k": "_kb"}[kind]) + c
                            ins = nc.scalar.activation(dst, p, ACT.Identity, bias=dat[0:R, col:col + 1])
                        else:
                            ins = nc.scalar.activation(dst, p, ACT.Identity)
                        ins.then_inc(s["job_used"].sem, 1)
                    if cfg.kind == "performer":
                        act.wait_ge(s["job_used"].sem, b["job_used"] + body.nth(("qk", qk_order[-1])) + 1)
                        for y in (2, 3, 0, 1):
                            ins = nc.scalar.activation(squares[:, n * y:n * y + n], k_t[0:R, y, 0:n], ACT.Square)
                            if y in (3, 1):
                                ins.then_inc(s["qk_ready"].sem, 1)

                def features(body, f):
                    if f == "fk":
                        act.wait_ge(s["k_done"].sem, b["k_done"] + body.i + 1)
                    for c in range(4):
                        dst = q_t[0:96, qcols(c)] if f == "fq" else k_chunk(c)
                        nc.scalar.activation(dst, job(body, (f, c))[0:96, 0:n], ACT.Exp)\
                            .then_inc(s["job_used"].sem, 1)

                def value_projections(body):
                    for g in range(G):
                        for v in range(halves):
                            nc.scalar.activation(v_t[:, g * W + WH * v:g * W + WH * v + WH],
                                                 job(body, ("v", (g, v)))[:, 0:WH], ACT.Identity)\
                                .then_inc(s["job_used"].sem, 1)

                def rel_scores(body, g):
                    nc.scalar.activation(rel[g][:, :, :].rearrange("p h r -> p (h r)"),
                                         job(body, ("rel", g))[:, 0:240], ACT.Identity)\
                        .then_inc(s["job_used"].sem, 1)

                def exponents(i, g):
                    t = G * i + g
                    act.wait_ge(s["z_full"].sem, b["z_full"] + t + 1)
                    act.wait_ge(s["px_full"].sem, b["px_full"] + t - 1)
                    nc.scalar.activation(p_t[g % 2][:, 0:H, 0:SLOT], z_t[g % 2][:, 0:H, :],
                                         ACT.Exp, scale=cfg.scale).then_inc(s["p_full"].sem, 1)

                def values(body, g):
                    t = G * body.i + g
                    if rel_kind:
                        nc.scalar.activation(rel_mass[g], job(body, ("mass", g))[:, 0:384], ACT.Identity)\
                            .then_inc(s["job_used"].sem, 1)
                    for v in range(halves):
                        act.wait_ge(s["av_full"].sem, b["av_full"] + halves * t + v + 1)
                        nc.scalar.activation(o_t[g % 2][:, v * WH:v * WH + WH], bank[halves * g + v][:, 0:WH],
                                             ACT.Identity).then_inc(s["av_used"].sem, 1)

                def turn(body, g):
                    if g == 0:
                        act.wait_ge(s["o_split"].sem, b["o_split"] + body.i)
                    for v in range(halves):
                        o = job(body, ("t", (g, v)))
                        m = no // halves
                        src = o[:, 0:128 * m].rearrange("p (c b s) -> p c b s", c=m, b=4)[:, :, :, 0:SLOT]
                        dst = o_f[:, 0:no * n].rearrange("p (c g b s) -> p c g b s", c=no, g=G, b=4)[
                            :, v * m:v * m + m, g, :, :]
                        nc.scalar.activation(dst, src, ACT.Identity).then_inc(s["job_used"].sem, 1)

                def project_out(body):
                    for k in range(2):
                        o = job(body, ("out", k))[:, 0:n]
                        hold(act)
                        dst = feat[:, k, bass.ds(n * body.i, n)]
                        if cfg.ob:
                            col = DATA_COLS.lo(cfg.ob) + k
                            ins = nc.scalar.activation(dst, o, ACT.Identity, bias=dat[:, col:col + 1])
                        else:
                            ins = nc.scalar.activation(dst, o, ACT.Identity)
                        ins.then_inc(s["job_used"].sem, 1)

                def steps(body):
                    exps = cfg.kind in ("softmax", "rel", "causal")
                    for step in body.steps:
                        name, g = (step, 0) if isinstance(step, str) else step
                        if name in PROJECTED:
                            projections(body, PROJECTED[name])
                        elif name in ("+fq", "+fk"):
                            features(body, name[1:])
                        elif name == "+v":
                            value_projections(body)
                        elif name == "+scores" and rel_kind:
                            rel_scores(body, g)
                        elif name == "values":
                            values(body, g)
                        elif name == "exp" and exps:
                            exponents(body.i, g)
                        elif name == "+exp" and exps:
                            exponents(body.i + 1, g)
                        elif name == "turn":
                            turn(body, g)
                        elif name == "out":
                            project_out(body)
                bodies(act, steps)

            def vector(dve):
                dve.wait_ge(s["att_ready"].sem, ready)

                def link(ins):
                    ins.then_inc(s["it_dve"].sem, 1)
                    k[1] += 1
                    dve.wait_ge(s["it_dve"].sem, b["it_dve"] + k[0] + k[1])

                def spread(body):
                    if cfg.kind == "causal":
                        dve.wait_ge(s["job_used"].sem, b["job_used"] + body.nth(("qk", qk_order[-1])) + 1)
                        cos = shp[0:R, SHAPE_COLS["cos"]].unsqueeze(1).to_broadcast([R, 4 * G, SLOT])
                        sin = shp[0:R, SHAPE_COLS["sin"]].unsqueeze(1).to_broadcast([R, 4 * G, SLOT])
                        for c in range(NC):
                            for x, xr in ((q_t[0:R, qcols(c)], q_turned[:, n * c:n * c + n]),
                                          (k_chunk(c), k_t[0:R, 2 + c, 0:n])):
                                x3, xr3 = (v.rearrange("p (m s) -> p m s", s=SLOT) for v in (x, xr))
                                nc.vector.tensor_tensor(x3, x3, cos, ALU.mult)
                                link(nc.vector.tensor_tensor(xr3, xr3, sin, ALU.mult))
                                link(nc.vector.tensor_tensor(x, x, xr, ALU.add))
                    for c in range(NC):
                        last = ("fk", c) if cfg.kind == "performer" else ("qk", qk.index(("k", c)))
                        dve.wait_ge(s["job_used"].sem, b["job_used"] + body.nth(last) + 1)
                        for h in range(HCH):
                            x = c * HCH + h
                            ins = nc.vector.tensor_scalar(k_x[0:R, x * n:(x + 1) * n], k_chunk(c),
                                                          heads[:, h:h + 1], None, ALU.mult)
                    ins.then_inc(s["k_done"].sem, 1)

                n3 = [128, H, SLOT]

                def shift(body, i, g):
                    t = G * i + g
                    j = g % 2
                    sc = bank[4 + j][:, 0:H * SLOT].rearrange("p (h s) -> p h s", s=SLOT)
                    z = z_t[j][:, 0:H, :]
                    mx = m12[:, j, 0:H]
                    dve.wait_ge(s["s_full"].sem, b["s_full"] + t + 1)
                    if cfg.kind == "performer":
                        dve.wait_ge(s["px_full"].sem, b["px_full"] + t - 1)
                        nc.vector.tensor_scalar(p_t[j][:, 0:H, 0:SLOT], sc, 1.0 / (2 * d), None, ALU.mult)\
                            .then_inc(s["s_used"].sem, 1)
                        return
                    if cfg.kind == "log2":
                        link(nc.vector.tensor_reduce(mx, sc, AX.X, ALU.max))
                        link(nc.vector.tensor_scalar(mx, mx, LOG2E, None, ALU.mult))
                        nc.vector.scalar_tensor_tensor(z, sc, LOG2E, bc(mx.unsqueeze(2), n3), ALU.mult,
                                                       ALU.subtract).then_inc(s["s_used"].sem, 1)
                        dve.wait_ge(s["s_used"].sem, b["s_used"] + t + 1)
                        zf, zi = (k_t[:, 2 + v, 0:H * SLOT].rearrange("p (h s) -> p h s", s=SLOT)
                                  for v in range(2))
                        link(nc.vector.tensor_scalar(z, z, -127.0, None, ALU.max))
                        magic = 1.5 * 2.0 ** 23
                        link(nc.vector.tensor_scalar(zf, z, magic, magic, ALU.add, ALU.subtract))
                        link(nc.vector.tensor_tensor(zi, zf, z, ALU.is_gt))
                        link(nc.vector.tensor_tensor(zi, zf, zi, ALU.subtract))
                        nc.vector.tensor_tensor(zf, z, zi, ALU.subtract)
                        bits = rel_p[:, :, :, :].rearrange("p h a c -> p (h a c)")[:, 0:H * SLOT]\
                            .rearrange("p (h s) -> p h s", s=SLOT)
                        link(nc.vector.tensor_scalar(bits.bitcast(I32), zi, 2.0 ** 23, 127.0 * 2 ** 23,
                                                     ALU.mult, ALU.add))
                        dve.wait_ge(s["px_full"].sem, b["px_full"] + t - 1)
                        nc.vector.scalar_tensor_tensor(p_t[j][:, 0:H, 0:SLOT], zf, 1.0, bits, ALU.add,
                                                       ALU.mult).then_inc(s["p_full"].sem, 1)
                        return
                    dve.wait_ge(s["p_full"].sem, b["p_full"] + t - 1)
                    src = sc
                    if cfg.kind == "causal":
                        mask = shp[:, SHAPE_COLS["causal"]].unsqueeze(1).to_broadcast(n3)
                        nc.vector.tensor_tensor(z, sc, mask, ALU.add).then_inc(s["s_used"].sem, 1)
                        dve.wait_ge(s["s_used"].sem, b["s_used"] + t + 1)
                        src = z
                    if cfg.kind == "rel":
                        dve.wait_ge(s["job_used"].sem, b["job_used"] + body.nth(("rel", g)) + 1)
                        rl = rel[j]
                        for v, ind in enumerate(("relv", "relh")):
                            pr = rel_p[:, :, :, :]
                            tb = rl[:, :, 10 * v:10 * v + 10].unsqueeze(2).to_broadcast([128, 12, 5, 10])
                            im = shp[:, SHAPE_COLS[ind]].rearrange("p (a r) -> p a r", r=10).unsqueeze(1)\
                                .to_broadcast([128, 12, 5, 10])
                            link(nc.vector.tensor_tensor(pr, tb, im, ALU.mult))
                            link(nc.vector.tensor_reduce(rel_u[:, v, :, :], pr, AX.X, ALU.add))
                        g4 = [128, 12, 5, 5]
                        z4 = z[:, :, 1:SLOT].rearrange("p h (a c) -> p h a c", c=5)
                        s4 = sc[:, :, 1:SLOT].rearrange("p h (a c) -> p h a c", c=5)
                        m0 = m12[:, 2, :].unsqueeze(2)
                        link(nc.vector.tensor_tensor(m0, rl[:, :, 0:1], rl[:, :, 10:11], ALU.add))
                        nc.vector.tensor_tensor(z[:, :, 0:1], sc[:, :, 0:1], m0, ALU.add)
                        nc.vector.tensor_tensor(z4, s4, rel_u[:, 0, :, :].unsqueeze(3).to_broadcast(g4),
                                                ALU.add).then_inc(s["s_used"].sem, 1)
                        dve.wait_ge(s["s_used"].sem, b["s_used"] + t + 1)
                        link(nc.vector.tensor_tensor(z4, z4, rel_u[:, 1, :, :].unsqueeze(2).to_broadcast(g4),
                                                     ALU.add))
                        src = z
                    link(nc.vector.tensor_reduce(mx, src, AX.X, ALU.max))
                    nc.vector.tensor_tensor(z, src, bc(mx.unsqueeze(2), n3), ALU.subtract)\
                        .then_inc(s["z_full"].sem, 1)

                def normalise(body, g):
                    t = G * body.i + g
                    j = g % 2
                    p = p_t[j][:, 0:H, 0:SLOT]
                    sm = m12[:, 2 + j, 0:H]
                    if cfg.kind == "performer":
                        dve.wait_ge(s["s_used"].sem, b["s_used"] + t + 1)
                    else:
                        dve.wait_ge(s["p_full"].sem, b["p_full"] + t + 1)
                    link(nc.vector.tensor_reduce(sm, p, AX.X, ALU.add))
                    if cfg.kind == "performer":
                        link(nc.vector.tensor_scalar(sm, sm, 1e-12, None, ALU.max))
                    link(nc.vector.reciprocal(sm, sm))
                    link(nc.vector.tensor_tensor(p, p, bc(sm.unsqueeze(2), n3), ALU.mult))
                    if cfg.kind == "rel":
                        if g == 0:
                            dve.wait_ge(s["av_full"].sem, b["av_full"] + halves * t)
                        else:
                            dve.wait_ge(s["job_full"].sem, b["job_full"] + body.nth(("mass", 0)) + 1)
                        hold(dve)
                        pk = p[:, :, 1:SLOT].rearrange("p h (a c) -> p h a c", c=5)
                        nc.vector.tensor_reduce(rel_u[:, 0, :, :], pk, AX.X, ALU.add)
                        link(nc.vector.tensor_reduce(rel_u[:, 1, :, :], pk.rearrange("p h a c -> p h c a"),
                                                     AX.X, ALU.add))
                        for v, ind in enumerate(("relv", "relh")):
                            pr = rel_p[:, :, :, :].rearrange("p h a c -> p h (a c)")\
                                .rearrange("p h (r k) -> p h r k", k=5)
                            pu = rel_u[:, v, :, :].unsqueeze(2).to_broadcast([128, 12, 10, 5])
                            im = shp[:, SHAPE_COLS[ind]].rearrange("p (a r) -> p r a", r=10).unsqueeze(1)\
                                .to_broadcast([128, 12, 10, 5])
                            link(nc.vector.tensor_tensor(pr, pu, im, ALU.mult))
                            link(nc.vector.tensor_reduce(rel_a[:, :, 10 * v:10 * v + 10], pr, AX.X, ALU.add))
                        for v in range(2):
                            link(nc.vector.tensor_tensor(rel_a[:, :, 10 * v:10 * v + 1],
                                                         rel_a[:, :, 10 * v:10 * v + 1], p[:, :, 0:1], ALU.add))
                    dve.wait_ge(s["av_full"].sem, b["av_full"] + halves * (t - 1))
                    nc.vector.transpose(p_x[j][:, 0:H, :].rearrange("p h s -> p (h s)"),
                                        p_t[j][:, 0:H, :].rearrange("p h s -> p (h s)"))\
                        .then_inc(s["px_full"].sem, 1)

                def split_result(body):
                    i = body.i
                    dve.wait_ge(s["job_used"].sem, b["job_used"] + body.nth(("t", (G - 1, halves - 1))) + 1)
                    if cfg.mix:
                        of3 = o_f[:, 0:2 * n].rearrange("p (c n) -> p c n", c=2)
                        link(nc.vector.tensor_tensor(of3, of3, mask_b[:, bass.ds(n * i, n)].unsqueeze(1)
                                                     .to_broadcast([128, 2, n]), ALU.mult))
                        hold(dve)
                        nc.vector.tensor_copy(mixed[:, 0, :], feat[:, 0, bass.ds(n * i, n)])
                        link(nc.vector.tensor_copy(mixed[:, 2, :], feat[:, 1, bass.ds(n * i, n)]))
                        nc.vector.tensor_tensor(mixed[:, 1, :], feat[:, 0, bass.ds(n * i, n)],
                                                mixed[:, 0, :].bitcast(F32), ALU.subtract)
                        nc.vector.tensor_tensor(mixed[64:128, 2, :], feat[64:128, 1, bass.ds(n * i, n)],
                                                mixed[64:128, 2, :].bitcast(F32), ALU.subtract)
                    link(nc.vector.tensor_copy(o_hi[:, 0:no * n], o_f[:, 0:no * n]))
                    if no == 2:
                        nc.vector.tensor_tensor(o_hi[64:128, n:2 * n], o_f[64:128, n:2 * n],
                                                o_hi[64:128, n:2 * n].bitcast(F32), ALU.subtract)
                    m = n if no == 2 else no * n
                    nc.vector.tensor_tensor(o_lo[:, 0:m], o_f[:, 0:m], o_hi[:, 0:m].bitcast(F32), ALU.subtract)\
                        .then_inc(s["o_split"].sem, 1)

                def steps(body):
                    if not body.first:
                        k[0], k[1] = k[2] + C * body.i, 0
                    for step in dve_order:
                        name, g = (step, 0) if isinstance(step, str) else step
                        if is_next(step):
                            if body.last:
                                continue
                            if name == "+spread":
                                spread(body)
                            else:
                                shift(body, body.i + 1, g)
                        elif body.first:
                            continue
                        elif name == "normalise":
                            normalise(body, g)
                        elif name == "shift":
                            shift(body, body.i, g)
                        else:
                            split_result(body)
                    if body.first:
                        k[2] = k[1]
                    assert body.first or body.last or k[1] == C, (cfg.dram, k)
                k = [0, 0, 0]
                bodies(dve, steps)
            for name, uses in (("s_used", cfg.kind != "softmax"), ("z_full", cfg.kind in ("softmax", "rel", "causal")),
                               ("p_full", cfg.kind != "performer"),
                               ("qk_ready", cfg.kind == "performer")):
                if not uses:
                    signals[name].at = b[name]
            phases.append(dict(tensor=tensor, scalar=scalar, vector=vector, gpsimd=gpsimd))

        qk4 = [("q", 0), ("q", 1), ("k", 0), ("k", 1)]
        std = dict(H=12, d=16, G=4, qk=qk4, qcol=lambda x: 96 * x, vcol=2 * D, C=3 * D)
        l0 = Attention("L0_att", "causal", 6, 32, 4, [(k, c) for k in ("q", "qr", "k", "kr") for c in range(2)],
                    lambda x: 96 * x, 4 * D, 5 * D, 25, scale=32 ** -0.5, low_rank=True)
        l1 = Attention("L1_att", "rel", 12, 64, 2, [(k, c) for k in ("q", "k") for c in range(6)],
                    lambda x: 128 * x, 12 * 128, 18 * 128, 35, scale=0.125, ob="L1_ob", no=6, R=128, NC=6)
        l2a = Attention("L2_att", "performer", dve_steps=17, ob="L2a_ob", NC=4, **std)
        l2f = Attention("L2_fat", "softmax", dve_steps=17, scale=0.25, bias="L2f", vb="L2f_vb", ob="L2f_ob", **std)
        l3a = Attention("L3_att", "log2", dve_steps=41, bias="L3a", vb="L3a_vb", ob="L3a_ob", **std)

        l3f = Attention("L3_fat", "softmax", dve_steps=19, scale=0.25, bias="L3f", vb="L3f_vb", ob="L3f_ob", mix=True,
                     **std)

        def attention(cfg, res, *others):
            attention_phase(cfg)
            add_back_phase(res, *others)

        conv_phase()
        features_phase(n_tok, attention_weights(l0, 1), norm_of=h_tok)
        load, split, w = expert_weights(32, a["L0_exp"], len(phases) + 1)
        attention(l0, h_tok, load)
        features_phase(n_tok, split, norm_of=h_tok)
        g = gates(32, "L0_g", "L0_gb", "softmax")
        experts_phase(32, a["L0_exp"], "L0_b1", "L0_b2", h_tok, ACT.Gelu, w, g)
        features_phase(n_tok, attention_weights(l1, len(phases)), norm_of=h_tok)
        load, split, w = expert_weights(8, a["L1_exp"], len(phases) + 1)
        attention(l1, h_tok, load)
        features_phase(n_tok, split, norm_of=h_tok)
        g = gates(8, "L1_g", None, "top1")
        experts_phase(8, a["L1_exp"], "L1_b1", "L1_b2", h_tok, ACT.Silu, w, g)
        features_phase(n_tok, attention_weights(l2a, len(phases)), norm_of=h_tok)
        attention(l2a, h_tok)
        norm_phase(h_tok, y_tok, attention_weights(l2f, len(phases)))
        features_phase(n_tok, ln="ln_L2f1", norm_of=y_tok)
        load, split, w = expert_weights(1, a["L2_mlp"], len(phases) + 1)
        attention(l2f, y_tok, load, split)
        features_phase(y_tok)
        experts_phase(1, a["L2_mlp"], "L2m_b1", "L2m_b2", y_tok, ACT.Gelu, w)
        load, split, w = expert_weights(4, a["L2_exp"], len(phases))
        features_phase(n_tok, load, split, ln="ln_L2f2", norm_of=y_tok)
        g = gates(4, "L2_g", "L2_gb", "top2")
        experts_phase(4, a["L2_exp"], "L2e_b1", "L2e_b2", y_tok, ACT.Gelu, w, g)
        add_phase(h_tok, y_tok)
        norm_phase(h_tok, n_tok, attention_weights(l3a, len(phases)))
        quantise_phase(n_tok)
        features_phase(n_tok)
        attention(l3a, h_tok)
        norm_phase(h_tok, y_tok)
        features_phase(n_tok, ln="ln_L3f1", norm_of=y_tok)
        ROUTE[0] = len(phases)
        route_phase()
        phases.append(attention_weights(l3f, len(phases)))
        load, split, w = expert_weights(1, a["L3_mlp"], len(phases) + 1)
        attention(l3f, y_tok, load, split)
        features_phase(n_tok, ln="ln_L3f2", norm_of=y_tok)
        experts_phase(1, a["L3_mlp"], "L3_b1", "L3_b2", y_tok, ACT.Gelu, w)
        add_phase(h_tok, y_tok)

        block = ctx.enter_context(nc.Block())
        loads = [(shp[:, :], a["shape_pack"]), (dat[:, :], a["data_pack"]), (row[:, :], a["row_pack"]),
                 (tok0[:, :, :], a["tok0"])]
        CONSTS = len(loads)
        started = [n for n in names if signals[n] and n not in
                   ("consts_in", "conv_in", "w_in0", "w_in1", "att_in", "out_done", "bridge", "phase_done", "holds")]

        def run(eng, kind):
            for n, ph in enumerate(phases):
                if kind in ph:
                    ph[kind](eng)
                if kind != "gpsimd":
                    eng.drain().then_inc(s["phase_done"].sem, 1)
                eng.wait_ge(s["phase_done"].sem, 3 * (n + 1))

        @block.sync
        def _(sp):
            for dst, src in ((conv_w[:, :, :], a["conv_w"]), (conv_row[:, :], a["conv_row"])):
                sp.dma_start(dst, src).then_inc(s["conv_in"].sem, 16)
            for c in range(PIX // 128):
                sp.dma_start(pix[:, c, :], a["pixels"][:, c, :]).then_inc(pix_in[c], 16)
            for dst, src in loads:
                sp.dma_start(dst, src).then_inc(s["consts_in"].sem, 16)
            for ph in phases:
                if "sync" in ph:
                    ph["sync"](sp)
            sp.wait_ge(s["phase_done"].sem, 3 * len(phases))
            sp.dma_start(out, h_tok[:, :, :]).then_inc(s["out_done"].sem, 16)
            sp.wait_ge(s["out_done"].sem, 16)

        @block.gpsimd
        def _(pool):
            for n in started:
                pool.sem_inc(signals[n].sem, START)
            run(pool, "gpsimd")

        @block.scalar
        def _(act):
            run(act, "scalar")

        @block.vector
        def _(dve):
            run(dve, "vector")

        @block.tensor
        def _(pe):
            run(pe, "tensor")


def pad2(w):
    o = np.zeros((128, 2, w.shape[1]), w.dtype)
    o[:, 0] = w[:DA]
    o[:DB, 1] = w[DA:]
    o[DB:, 1] = w[DA:]
    return o


def shape_pack():
    o = np.zeros((128, SHAPE_COLS.n), np.float32)
    p = np.arange(128)
    o[p, SHAPE_COLS.lo("ident") + p] = 1
    for name, d, rows in (("head16", 16, 96), ("head32", 32, 96), ("head64", 64, 128)):
        r = np.arange(rows)
        o[r, SHAPE_COLS.lo(name) + r // d] = 1
    inv = 1.0 / 10000.0 ** (np.arange(0, 32, 2, dtype=np.float32) / 32)
    f = np.outer(np.arange(SLOT, dtype=np.float32), inv).astype(np.float32)
    emb = np.concatenate([f, f], 1)
    r = np.arange(96)
    o[:96, SHAPE_COLS["cos"]] = np.cos(emb).T[r % 32]
    o[:96, SHAPE_COLS["sin"]] = (np.sin(emb).T * np.where(np.arange(32) < 16, -1, 1)[:, None])[r % 32]
    q = p % 32
    o[:, SHAPE_COLS["causal"]] = np.where(np.arange(SLOT)[None] > q[:, None], -BIG, 0)
    hn = np.zeros((128, D), np.float32)
    for k in range(2):
        for c in range(96):
            hn[(3 * k + c // 32) * 16:(3 * k + c // 32) * 16 + 16, 96 * k + c] = -0.5
    o[:, SHAPE_COLS["halfnorm"]] = hn
    for name, div in (("relv", True), ("relh", False)):
        ind = np.zeros((128, SIDE, 10), np.float32)
        for i in range(128):
            m = i % 32 - 1
            for k in range(SIDE):
                if m < 0 or m >= SIDE * SIDE:
                    ind[i, k, 0] = 1
                else:
                    ind[i, k, k - (m // SIDE if div else m % SIDE) + 5] = 1
        o[:, SHAPE_COLS["" + name]] = ind.reshape(128, 50)
    o[:, SHAPE_COLS["order8"]] = np.arange(8, 0, -1)[None]
    return o


def expert_pack(w1, w2):
    E = w1.shape[0]
    o = np.zeros((E, 128, RAW), w1.dtype)
    v = o[:, :, :2 * HID].reshape(E, 128, 2, HID)
    v[:, :, 0] = w1[:, :DA]
    v[:, :DB, 1] = w1[:, DA:]
    v[:, DB:, 1] = w1[:, DA:]
    o[:, :, :2 * HID] = v.reshape(E, 128, 2 * HID)
    o[:, :, 2 * HID:] = w2.reshape(E, HC, 128, D).transpose(0, 2, 1, 3).reshape(E, 128, HC * D)
    return o


def chunked_bias(b):
    return b.reshape(-1, HC, 128).transpose(2, 0, 1).reshape(128, -1)


def layout(i):
    g = {k: np.asarray(v) for k, v in i.items()}
    f = np.float32
    dat = np.zeros((128, DATA_COLS.n), f)
    row = np.zeros((1, ROW_COLS.n), f)

    def col(name, v):
        dat[:v.shape[0], DATA_COLS[name]] = v
    col("L0_b1", chunked_bias(g["L0_ffn_b1"]))
    col("L1_b1", chunked_bias(g["L1_ffn_b1"]))
    col("L2m_b1", chunked_bias(g["L2_ffn_mlp_b1"]))
    col("L2e_b1", chunked_bias(g["L2_ffn_exp_b1"]))
    col("L3_b1", chunked_bias(g["L3_ffn_bf1"]))
    for name, v in (("L2f_qb", g["L2_ffn_in_b"][:D]), ("L2f_kb", g["L2_ffn_in_b"][D:2 * D]),
                    ("L3a_qb", g["L3_attn_bq"]), ("L3a_kb", g["L3_attn_bk"]),
                    ("L3f_qb", g["L3_ffn_bq"]), ("L3f_kb", g["L3_ffn_bk"])):
        col(name, v.reshape(2, 96).T)
    for name, v in (("L1_ob", g["L1_attn_proj_b"]), ("L2a_ob", g["L2_attn_proj_b"]), ("L2f_ob", g["L2_ffn_out_b"]),
                    ("L3a_ob", g["L3_attn_bo"]), ("L3f_ob", g["L3_ffn_bm"])):
        col(name, np.stack([v[:128], v[64:]], 1))
    for name, gg, bb in (("ln_L2f1", g["L2_ffn_ln1_g"], g["L2_ffn_ln1_b"]), ("ln_L2f2", g["L2_ffn_ln2_g"], g["L2_ffn_ln2_b"]),
                         ("ln_L3f1", g["L3_ffn_g1"], g["L3_ffn_b1"]), ("ln_L3f2", g["L3_ffn_g2"], g["L3_ffn_b2"])):
        col(name, np.concatenate([pad2(gg[:, None])[:, :, 0], pad2(bb[:, None])[:, :, 0]], 1))
    col("L0_g", pad2(g["L0_ffn_gate_w"]).reshape(128, -1))
    col("L1_g", pad2(g["L1_ffn_Wg"]).reshape(128, -1))
    col("L2_g", pad2(g["L2_ffn_gate_w"].T).reshape(128, -1))
    wr = np.zeros((D, 2), f)
    wr[:, 0] = g["L3_ffn_Wr"]
    col("L3_r", pad2(wr).reshape(128, -1))
    col("L0_b2", g["L0_ffn_b2"])
    col("L1_b2", g["L1_ffn_b2"])
    col("L2e_b2", g["L2_ffn_exp_b2"])
    rand = np.zeros((96, 2, D), f)
    for h in range(12):
        rand[16 * (h % 6):16 * (h % 6) + 16, h // 6, 32 * (h % 6):32 * (h % 6) + 32] = g["L2_attn_rand_matrix"][h]
    col("rand", rand.reshape(96, -1))
    rows = [0] + list(range(11, 20))
    tk = np.zeros((128, 2, 20), f)
    for h in range(2):
        tk[64 * h:64 * h + 64, h, :10] = g["L1_attn_tab_kv"][rows].T
        tk[64 * h:64 * h + 64, h, 10:] = g["L1_attn_tab_kh"][rows].T
    col("tabk", tk.reshape(128, 40))
    tv = np.zeros((4, 32, 64), f)
    tv[:, :10] = g["L1_attn_tab_vv"][rows][None]
    tv[:, 10:20] = g["L1_attn_tab_vh"][rows][None]
    col("tabv", tv.reshape(128, 64))

    def rowset(name, v):
        row[0, ROW_COLS[name]] = v
    row[0, ROW_COLS["ones"]] = 1
    for name, v in (("L0_gb", g["L0_ffn_gate_b"]), ("L2_gb", g["L2_ffn_gate_b"]),
                    ("L2f_vb", g["L2_ffn_in_b"][2 * D:]), ("L3a_vb", g["L3_attn_bv"]), ("L3f_vb", g["L3_ffn_bv"]),
                    ("L2m_b2", g["L2_ffn_mlp_b2"]), ("L3_b2", g["L3_ffn_bf2"]),
                    ("L3_bo", g["L3_ffn_bo"]), ("L3_bm", g["L3_ffn_bm"])):
        rowset(name, v)
    row[0, ROW_COLS.lo("L3_br")] = g["L3_ffn_br"]
    x = g["x"][:, :, :80, :80].reshape(IMG, 3, SIDE, 16, SIDE, 16).transpose(1, 3, 5, 0, 2, 4)
    px = np.zeros((PIX, IMG, SLOT), f)
    px[:, :, 1:] = x.reshape(PIX, IMG, SIDE * SIDE)
    bounds = np.arange(1.0 / 32, 1.0, 1.0 / 32, dtype=f)
    frac = np.arange(0.0, 1.0 - 1e-06, 1.0 / SIDE, dtype=f)
    bins = np.searchsorted(bounds, frac, side="right")
    pos = g["L0_tok_pos_table"][(bins[:, None] * 32 + bins).reshape(-1)]
    tok0 = np.zeros((IMG, SLOT, D), f)
    tok0[:, 0] = g["cls_tok"][0, 0]
    tok0[:, 1:] = pos
    arrays = {
        "conv_row": np.concatenate([(np.arange(TOK) % SLOT != 0).astype(f), g["L0_tok_conv_b"]])[None],
        "shape_pack": shape_pack(), "data_pack": dat, "row_pack": row,
        "pixels": px.reshape(PIX // 128, 128, TOK).transpose(1, 0, 2),
        "conv_w": g["L0_tok_conv_w"].reshape(D, PIX).T.reshape(PIX // 128, 128, D).transpose(1, 0, 2),
        "tok0": tok0.reshape(TILES, 128, D).transpose(1, 0, 2),
        "L0_exp": expert_pack(g["L0_ffn_w1"], g["L0_ffn_w2"]),
        "L1_exp": expert_pack(g["L1_ffn_W1"], g["L1_ffn_W2"]),
        "L2_mlp": expert_pack(g["L2_ffn_mlp_w1"][None], g["L2_ffn_mlp_w2"][None]),
        "L2_exp": expert_pack(g["L2_ffn_exp_w1"], g["L2_ffn_exp_w2"]),
        "L3_mlp": expert_pack(g["L3_ffn_W1"][None], g["L3_ffn_W2"][None]),
    }

    def att(name, qkv, o):
        o = pad2(o).reshape(128, -1) if o.shape[0] == D else \
            o.reshape(-1, 128, D).transpose(1, 0, 2).reshape(128, -1)
        arrays[name] = np.concatenate([pad2(qkv).reshape(128, -1), o], 1) if qkv is not None else o

    def twice(m):
        m = m.T
        return [m[:, :DA], m[:, DA:], m[:, DA:]]
    turned = (np.arange(D) // 32) * 32 + (np.arange(D) % 32 + 16) % 32
    att("L0_att", None, g["L0_attn_o_w"])
    arrays["L0_att_low"] = np.concatenate(
        twice(g["L0_attn_qA"]) + twice(g["L0_attn_kA"]) + twice(g["L0_attn_vA"])
        + [g["L0_attn_qB"], g["L0_attn_qB"][:, turned], g["L0_attn_kB"], g["L0_attn_kB"][:, turned],
           g["L0_attn_vB"]], 1)
    att("L1_att", g["L1_attn_qkv_w"].T, g["L1_attn_proj_w"].T)
    att("L2_att", g["L2_attn_qkv_w"].T, g["L2_attn_proj_w"].T)
    att("L2_fat", g["L2_ffn_in_w"].T, g["L2_ffn_out_w"].T)
    att("L3_att", np.concatenate([g["L3_attn_Wq"], g["L3_attn_Wk"], g["L3_attn_Wv"]], 1), g["L3_attn_Wo"])
    att("L3_fat", np.concatenate([g["L3_ffn_Wq"], g["L3_ffn_Wk"], g["L3_ffn_Wv"]], 1), g["L3_ffn_Wo"])
    arrays["L3_fat"] = np.concatenate([arrays["L3_fat"], pad2(g["L3_ffn_Wm"]).reshape(128, -1)], 1)
    t = np.arange(SLOT)
    arrays["earlier"] = np.tile((t[None, :] < t[:, None]).astype(f).reshape(1, -1), (IMG, 1))
    return {k: np.ascontiguousarray(v) for k, v in arrays.items()}


def kernel(**inputs):
    import numpy as _np
    import concourse.bacc as _bacc
    from concourse import mybir as _mybir
    from concourse.bass_utils import run_bass_kernel_spmd as _run

    nc = _bacc.Bacc("TRN2", target_bir_lowering=False, num_devices=1)
    arrays = layout(inputs)
    args = {k: nc.dram_tensor("in_" + k, v.shape, _mybir.dt.from_np(v.dtype), kind="ExternalInput").ap()
            for k, v in arrays.items()}
    o = nc.dram_tensor("out_0", (128, TILES, D), _mybir.dt.float32, kind="ExternalOutput").ap()
    vit_tower(nc, args, o)
    r = _run(nc, [{"in_" + k: v for k, v in arrays.items()}], core_ids=[0])
    return _np.ascontiguousarray(r.results[0]["out_0"].transpose(1, 0, 2).reshape(IMG, SLOT, D))
```
